# Optimizing a Trainium2 kernel written in Bass

```python
import numpy as np
import jax
import jax.numpy as jnp

def _softmax(x, axis=-1):
    return jax.nn.softmax(x, axis=axis)

def _gelu(x):
    return jax.nn.gelu(x, approximate=True)

def _silu(x):
    return jax.nn.silu(x)

def _sigmoid(x):
    return jax.nn.sigmoid(x)

def _layernorm(x, axis=-1, eps=1e-05):
    m = jnp.mean(x, axis=axis, keepdims=True)
    v = jnp.var(x, axis=axis, keepdims=True)
    return (x - m) / jnp.sqrt(v + eps)

def _scatter_add(tgt, idx, src, axis=0):
    return tgt.at[idx].add(src)

def _segment_sum(src, seg, n):
    return jax.ops.segment_sum(src, seg, n)
kernel_name = 'mk_flamingo_gated_d1_seqx_r4_3f2243'

def setup_inputs(seed: int=0):
    np.random.seed(seed)
    _w = jnp.asarray

    def _rec_inputs():
        import jax
        import jax.numpy as jnp
        _rk = jax.random.key(seed)
        x = -4.161e-06 + 1 * jax.random.normal(jax.random.fold_in(_rk, 1), (8, 112, 512), jnp.float32)
        _lenS = 112 - jax.random.randint(jax.random.fold_in(_rk, 7), (8,), 0, max(1, 112 // 4) + 1, jnp.int32)
        _lenS2 = 375 - jax.random.randint(jax.random.fold_in(_rk, 8), (8,), 0, max(1, 375 // 4) + 1, jnp.int32)
        _ctx_2048P = jax.random.normal(jax.random.fold_in(_rk, 11), (8, 16, 512), jnp.float32)
        _ctx_2048c = jax.random.dirichlet(jax.random.fold_in(_rk, 511), 0.3 * jnp.ones((16,), jnp.float32), (8, 375))
        _ctx_2048t = jnp.einsum('bsk,bkd->bsd', _ctx_2048c, _ctx_2048P)
        _ctx_2048t = _ctx_2048t * jax.lax.rsqrt(jnp.mean(jnp.square(_ctx_2048t)) + 1e-12) * 0.953939
        ctx_2048 = -0.000192764 + 0.999654 * (_ctx_2048t + 0.3 * jax.random.normal(jax.random.fold_in(_rk, 611), (8, 375, 512), jnp.float32))
        _g = jax.random.normal(jax.random.fold_in(_rk, 9001), (2, 1), jnp.float32)
        _g = jnp.sign(_g) * jnp.maximum(jnp.abs(_g), 1.0) + (_g == 0) * 1.0
        g_xattn = _g[0]
        g_ffn = _g[1]
        return (x, ctx_2048, g_xattn, g_ffn)
    x, ctx_2048, g_xattn, g_ffn = _rec_inputs()

    def _L0_xattn_setup():
        import jax, jax.numpy as jnp
        import numpy as np
        FP8_MAX = 448.0
        EPS = 1e-05

        def _fp8_roundtrip(x):
            return x.astype(jnp.float8_e4m3fn).astype(jnp.float32)

        def _div_clamp_fp8(x, scale):
            y = jnp.clip(x.astype(jnp.float32) / scale, -FP8_MAX, FP8_MAX)
            y = y.astype(jnp.bfloat16).astype(jnp.float32)
            return _fp8_roundtrip(y)

        def _ln(x, w, b):
            mu = jnp.mean(x, axis=-1, keepdims=True)
            var = jnp.mean(jnp.square(x - mu), axis=-1, keepdims=True)
            return (x - mu) * jax.lax.rsqrt(var + EPS) * w + b

        def _fp8_linear_pertensor(x, wq, w_scale, in_scale):
            xq = _div_clamp_fp8(x, in_scale)
            return jnp.einsum('bsi,oi->bso', xq * in_scale, wq) * w_scale

        def _gqa(q, k, v):
            scale = 1.0 / np.sqrt(q.shape[-1])
            scores = jnp.einsum('bsghd,btgd->bghst', q, k) * scale
            p = jax.nn.softmax(scores, axis=-1)
            return jnp.einsum('bghst,btgd->bsghd', p, v)
        key = jax.random.key(seed)
        ks = jax.random.split(key, 8)
        B, S, SC, H, NH, G, D = (2, 512, 128, 512, 16, 8, 128)

        def qw(k, out_f, in_f):
            w = jax.random.normal(k, (out_f, in_f), jnp.float32) * 0.02
            sc = jnp.max(jnp.abs(w)) / FP8_MAX
            return (_fp8_roundtrip(w / sc), sc.astype(jnp.float32))
        wq, wq_s = qw(ks[0], NH * D, H)
        wqx, wqx_s = qw(ks[1], NH * D, H)
        wk, wk_s = qw(ks[2], G * D, H)
        wv, wv_s = qw(ks[3], G * D, H)
        wproj, wp_s = qw(ks[4], H, 2 * NH * D)
        return {'hidden_states': jax.random.normal(ks[5], (B, S, H), jnp.float32), 'cond': jax.random.normal(ks[6], (B, SC, H), jnp.float32), 'ln_w': jnp.ones((H,), jnp.float32), 'ln_b': jnp.zeros((H,), jnp.float32), 'wq': wq, 'wq_scale': wq_s, 'q_in_scale': jnp.full((H,), 0.05, jnp.float32), 'wqx': wqx, 'wqx_scale': wqx_s, 'qx_in_scale': jnp.full((H,), 0.05, jnp.float32), 'wk': wk, 'wk_scale': wk_s, 'k_in_scale': jnp.full((H,), 0.05, jnp.float32), 'wv': wv, 'wv_scale': wv_s, 'v_in_scale': jnp.full((H,), 0.05, jnp.float32), 'w_kv_x': jax.random.normal(ks[7], (2 * G * D, H), jnp.float32) * 0.02, 'qln_w': jnp.ones((D,), jnp.float32), 'qln_b': jnp.zeros((D,), jnp.float32), 'kln_w': jnp.ones((D,), jnp.float32), 'kln_b': jnp.zeros((D,), jnp.float32), 'qxln_w': jnp.ones((D,), jnp.float32), 'qxln_b': jnp.zeros((D,), jnp.float32), 'kxln_w': jnp.ones((D,), jnp.float32), 'kxln_b': jnp.zeros((D,), jnp.float32), 'wproj': wproj, 'proj_w_scale': wp_s, 'proj_in_scale': jnp.asarray(0.05, jnp.float32), 'proj_smooth': jnp.full((2 * NH * D,), 0.05, jnp.float32)}
    _L0_xattn_all = _L0_xattn_setup()
    _L0_xattn_in = {k: v for k, v in _L0_xattn_all.items() if k in ('ln_w', 'ln_b', 'wq', 'wq_scale', 'q_in_scale', 'wqx', 'wqx_scale', 'qx_in_scale', 'wk', 'wk_scale', 'k_in_scale', 'wv', 'wv_scale', 'v_in_scale', 'w_kv_x', 'qln_w', 'qln_b', 'kln_w', 'kln_b', 'qxln_w', 'qxln_b', 'kxln_w', 'kxln_b', 'wproj', 'proj_w_scale', 'proj_in_scale', 'proj_smooth')}
    del _L0_xattn_all

    def _L0_ffn_setup():
        import jax, jax.numpy as jnp
        import numpy as np
        B, T, D = (4, 512, 512)
        E = 8
        K = 2
        F = 2048 // (E // 2)
        key = jax.random.key(seed)
        ks = jax.random.split(key, 5)
        s_in = 1.0 / np.sqrt(D)
        s_mid = 1.0 / np.sqrt(F)
        x = jax.random.normal(ks[0], (B, T, D), dtype=jnp.float32)
        Wr = jax.random.normal(ks[1], (D, E), dtype=jnp.float32) * s_in
        Wg = jax.random.normal(ks[2], (E, D, F), dtype=jnp.float32) * s_in
        Wu = jax.random.normal(ks[3], (E, D, F), dtype=jnp.float32) * s_in
        Wd = jax.random.normal(ks[4], (E, F, D), dtype=jnp.float32) * s_mid
        return {'x': x, 'Wr': Wr, 'Wg': Wg, 'Wu': Wu, 'Wd': Wd}
    _L0_ffn_all = _L0_ffn_setup()
    _L0_ffn_in = {k: v for k, v in _L0_ffn_all.items() if k in ('Wr', 'Wg', 'Wu', 'Wd')}
    del _L0_ffn_all
    return {'x': x, 'ctx_2048': ctx_2048, 'g_xattn': g_xattn, 'g_ffn': g_ffn, 'L0_xattn_ln_w': _L0_xattn_in['ln_w'], 'L0_xattn_ln_b': _L0_xattn_in['ln_b'], 'L0_xattn_wq': _L0_xattn_in['wq'], 'L0_xattn_wq_scale': _L0_xattn_in['wq_scale'], 'L0_xattn_q_in_scale': _L0_xattn_in['q_in_scale'], 'L0_xattn_wqx': _L0_xattn_in['wqx'], 'L0_xattn_wqx_scale': _L0_xattn_in['wqx_scale'], 'L0_xattn_qx_in_scale': _L0_xattn_in['qx_in_scale'], 'L0_xattn_wk': _L0_xattn_in['wk'], 'L0_xattn_wk_scale': _L0_xattn_in['wk_scale'], 'L0_xattn_k_in_scale': _L0_xattn_in['k_in_scale'], 'L0_xattn_wv': _L0_xattn_in['wv'], 'L0_xattn_wv_scale': _L0_xattn_in['wv_scale'], 'L0_xattn_v_in_scale': _L0_xattn_in['v_in_scale'], 'L0_xattn_w_kv_x': _L0_xattn_in['w_kv_x'], 'L0_xattn_qln_w': _L0_xattn_in['qln_w'], 'L0_xattn_qln_b': _L0_xattn_in['qln_b'], 'L0_xattn_kln_w': _L0_xattn_in['kln_w'], 'L0_xattn_kln_b': _L0_xattn_in['kln_b'], 'L0_xattn_qxln_w': _L0_xattn_in['qxln_w'], 'L0_xattn_qxln_b': _L0_xattn_in['qxln_b'], 'L0_xattn_kxln_w': _L0_xattn_in['kxln_w'], 'L0_xattn_kxln_b': _L0_xattn_in['kxln_b'], 'L0_xattn_wproj': _L0_xattn_in['wproj'], 'L0_xattn_proj_w_scale': _L0_xattn_in['proj_w_scale'], 'L0_xattn_proj_in_scale': _L0_xattn_in['proj_in_scale'], 'L0_xattn_proj_smooth': _L0_xattn_in['proj_smooth'], 'L0_ffn_Wr': _L0_ffn_in['Wr'], 'L0_ffn_Wg': _L0_ffn_in['Wg'], 'L0_ffn_Wu': _L0_ffn_in['Wu'], 'L0_ffn_Wd': _L0_ffn_in['Wd']}

def reference(x, ctx_2048, g_xattn, g_ffn, L0_xattn_ln_w, L0_xattn_ln_b, L0_xattn_wq, L0_xattn_wq_scale, L0_xattn_q_in_scale, L0_xattn_wqx, L0_xattn_wqx_scale, L0_xattn_qx_in_scale, L0_xattn_wk, L0_xattn_wk_scale, L0_xattn_k_in_scale, L0_xattn_wv, L0_xattn_wv_scale, L0_xattn_v_in_scale, L0_xattn_w_kv_x, L0_xattn_qln_w, L0_xattn_qln_b, L0_xattn_kln_w, L0_xattn_kln_b, L0_xattn_qxln_w, L0_xattn_qxln_b, L0_xattn_kxln_w, L0_xattn_kxln_b, L0_xattn_wproj, L0_xattn_proj_w_scale, L0_xattn_proj_in_scale, L0_xattn_proj_smooth, L0_ffn_Wr, L0_ffn_Wg, L0_ffn_Wu, L0_ffn_Wd):
    import jax
    import jax.numpy as jnp

    def _L0_xattn_ref(hidden_states, cond, ln_w, ln_b, wq, wq_scale, q_in_scale, wqx, wqx_scale, qx_in_scale, wk, wk_scale, k_in_scale, wv, wv_scale, v_in_scale, w_kv_x, qln_w, qln_b, kln_w, kln_b, qxln_w, qxln_b, kxln_w, kxln_b, wproj, proj_w_scale, proj_in_scale, proj_smooth):
        import jax, jax.numpy as jnp
        import numpy as np
        FP8_MAX = 448.0
        EPS = 1e-05

        def _fp8_roundtrip(x):
            return x.astype(jnp.float8_e4m3fn).astype(jnp.float32)

        def _div_clamp_fp8(x, scale):
            y = jnp.clip(x.astype(jnp.float32) / scale, -FP8_MAX, FP8_MAX)
            y = y.astype(jnp.bfloat16).astype(jnp.float32)
            return _fp8_roundtrip(y)

        def _ln(x, w, b):
            mu = jnp.mean(x, axis=-1, keepdims=True)
            var = jnp.mean(jnp.square(x - mu), axis=-1, keepdims=True)
            return (x - mu) * jax.lax.rsqrt(var + EPS) * w + b

        def _fp8_linear_pertensor(x, wq, w_scale, in_scale):
            xq = _div_clamp_fp8(x, in_scale)
            return jnp.einsum('bsi,oi->bso', xq * in_scale, wq) * w_scale

        def _gqa(q, k, v):
            scale = 1.0 / np.sqrt(q.shape[-1])
            scores = jnp.einsum('bsghd,btgd->bghst', q, k) * scale
            p = jax.nn.softmax(scores, axis=-1)
            return jnp.einsum('bghst,btgd->bsghd', p, v)
        b, s, _ = hidden_states.shape
        sc = cond.shape[1]
        d = qln_w.shape[0]
        nh = wq.shape[0] // d
        g = wk.shape[0] // d
        hpg = nh // g
        ln_out = _ln(hidden_states, ln_w, ln_b)
        q = _fp8_linear_pertensor(ln_out, wq, wq_scale, q_in_scale).reshape(b, s, g, hpg, d)
        q = _ln(q, qln_w, qln_b)
        k = _fp8_linear_pertensor(ln_out, wk, wk_scale, k_in_scale).reshape(b, s, g, d)
        k = _ln(k, kln_w, kln_b)
        v = _fp8_linear_pertensor(ln_out, wv, wv_scale, v_in_scale).reshape(b, s, g, d)
        core = _gqa(q, k, v).reshape(b, s, nh * d)
        qx = _fp8_linear_pertensor(ln_out, wqx, wqx_scale, qx_in_scale).reshape(b, s, g, hpg, d)
        qx = _ln(qx, qxln_w, qxln_b)
        kvx = jnp.einsum('bsi,oi->bso', cond, w_kv_x)
        kx, vx = jnp.split(kvx, 2, axis=-1)
        kx = _ln(kx.reshape(b, sc, g, d), kxln_w, kxln_b)
        vx = vx.reshape(b, sc, g, d)
        xout = _gqa(qx, kx, vx).reshape(b, s, nh * d)
        cat = jnp.concatenate([core, xout], axis=-1)
        catq = _div_clamp_fp8(cat, proj_smooth)
        return jnp.einsum('bsi,oi->bso', catq, wproj) * (proj_in_scale * proj_w_scale)

    def _L0_ffn_ref(x, Wr, Wg, Wu, Wd):
        import jax, jax.numpy as jnp
        import numpy as np
        B, T, D = (4, 512, 512)
        E = 8
        K = 2
        F = 2048 // (E // 2)
        probs = jax.nn.softmax(x @ Wr, axis=-1)
        topk_w, topk_idx = jax.lax.top_k(probs, K)
        topk_w = topk_w / jnp.sum(topk_w, axis=-1, keepdims=True)
        output = jnp.zeros_like(x)
        for i in range(E):
            sel = topk_idx == i
            w_i = jnp.sum(topk_w * sel.astype(x.dtype), axis=-1, keepdims=True)
            h = jax.nn.silu(x @ Wg[i]) * (x @ Wu[i])
            e_out = h @ Wd[i]
            output = output + w_i * e_out
        return output
    x = x + jnp.tanh(g_xattn[0]) * _L0_xattn_ref(_layernorm(x, axis=-1), ctx_2048, L0_xattn_ln_w, L0_xattn_ln_b, L0_xattn_wq, L0_xattn_wq_scale, L0_xattn_q_in_scale, L0_xattn_wqx, L0_xattn_wqx_scale, L0_xattn_qx_in_scale, L0_xattn_wk, L0_xattn_wk_scale, L0_xattn_k_in_scale, L0_xattn_wv, L0_xattn_wv_scale, L0_xattn_v_in_scale, L0_xattn_w_kv_x, L0_xattn_qln_w, L0_xattn_qln_b, L0_xattn_kln_w, L0_xattn_kln_b, L0_xattn_qxln_w, L0_xattn_qxln_b, L0_xattn_kxln_w, L0_xattn_kxln_b, L0_xattn_wproj, L0_xattn_proj_w_scale, L0_xattn_proj_in_scale, L0_xattn_proj_smooth)
    x = x + jnp.tanh(g_ffn[0]) * _L0_ffn_ref(_layernorm(x, axis=-1), L0_ffn_Wr, L0_ffn_Wg, L0_ffn_Wu, L0_ffn_Wd)
    return x

_drawn_inputs = setup_inputs


def setup_inputs(seed=0):
    import zlib

    import numpy as np

    out = dict(_drawn_inputs(seed))
    spreads = {'L0_xattn_ln_w': (1.0, 0.2),
     'L0_xattn_ln_b': (0.0, 0.1),
     'L0_xattn_q_in_scale': (0.05000000074505806, 0.6),
     'L0_xattn_qx_in_scale': (0.05000000074505806, 0.6),
     'L0_xattn_k_in_scale': (0.05000000074505806, 0.6),
     'L0_xattn_v_in_scale': (0.05000000074505806, 0.6),
     'L0_xattn_qln_w': (1.0, 0.547),
     'L0_xattn_qln_b': (0.0, 0.445),
     'L0_xattn_kln_w': (1.0, 0.2),
     'L0_xattn_kln_b': (0.0, 2.0),
     'L0_xattn_qxln_w': (1.0, 0.2),
     'L0_xattn_qxln_b': (0.0, 0.362),
     'L0_xattn_kxln_w': (1.0, 0.2),
     'L0_xattn_kxln_b': (0.0, 2.0),
     'L0_xattn_proj_smooth': (0.05000000074505806, 0.2)}
    factors = {}
    for name, (base, spread) in spreads.items():
        noise = np.random.default_rng([zlib.crc32(name.encode()), seed]).standard_normal(out[name].shape)
        drawn = base * np.exp(spread * noise) if base else spread * noise
        out[name] = jnp.asarray(drawn.astype(out[name].dtype))
    for name, factor in factors.items():
        out[name] = (out[name] * factor).astype(out[name].dtype)
    return out
```

```python
from contextlib import ExitStack

import concourse.bass as bass
from concourse import mybir

F32 = mybir.dt.float32
F32R = mybir.dt.float32r
BF16 = mybir.dt.bfloat16
U16 = mybir.dt.uint16
U32 = mybir.dt.uint32
ALU = mybir.AluOpType
ACT = mybir.ActivationFunctionType
AX = mybir.AxisListType.X

P = 128
B, T, D = 8, 112, 512
TC, NC = 375, 3
CT = TC // NC
KB = D // P
NH, G, HD = 16, 8, 128
HPG = NH // G
GP = 4
HP = NH // GP
NT = B * T
EX, FF = 8, 512
FB = FF // P
HALF = NT // 2
EPS = 1e-5
SCALE = float(HD) ** -0.5
FP8_MAX = 448.0

CQ, CQX, CK, CKX, CVX, CV = 0, 512, 1024, 1280, 1536, 1792
WC = 2048
LNC = 1536

V_LNW, V_LNB, V_SQ, V_SQX, V_SK, V_SV = 0, 4, 8, 12, 16, 20
V_QW, V_QB, V_KW, V_KB, V_QXW, V_QXB, V_KXW, V_KXB = range(24, 32)
NV = 32
S_WQ, S_WQX, S_WK, S_WV, S_PIN, S_PW, S_GX, S_GF = range(8)


def transformer_block(nc, x, ctxT, vecs, scalars, smooth, w_in, wproj, Wr, Wg, Wu, Wd, out):
    catd = nc.dram_tensor("cat_scratch", (GP * B, P, 8 * T), BF16)
    cat_w = catd.ap() if hasattr(catd, "ap") else catd
    with ExitStack() as top:
        def sb(ctx, name, shape, dt=F32):
            return ctx.enter_context(nc.sbuf_tensor(name, shape, dt))

        def ps(ctx, name, shape, dt=F32):
            return ctx.enter_context(nc.psum_tensor(name, shape, dt))

        def sem(ctx, name):
            return ctx.enter_context(nc.semaphore(name))

        vec = sb(top, "vec", [P, NV])
        scal = sb(top, "scal", [P, 8])
        gate = sb(top, "gate", [P, 2])
        proj_scale = sb(top, "proj_scale", [P, 1])
        ident = sb(top, "ident", [P, P])
        mhalf = sb(top, "mhalf", [P, 16])
        epst = sb(top, "epst", [P, 16])

        with ExitStack() as c:
            xq = sb(c, "xq", [P, 4, KB, NT], BF16)
            smi = sb(c, "smi", [P, GP, 8])
            wsc = sb(c, "wsc", [P, 4, KB])
            with ExitStack() as c0:
                quantise_inputs(nc, c0, sb, ps, sem, x, vecs, scalars, smooth, vec, scal, gate,
                                proj_scale, ident, mhalf, epst, xq, smi, wsc)
            with ExitStack() as c1:
                attention(nc, c1, sb, ps, sem, ctxT, w_in, cat_w, vec, ident, mhalf, epst, xq, smi, wsc)
        with ExitStack() as c:
            x1 = sb(c, "x1", [P, B, D])
            xT = sb(c, "xT", [P, KB, NT])
            xhi = sb(c, "xhi", [P, KB, NT], F32R)
            xlo = sb(c, "xlo", [P, KB, NT], F32R)
            coef = sb(c, "coef", [P, B, EX])
            with ExitStack() as c2:
                projection(nc, c2, sb, ps, sem, x, wproj, cat_w, Wr, ident, mhalf, gate, proj_scale,
                           x1, xT, xhi, xlo, coef)
            with ExitStack() as c3:
                experts(nc, c3, sb, ps, sem, Wg, Wu, Wd, x1, xhi, xlo, coef, out)


def quantise_inputs(nc, c, sb, ps, sem, x, vecs, scalars, smooth, vec, scal, gate, proj_scale,
                    ident, mhalf, epst, xq, smi, wsc):
    xs = sb(c, "xs", [P, B, D])
    st = sb(c, "st", [P, B, 6])
    mv = sb(c, "mv", [P, B, 2])
    mv2 = sb(c, "mv2", [P, B, 2])
    rstd = sb(c, "rstd", [P, 2, B])
    hT = sb(c, "hT", [P, KB, NT])
    inv = sb(c, "inv", [P, 4, KB])
    smr = sb(c, "smr", [P, GP, 8])
    yq = sb(c, "yq", [P, KB, NT], BF16)
    ye = sb(c, "ye", [P, KB, NT], BF16)
    ysum = sb(c, "ysum", [P, KB, NT])
    pt = ps(c, "pt", [P, 2, 512])

    vec_in = sem(c, "vec_in")
    x_in = [sem(c, f"x_in{b}") for b in range(B)]
    const_done = sem(c, "const_done")
    pool_self = sem(c, "pool_self")
    stat_done = sem(c, "stat_done")
    rstd_done = sem(c, "rstd_done")
    dve = sem(c, "dve_chain0")
    norm_done = sem(c, "norm_done")
    tr_done = sem(c, "tr_done")
    hT_done = sem(c, "hT_done")
    scal_done = sem(c, "scal_done")
    block = c.enter_context(nc.Block())

    @block.sync
    def _(sp):
        sp.dma_start(vec[:, :], vecs).then_inc(vec_in, 16)
        sp.dma_start(scal[:, :], scalars.partition_broadcast(P)).then_inc(vec_in, 16)
        sp.dma_start(smr[:, :, :], smooth).then_inc(vec_in, 16)
        for b in range(B):
            sp.dma_start(xs[0:T, b, :], x[b]).then_inc(x_in[b], 16)

    @block.gpsimd
    def _(pool):
        pool.memset(ident[:, :], 0.0).then_inc(pool_self, 1)
        pool.memset(mhalf[:, :], -0.5).then_inc(pool_self, 1)
        pool.memset(epst[:, :], EPS).then_inc(pool_self, 1)
        pool.wait_ge(pool_self, 3)
        pool.affine_select(out=ident[:, :], in_=ident[:, :], compare_op=ALU.not_equal, fill=1.0,
                           base=0, pattern=[[-1, P]], channel_multiplier=1).then_inc(const_done, 1)
        for n, m in enumerate((mv, mv2)):
            pool.wait_ge(stat_done, n + 1)
            pool.tensor_tensor(rstd[0:T, n, :], m[0:T, :, 1], mhalf[0:T, 0:B],
                               ALU.pow).then_inc(rstd_done, 1)

    @block.scalar
    def _(act):
        act.wait_ge(vec_in, 48)
        act.activation(gate[:, :], scal[:, S_GX:S_GF + 1], ACT.Tanh).then_inc(scal_done, 1)
        for n in range(2 * KB):
            k, h = n // 2, n % 2
            act.wait_ge(tr_done, n + 1)
            act.activation(hT[:, k, h * HALF:(h + 1) * HALF], pt[:, n % 2, 0:HALF], ACT.Identity,
                           bias=vec[:, V_LNB + k:V_LNB + k + 1],
                           scale=vec[:, V_LNW + k:V_LNW + k + 1]).then_inc(hT_done, 1)

    @block.tensor
    def _(pe):
        pe.wait_ge(const_done, 1)
        pe.wait_ge(norm_done, 1)
        for n in range(2 * KB):
            k, h = n // 2, n % 2
            if n >= 2:
                pe.wait_ge(hT_done, n - 1)
            for b in range(4):
                t = pe.transpose(pt[:, n % 2, b * T:(b + 1) * T], xs[0:T, 4 * h + b, k * P:(k + 1) * P],
                                 ident[0:T, 0:T])
            t.then_inc(tr_done, 1)

    @block.vector
    def _(v):
        count = [0]

        def link(ins):
            count[0] += 1
            ins.then_inc(dve, 1)
            v.wait_ge(dve, count[0])

        for b in range(B):
            v.wait_ge(x_in[b], 16)
            last = v.bn_stats(st[0:T, b, :], xs[0:T, b, :])
        link(last)
        for b in range(B):
            last = v.bn_aggr(mv[0:T, b, :], st[0:T, b, :])
        link(last)
        v.tensor_scalar(mv[0:T, :, 1], mv[0:T, :, 1], EPS, None, ALU.add).then_inc(stat_done, 1)
        v.wait_ge(vec_in, 48)
        link(v.reciprocal(inv[:, :, :].rearrange("p a b -> p (a b)"), vec[:, V_SQ:V_SV + KB]))
        link(v.reciprocal(smi[:, :, :], smr[:, :, :]))
        for n in range(4):
            last = v.tensor_scalar(wsc[:, n, :], vec[:, V_SQ + 4 * n:V_SQ + 4 * n + 4],
                                   scal[:, S_WQ + n:S_WQ + n + 1], None, ALU.mult)
        link(last)
        for col in (V_KW, V_KB, V_KXW, V_KXB):
            last = v.tensor_scalar(vec[:, col:col + 1], vec[:, col:col + 1], SCALE, None, ALU.mult)
        link(last)
        link(v.tensor_tensor(proj_scale[:, :], scal[:, S_PIN:S_PIN + 1], scal[:, S_PW:S_PW + 1], ALU.mult))
        v.wait_ge(scal_done, 1)
        link(v.tensor_tensor(proj_scale[:, :], proj_scale[:, :], gate[:, 0:1], ALU.mult))
        v.wait_ge(rstd_done, 1)
        for b in range(B):
            last = v.tensor_scalar(xs[0:T, b, :], xs[0:T, b, :], mv[0:T, b, 0:1], rstd[0:T, 0, b:b + 1],
                                   ALU.subtract, ALU.mult)
        link(last)
        for b in range(B):
            last = v.bn_stats(st[0:T, b, :], xs[0:T, b, :])
        link(last)
        for b in range(B):
            last = v.bn_aggr(mv2[0:T, b, :], st[0:T, b, :])
        link(last)
        v.tensor_scalar(mv2[0:T, :, 1], mv2[0:T, :, 1], EPS, None, ALU.add).then_inc(stat_done, 1)
        v.wait_ge(rstd_done, 2)
        for b in range(B):
            last = v.tensor_scalar(xs[0:T, b, :], xs[0:T, b, :], mv2[0:T, b, 0:1], rstd[0:T, 1, b:b + 1],
                                   ALU.subtract, ALU.mult)
        last.then_inc(norm_done, 1)
        v.wait_ge(hT_done, 2 * KB)
        for n in range(4):
            for k in range(KB):
                last = v.tensor_scalar(yq[:, k, :], hT[:, k, :], inv[:, n, k:k + 1], FP8_MAX,
                                       ALU.mult, ALU.min)
            link(last)
            round_fp8(v, link, flat(xq[:, n, :, :]), flat(yq[:, :, :]), flat(ye[:, :, :]),
                      flat(ysum[:, :, :]))


def flat(ap):
    return ap.rearrange("p a b -> p (a b)")


def round_fp8(v, link, out, y, e, total):
    link(v.tensor_scalar(y, y, -FP8_MAX, None, ALU.max))
    link(v.tensor_scalar(e.bitcast(U16), y.bitcast(U16), 0x7F80, None, ALU.bitwise_and))
    link(v.tensor_scalar(e, e, 2.0 ** -6, 1.5 * 2.0 ** 20, ALU.max, ALU.mult))
    link(v.tensor_tensor(total, y, e, ALU.add))
    link(v.tensor_tensor(out, total, e, ALU.subtract))


def attention(nc, c, sb, ps, sem, ctxT, w_in, catd, vec, ident, mhalf, epst, xq, smi, wsc):
    w_raw = sb(c, "w_raw", [P, KB, WC])
    w_hi = sb(c, "w_hi", [P, KB, WC], F32R)
    w_lo = sb(c, "w_lo", [P, KB, WC], F32R)
    w_mean = sb(c, "w_mean", [P, KB, LNC // HD])
    smg = sb(c, "smg", [P, 8])
    c_raw = sb(c, "c_raw", [P, NC, KB, CT])
    c_hi = sb(c, "c_hi", [P, NC, KB, CT], F32R)
    c_lo = sb(c, "c_lo", [P, NC, KB, CT], F32R)
    xqs = sb(c, "xqs", [P, 4, KB, T], F32R)
    nq = sb(c, "nq", [P, 512])
    nqx = sb(c, "nqx", [P, 512])
    nk = sb(c, "nk", [P, 256])
    nkx = sb(c, "nkx", [P, NC, 256])
    val = sb(c, "val", [P, 2, 256])
    valx = sb(c, "valx", [P, 2, NC, 256])
    sq = sb(c, "sq", [P, 2, 512])
    ss = sb(c, "ss", [P, 16])
    va = sb(c, "va", [P, 16])
    rs = sb(c, "rs", [P, 16])
    qT = sb(c, "qT", [P, HP * T])
    qxT = sb(c, "qxT", [P, HP * T])
    kT = sb(c, "kT", [P, 2 * T])
    kxT = sb(c, "kxT", [P, 2, TC])
    nmax = sb(c, "nmax", [P, 8])
    lsum = sb(c, "lsum", [P, 8])
    linv = sb(c, "linv", [P, 8])
    pself = sb(c, "pself", [P, HP, T])
    pcross = sb(c, "pcross", [P, HP, TC])
    pselfT = sb(c, "pselfT", [P, HP, T])
    pcrossT = sb(c, "pcrossT", [P, NC, HP, T])
    yb = sb(c, "yb", [P, 8 * T], BF16)
    ye = sb(c, "ye1", [P, 8 * T], BF16)
    ysum = sb(c, "ysum1", [P, 8 * T])
    cat = sb(c, "cat", [P, 8 * T], BF16)

    p_proj = ps(c, "p_proj", [P, 2, 512])
    p_tr = ps(c, "p_tr", [P, 2, 512])
    p_self = ps(c, "p_self", [P, 512])
    p_cross = ps(c, "p_cross", [P, 2, 512])
    p_out = ps(c, "p_out", [P, 512])

    w_in_done = [sem(c, f"w_in{k}") for k in range(KB)]
    c_in_done = [sem(c, f"c_in{k}") for k in range(NC)]
    w_cen = sem(c, "w_cen")
    wh_done = sem(c, "wh_done")
    wl_done = sem(c, "wl_done")
    ch_done = sem(c, "ch_done")
    cl_done = sem(c, "cl_done")
    xqs_done = sem(c, "xqs_done")
    pj_rdy = sem(c, "pj_rdy")
    pj_done = sem(c, "pj_done")
    rd_done = sem(c, "rd_done")
    va_done = sem(c, "va_done")
    rs_done = sem(c, "rs_done")
    ln_done = sem(c, "ln_done")
    tr_rdy = sem(c, "tr_rdy")
    t_done = sem(c, "t_done")
    pt_done = sem(c, "pt_done")
    ss_rdy = sem(c, "ss_rdy")
    ms_done = sem(c, "ms_done")
    es_done = sem(c, "es_done")
    ns_done = sem(c, "ns_done")
    sx_rdy = sem(c, "sx_rdy")
    mx_done = sem(c, "mx_done")
    ex_done = sem(c, "ex_done")
    nx_done = sem(c, "nx_done")
    ou_rdy = sem(c, "ou_rdy")
    ya_done = sem(c, "ya_done")
    ct_done = sem(c, "ct_done")
    cat_out = sem(c, "cat_out")
    dv = sem(c, "dve_chain1")
    chp = sem(c, "dve_chain_w")
    block = c.enter_context(nc.Block())

    def passes(eng, prepare, step):
        with eng.Fori(0, GP) as gp:
            prepare(gp)
            s0 = gp * B
            step(gp, s0, 0, None)
            with eng.Fori(0, 3) as i:
                s = s0 + 2 * i
                step(gp, s + 1, 1, s)
                step(gp, s + 2, 0, s + 1)
            step(gp, s0 + 7, 1, s0 + 6)
            step(gp, None, 0, s0 + 7)

    @block.sync
    def _(sp):
        def load_w(gp, first=False):
            for k in range(KB):
                if not first:
                    sp.wait_ge(wl_done, 4 * gp + k + 1)
                    sp.wait_ge(wh_done, 4 * gp + k + 1)
                sp.dma_start(w_raw[:, k, :], w_in[gp, :, k, :]).then_inc(w_in_done[k], 16)

        def load_c(s, b, k):
            sp.wait_ge(ch_done, 3 * s + k + 1)
            sp.wait_ge(cl_done, 3 * s + k + 1)
            sp.dma_start(c_raw[:, k, :, :], ctxT[b, k]).then_inc(c_in_done[k], 16)

        def store(st):
            sp.wait_ge(ct_done, st + 1)
            sp.dma_start(catd[st], cat[:, :]).then_inc(cat_out, 16)

        load_w(0, first=True)
        with sp.Fori(0, GP - 1) as gp:
            for k in range(NC):
                load_c(gp * B, 0, k)
            with sp.Fori(1, B) as b:
                for k in range(NC):
                    load_c(gp * B + b, b, k)
                store(gp * B + b - 1)
            load_w(gp + 1)
            store(gp * B + B - 1)
        g = GP - 1
        for k in range(NC):
            load_c(g * B, 0, k)
        with sp.Fori(1, B) as b:
            for k in range(NC):
                load_c(g * B + b, b, k)
            store(g * B + b - 1)
        store(g * B + B - 1)
        sp.wait_ge(cat_out, 16 * GP * B)

    @block.gpsimd
    def _(pool):
        pool.sem_inc(cl_done, 3)
        pool.sem_inc(va_done, 6)
        pool.sem_inc(rs_done, 6)

        def rstd(s, j):
            rows, lo, hi = STAT[j]
            pool.wait_ge(rd_done, 6 * (s + 1) + j + 1)
            pool.tensor_tensor(va[0:rows, lo:hi], ss[0:rows, lo:hi], epst[0:rows, lo:hi],
                               ALU.add).then_inc(va_done, 1)
            pool.wait_ge(va_done, 6 * (s + 1) + j + 1)
            pool.wait_ge(ln_done, 6 * s + j + 1)
            pool.tensor_tensor(rs[0:rows, lo:hi], va[0:rows, lo:hi], mhalf[0:rows, lo:hi],
                               ALU.pow).then_inc(rs_done, 1)

        def c_low(s, k):
            pool.wait_ge(ch_done, 3 * (s + 1) + k + 1)
            pool.wait_ge(pj_rdy, 6 * s + 4 + k)
            pool.tensor_tensor(flat(c_lo[:, k, :, :]), flat(c_raw[:, k, :, :]),
                               flat(c_hi[:, k, :, :]).bitcast(F32), ALU.subtract).then_inc(cl_done, 1)

        def step(gp, s, par, t):
            if s is None:
                return
            for j in range(3):
                rstd(s, j)
                c_low(s, j)
            for j in range(3, 6):
                rstd(s, j)

        passes(pool, lambda gp: None, step)

    @block.scalar
    def _(act):
        act.sem_inc(ch_done, 3)
        act.sem_inc(pj_done, 6)
        act.sem_inc(t_done, 5)
        act.sem_inc(es_done, 1)
        act.sem_inc(ex_done, 4)
        act.sem_inc(wh_done, 4)

        def prepare(gp):
            act.wait_ge(pj_rdy, 6 * B * gp + 6)
            for k in range(KB):
                act.wait_ge(w_cen, 4 * gp + k + 1)
                for n, (lo, hi) in enumerate(SCALED):
                    act.activation(w_hi[:, k, lo:hi], w_raw[:, k, lo:hi], ACT.Copy, scale=wsc[:, n, k:k + 1])
                act.activation(w_hi[:, k, CKX:CV], w_raw[:, k, CKX:CV], ACT.Copy).then_inc(wh_done, 1)

        def c_high(s, k):
            act.wait_ge(c_in_done[k], 16 * (s + 1))
            act.wait_ge(pj_rdy, 6 * s + 4 + k)
            act.activation(flat(c_hi[:, k, :, :]), flat(c_raw[:, k, :, :]), ACT.Copy).then_inc(ch_done, 1)

        def take(s, j, par):
            bank = p_proj[:, j % 2, :]
            act.wait_ge(pj_rdy, 6 * (s + 1) + j + 1)
            act.wait_ge(tr_rdy, 10 * s + (j + 1 if j < 3 else 5))
            if j < 2:
                act.activation((nq, nqx)[j][0:T, :], bank[0:T, :], ACT.Copy)
                n, rows = 512, T
            elif j == 2:
                act.wait_ge(ou_rdy, 2 * s)
                act.activation(nk[0:T, :], bank[0:T, 0:256], ACT.Copy)
                act.activation(val[0:T, par, :], bank[0:T, 256:512], ACT.Copy)
                n, rows = 256, T
            else:
                act.activation(nkx[0:CT, j - 3, :], bank[0:CT, 0:256], ACT.Copy)
                act.activation(valx[0:CT, par, j - 3, :], bank[0:CT, 256:512], ACT.Copy)
                n, rows = 256, CT
            act.wait_ge(rd_done, 6 * (s + 1) + j - 1)
            act.activation(sq[0:rows, j % 2, 0:n], bank[0:rows, 0:n], ACT.Square,
                           scale=float(HD) ** -0.5).then_inc(pj_done, 1)

        def turned(t, n):
            act.wait_ge(tr_rdy, 10 * (t + 1) + n + 1)
            if n in (0, 2):
                act.wait_ge(ss_rdy, t + 1)
            else:
                act.wait_ge(sx_rdy, 4 * t + 4)
            dst = (qT[:, :], qxT[:, :], kT[:, :], kxT[:, 0, :], kxT[:, 1, :])[n]
            w, b = ((V_QW, V_QB), (V_QXW, V_QXB), (V_KW, V_KB), (V_KXW, V_KXB), (V_KXW, V_KXB))[n]
            act.activation(dst, p_tr[:, n % 2, 0:TURNED[n]], ACT.Identity, bias=vec[:, b:b + 1],
                           scale=vec[:, w:w + 1]).then_inc(t_done, 1)

        def exp_self(t):
            act.wait_ge(ms_done, t + 2)
            act.wait_ge(tr_rdy, 10 * t + 6)
            act.wait_ge(ns_done, t + 1)
            for h in range(HP):
                last = act.activation(pself[0:T, h, :], p_self[0:T, h * T:(h + 1) * T], ACT.Exp,
                                      bias=nmax[0:T, h:h + 1], accum_out=lsum[0:T, h:h + 1])
            last.then_inc(es_done, 1)

        def exp_cross(t, h):
            act.wait_ge(mx_done, 4 * (t + 1) + h + 1)
            act.wait_ge(tr_rdy, 10 * t + 7 + h)
            act.wait_ge(nx_done, 4 * t + h + 1)
            act.activation(pcross[0:T, h, :], p_cross[0:T, h % 2, 0:TC], ACT.Exp,
                           bias=nmax[0:T, 4 + h:5 + h], accum_out=lsum[0:T, 4 + h:5 + h]).then_inc(ex_done, 1)

        def step(gp, s, par, t):
            if s is not None:
                for k in range(NC):
                    c_high(s, k)
                take(s, 0, par)
            if t is not None:
                turned(t, 0)
                turned(t, 1)
            if s is not None:
                take(s, 1, par)
            if t is not None:
                turned(t, 2)
                turned(t, 3)
                turned(t, 4)
                exp_self(t)
            if s is not None:
                take(s, 2, par)
            if t is not None:
                exp_cross(t, 0)
                exp_cross(t, 1)
            if s is not None:
                take(s, 3, par)
            if t is not None:
                exp_cross(t, 2)
                exp_cross(t, 3)
            if s is not None:
                take(s, 4, par)
                take(s, 5, par)

        passes(act, prepare, step)

    @block.tensor
    def _(pe):
        pe.sem_inc(pj_rdy, 6)
        pe.sem_inc(tr_rdy, 10)
        pe.sem_inc(ss_rdy, 1)
        pe.sem_inc(sx_rdy, 4)
        pe.sem_inc(ou_rdy, 2)

        def prepare(gp):
            pe.wait_ge(wl_done, 4 * gp + 8)
            pe.wait_ge(wh_done, 4 * gp + 8)

        def project(s, j):
            pe.wait_ge(pj_done, 6 * (s + 1) + j - 1)
            bank = p_proj[:, j % 2, :]
            if j == 0:
                pe.wait_ge(xqs_done, s + 1)
            if j < 3:
                for n, o, lo, w in (((0, 0, CQ, 512),), ((1, 0, CQX, 512),),
                                    ((2, 0, CK, 256), (3, 256, CV, 256)))[j]:
                    for i in range(2 * KB):
                        k = i // 2
                        m = pe.matmul(bank[0:T, o:o + w], xqs[:, n, k, :], (w_hi, w_lo)[i % 2][:, k, lo:lo + w],
                                      start=(i == 0), stop=(i == 2 * KB - 1))
            else:
                ch = j - 3
                pe.wait_ge(ch_done, 3 * (s + 1) + ch + 1)
                pe.wait_ge(cl_done, 3 * (s + 1) + ch + 1)
                for i in range(3 * KB):
                    k = i // 3
                    a, w = ((c_hi, w_hi), (c_hi, w_lo), (c_lo, w_hi))[i % 3]
                    m = pe.matmul(bank[0:CT, :], a[:, ch, k, :], w[:, k, CKX:CV],
                                  start=(i == 0), stop=(i == 3 * KB - 1))
            m.then_inc(pj_rdy, 1)

        def bank_free(t, n):
            if n < 2:
                pe.wait_ge(pt_done, 5 * t + 4 + n)
            elif n < 7:
                pe.wait_ge(t_done, 5 * (t + 1) + n - 1)
            else:
                pe.wait_ge(pt_done, 5 * (t + 1) + n - 6)

        def turn(t, n):
            pe.wait_ge(ln_done, 6 * (t + 1) + (1, 2, 3, 6, 6)[n])
            bank_free(t, n)
            if n < 3:
                src = (nq, nqx, nk)[n]
                for h in range((4, 4, 2)[n]):
                    m = pe.transpose(p_tr[:, n % 2, h * T:(h + 1) * T], src[0:T, h * P:(h + 1) * P],
                                     ident[0:T, 0:T])
            else:
                for k in range(NC):
                    m = pe.transpose(p_tr[:, n % 2, k * CT:(k + 1) * CT],
                                     nkx[0:CT, k, (n - 3) * P:(n - 2) * P], ident[0:CT, 0:CT])
            m.then_inc(tr_rdy, 1)

        def score_self(t):
            pe.wait_ge(t_done, 5 * (t + 1) + 3)
            pe.wait_ge(es_done, t + 1)
            for h in range(HP):
                m = pe.matmul(p_self[0:T, h * T:(h + 1) * T], qT[:, h * T:(h + 1) * T],
                              kT[:, h // HPG * T:(h // HPG + 1) * T], start=True, stop=True)
            m.then_inc(ss_rdy, 1)

        def score_cross(t, h):
            pe.wait_ge(t_done, 5 * (t + 1) + 4 + h // HPG)
            pe.wait_ge(ex_done, 4 * (t + 1) + h - 1)
            pe.matmul(p_cross[0:T, h % 2, 0:TC], qxT[:, h * T:(h + 1) * T], kxT[:, h // HPG, :],
                      start=True, stop=True).then_inc(sx_rdy, 1)

        def turn_self(t):
            pe.wait_ge(ns_done, t + 2)
            bank_free(t, 5)
            for h in range(HP):
                m = pe.transpose(p_tr[0:T, 1, h * T:(h + 1) * T], pself[0:T, h, :], ident[0:T, 0:T])
            m.then_inc(tr_rdy, 1)

        def turn_cross(t, h):
            pe.wait_ge(nx_done, 4 * (t + 1) + h + 1)
            bank_free(t, 6 + h)
            for k in range(NC):
                m = pe.transpose(p_tr[0:CT, h % 2, k * T:(k + 1) * T], pcross[0:T, h, k * CT:(k + 1) * CT],
                                 ident[0:T, 0:T])
            m.then_inc(tr_rdy, 1)

        def outputs(t, g, par):
            pe.wait_ge(pt_done, 5 * (t + 1) + (3, 5)[g])
            pe.wait_ge(pj_done, 6 * (t + 1) + 6)
            pe.wait_ge(ya_done, 2 * (t + 1) + g)
            pe.matmul(p_out[:, 0:HPG * T], val[0:T, par, g * P:(g + 1) * P],
                      flat(pselfT[0:T, HPG * g:HPG * (g + 1), :]), start=True, stop=True)
            for k in range(NC):
                m = pe.matmul(p_out[:, HPG * T:2 * HPG * T], valx[0:CT, par, k, g * P:(g + 1) * P],
                              flat(pcrossT[0:CT, k, HPG * g:HPG * (g + 1), :]),
                              start=(k == 0), stop=(k == NC - 1))
            m.then_inc(ou_rdy, 1)

        def step(gp, s, par, t):
            if s is not None:
                project(s, 0)
            if t is not None:
                turn(t, 0)
                turn(t, 1)
            if s is not None:
                project(s, 1)
            if t is not None:
                turn(t, 2)
                turn(t, 3)
                turn(t, 4)
                score_self(t)
            if s is not None:
                project(s, 2)
            if t is not None:
                score_cross(t, 0)
                score_cross(t, 1)
                turn_self(t)
            if s is not None:
                project(s, 3)
            if t is not None:
                turn_cross(t, 0)
                score_cross(t, 2)
                turn_cross(t, 1)
                score_cross(t, 3)
            if s is not None:
                project(s, 4)
            if t is not None:
                outputs(t, 0, 1 - par)
                turn_cross(t, 2)
                turn_cross(t, 3)
            if s is not None:
                project(s, 5)
            if t is not None:
                outputs(t, 1, 1 - par)

        passes(pe, prepare, step)

    @block.vector
    def _(v):
        v.sem_inc(rd_done, 6)
        v.sem_inc(ln_done, 6)
        v.sem_inc(pt_done, 5)
        v.sem_inc(ms_done, 1)
        v.sem_inc(ns_done, 1)
        v.sem_inc(mx_done, 4)
        v.sem_inc(nx_done, 4)
        v.sem_inc(ya_done, 2)
        v.sem_inc(wl_done, 4)
        CH, CHP = 9, 8

        def prepare(gp):
            v.tensor_copy(smg[:, :], smi[:, gp, :])
            for k in range(KB):
                raw = w_raw[:, k, 0:LNC].rearrange("p (h d) -> p h d", d=HD)
                v.wait_ge(w_in_done[k], 16 * (gp + 1))
                v.tensor_reduce(w_mean[:, k, :], raw, AX, ALU.add).then_inc(chp, 1)
                v.wait_ge(chp, CHP * gp + 2 * k + 1)
                v.tensor_scalar(w_mean[:, k, :], w_mean[:, k, :], 1.0 / HD, None, ALU.mult).then_inc(chp, 1)
                v.wait_ge(chp, CHP * gp + 2 * k + 2)
                v.tensor_tensor(raw, raw, w_mean[:, k, :].unsqueeze(2).to_broadcast([P, LNC // HD, HD]),
                                ALU.subtract).then_inc(w_cen, 1)
            for k in range(KB):
                v.wait_ge(wh_done, 4 * (gp + 1) + k + 1)
                for n, (lo, hi) in enumerate(SCALED):
                    v.scalar_tensor_tensor(out=w_lo[:, k, lo:hi], in0=w_raw[:, k, lo:hi],
                                           scalar=wsc[:, n, k:k + 1], in1=w_hi[:, k, lo:hi].bitcast(F32),
                                           op0=ALU.mult, op1=ALU.subtract)
                v.tensor_tensor(w_lo[:, k, CKX:CV], w_raw[:, k, CKX:CV], w_hi[:, k, CKX:CV].bitcast(F32),
                                ALU.subtract).then_inc(wl_done, 1)

        def inputs(s, b):
            v.wait_ge(pj_rdy, 6 * s + 3)
            for n in range(4):
                last = v.tensor_copy(xqs[:, n, :, :], xq[:, n, :, bass.ds(b * T, T)])
            last.then_inc(xqs_done, 1)

        def sums(s, j):
            rows, lo, hi = STAT[j]
            v.wait_ge(pj_done, 6 * (s + 1) + j + 1)
            v.wait_ge(va_done, 6 * s + j + 1)
            v.tensor_reduce(ss[0:rows, lo:hi],
                            sq[0:rows, j % 2, 0:(hi - lo) * HD].rearrange("p (h d) -> p h d", d=HD),
                            AX, ALU.add).then_inc(rd_done, 1)

        def scale(s, j):
            rows, lo, hi = STAT[j]
            v.wait_ge(rs_done, 6 * (s + 1) + j + 1)
            buf = (nq[0:T, :], nqx[0:T, :], nk[0:T, :], nkx[0:CT, 0, :], nkx[0:CT, 1, :], nkx[0:CT, 2, :])[j]
            buf = buf.rearrange("p (h d) -> p h d", d=HD)
            v.tensor_tensor(buf, buf, rs[0:rows, lo:hi].unsqueeze(2).to_broadcast([rows, hi - lo, HD]),
                            ALU.mult).then_inc(ln_done, 1)

        def max_self(t):
            v.wait_ge(ss_rdy, t + 2)
            v.wait_ge(es_done, t + 1)
            v.tensor_reduce(nmax[0:T, 0:HP], p_self[0:T, 0:HP * T].rearrange("p (h d) -> p h d", d=T),
                            AX, ALU.max, negate=True).then_inc(ms_done, 1)

        def norm_self(t):
            v.wait_ge(es_done, t + 2)
            v.wait_ge(tr_rdy, 10 * t + 6)
            v.reciprocal(linv[0:T, 0:HP], lsum[0:T, 0:HP]).then_inc(dv, 1)
            v.wait_ge(dv, CH * t + 1)
            v.tensor_tensor(pself[0:T, :, :], pself[0:T, :, :],
                            linv[0:T, 0:HP].unsqueeze(2).to_broadcast([T, HP, T]), ALU.mult).then_inc(ns_done, 1)

        def max_cross(t, h):
            v.wait_ge(sx_rdy, 4 * (t + 1) + h + 1)
            v.wait_ge(ex_done, 4 * t + h + 1)
            v.tensor_reduce(nmax[0:T, 4 + h:5 + h], p_cross[0:T, h % 2, 0:TC], AX, ALU.max,
                            negate=True).then_inc(mx_done, 1)

        def norm_cross(t, h):
            v.wait_ge(ex_done, 4 * (t + 1) + h + 1)
            v.reciprocal(linv[0:T, 4 + h:5 + h], lsum[0:T, 4 + h:5 + h]).then_inc(dv, 1)
            v.wait_ge(dv, CH * t + 2 + h)
            v.tensor_scalar(pcross[0:T, h, :], pcross[0:T, h, :], linv[0:T, 4 + h:5 + h], None,
                            ALU.mult).then_inc(nx_done, 1)

        def take_self(t):
            v.wait_ge(tr_rdy, 10 * (t + 1) + 6)
            v.wait_ge(ou_rdy, 2 * t + 2)
            v.tensor_copy(flat(pselfT[0:T, :, :]), p_tr[0:T, 1, 0:HP * T]).then_inc(pt_done, 1)

        def take_cross(t, h):
            v.wait_ge(tr_rdy, 10 * (t + 1) + 7 + h)
            v.wait_ge(ou_rdy, 2 * t + 2)
            v.tensor_copy(pcrossT[0:CT, :, h, :],
                          p_tr[0:CT, h % 2, 0:NC * T].rearrange("p (k t) -> p k t", k=NC)).then_inc(pt_done, 1)

        def smoothed(t, g):
            v.wait_ge(ou_rdy, 2 * (t + 1) + g + 1)
            v.tensor_tensor(yb[:, g * 4 * T:(g + 1) * 4 * T].rearrange("p (a t) -> p a t", t=T),
                            p_out[:, 0:4 * T].rearrange("p (a t) -> p a t", t=T),
                            smg[:, 4 * g:4 * g + 4].unsqueeze(2).to_broadcast([P, 4, T]),
                            ALU.mult).then_inc(ya_done, 1)

        def rounded(t):
            v.wait_ge(ya_done, 2 * (t + 1) + 2)
            v.tensor_scalar(yb[:, :], yb[:, :], FP8_MAX, -FP8_MAX, ALU.min, ALU.max).then_inc(dv, 1)
            v.wait_ge(dv, CH * t + 6)
            v.tensor_scalar(ye[:, :].bitcast(U16), yb[:, :].bitcast(U16), 0x7F80, None,
                            ALU.bitwise_and).then_inc(dv, 1)
            v.wait_ge(dv, CH * t + 7)
            v.tensor_scalar(ye[:, :], ye[:, :], 2.0 ** -6, 1.5 * 2.0 ** 20, ALU.max, ALU.mult).then_inc(dv, 1)
            v.wait_ge(dv, CH * t + 8)
            v.tensor_tensor(ysum[:, :], yb[:, :], ye[:, :], ALU.add).then_inc(dv, 1)
            v.wait_ge(dv, CH * t + 9)
            v.wait_ge(cat_out, 16 * t)
            v.tensor_tensor(cat[:, :], ysum[:, :], ye[:, :], ALU.subtract).then_inc(ct_done, 1)

        def step(s, t, b_next):
            if s is not None:
                sums(s, 0)
                sums(s, 1)
                scale(s, 0)
                scale(s, 1)
            if t is not None:
                max_self(t)
            if s is not None:
                sums(s, 2)
            if t is not None:
                norm_self(t)
                max_cross(t, 0)
                max_cross(t, 1)
            if s is not None:
                scale(s, 2)
                if b_next is not None:
                    inputs(s + 1, b_next)
            if t is not None:
                take_self(t)
                norm_cross(t, 0)
                norm_cross(t, 1)
            if s is not None:
                sums(s, 3)
            if t is not None:
                take_cross(t, 0)
                max_cross(t, 2)
                take_cross(t, 1)
                max_cross(t, 3)
            if s is not None:
                scale(s, 3)
            if t is not None:
                norm_cross(t, 2)
                norm_cross(t, 3)
            if s is not None:
                sums(s, 4)
                scale(s, 4)
            if t is not None:
                smoothed(t, 0)
                take_cross(t, 2)
                take_cross(t, 3)
            if s is not None:
                sums(s, 5)
                scale(s, 5)
            if t is not None:
                smoothed(t, 1)
                rounded(t)

        with v.Fori(0, GP) as gp:
            prepare(gp)
            s0 = gp * B
            inputs(s0, 0)
            step(s0, None, 1)
            with v.Fori(0, 3) as i:
                s = s0 + 2 * i
                step(s + 1, s, 2 * i + 2)
                step(s + 2, s + 1, 2 * i + 3)
            step(s0 + 7, s0 + 6, None)
            step(None, s0 + 7, None)


STAT = ((T, 0, 4), (T, 4, 8), (T, 8, 10), (CT, 10, 12), (CT, 12, 14), (CT, 14, 16))
TURNED = (HP * T, HP * T, 2 * T, TC, TC)
SCALED = ((CQ, CQX), (CQX, CK), (CK, CKX), (CV, WC))


def projection(nc, c, sb, ps, sem, x, wproj, catd, Wr, ident, mhalf, gate, proj_scale,
               x1, xT, xhi, xlo, coef):
    NB = 8
    w_raw = sb(c, "p_raw", [P, 4, D])
    w_hi = sb(c, "p_hi", [P, 2, D], F32R)
    w_lo = sb(c, "p_lo", [P, 2, D], F32R)
    cat = sb(c, "p_cat", [P, 2, B, NB * T], BF16)
    catr = sb(c, "p_catr", [P, 2, B, T], F32R)
    xs = sb(c, "xs1", [P, B, D])
    st = sb(c, "st1", [P, B, 6])
    mv = sb(c, "mv1", [P, B, 2])
    rstd = sb(c, "rstd1", [P, B])
    wr = sb(c, "wr", [P, KB, EX])
    lg = sb(c, "lg", [P, B, EX])
    pr = sb(c, "pr", [P, B, EX])
    m1 = sb(c, "m1", [P, B])
    top = sb(c, "top", [P, B, EX])
    idx = sb(c, "idx", [P, B, EX], U32)
    idf = sb(c, "idf", [P, B, EX])
    iota = sb(c, "iota", [P, EX])
    sel = sb(c, "sel", [P, B, EX])
    acc = ps(c, "p_acc", [P, B, D])

    x_in = sem(c, "x_in_p")
    wr_in = sem(c, "wr_in")
    w_load = [sem(c, f"pw_load{r}") for r in range(4)]
    cat_load = [sem(c, f"cat_load{r}") for r in range(2)]
    hi_done = sem(c, "ph_done")
    lo_done = sem(c, "pl_done")
    cr_done = sem(c, "cr_done")
    mm_done = sem(c, "pm_done")
    dve = sem(c, "dve_chain2")
    stat_done = sem(c, "stat_done1")
    rstd_done = sem(c, "rstd_done1")
    iota_done = sem(c, "iota_done")
    norm_done = sem(c, "norm_done1")
    tr_done = sem(c, "tr_done1")
    xT_done = sem(c, "xT_done")
    xh_done = sem(c, "xh_done")
    xl_done = sem(c, "xl_done")
    lg_rdy = sem(c, "lg_rdy")
    lg_cen = sem(c, "lg_cen")
    ex_done = sem(c, "lg_exp")
    block = c.enter_context(nc.Block())
    N = 2 * NB

    @block.sync
    def _(sp):
        sp.dma_start(xs[0:T, :, :], x.rearrange("b t d -> t b d")).then_inc(x_in, 16)
        sp.dma_start(wr[:, :, :], Wr.rearrange("(k p) e -> p k e", p=P)).then_inc(wr_in, 16)
        with sp.Fori(0, GP // 2) as i:
            for n in range(N):
                if n % NB == 0:
                    r = n // NB
                    sp.wait_ge(cr_done, N * i + NB * (r + 1))
                    sp.dma_start(cat[:, r, :, :], catd[bass.ds((2 * i + r) * B, B)].rearrange("b p n -> p b n")
                                 ).then_inc(cat_load[r], 16)
                sp.wait_ge(hi_done, N * (i + 1) + n - 3)
                sp.wait_ge(lo_done, N * (i + 1) + n - 3)
                sp.dma_start(w_raw[:, n % 4, :], wproj[2 * i + n // NB, n % NB]).then_inc(w_load[n % 4], 16)

    @block.gpsimd
    def _(pool):
        pool.iota(iota[:, :], pattern=[[1, EX]], base=0, channel_multiplier=0,
                  allow_small_or_imprecise_dtypes=True).then_inc(iota_done, 1)
        pool.wait_ge(stat_done, 1)
        pool.tensor_tensor(rstd[0:T, :], mv[0:T, :, 1], mhalf[0:T, 0:B], ALU.pow).then_inc(rstd_done, 1)

    @block.scalar
    def _(act):
        act.sem_inc(hi_done, N)
        with act.Fori(0, GP // 2) as i:
            for n in range(N):
                act.wait_ge(w_load[n % 4], 64 * i + 16 * (n // 4 + 1))
                act.wait_ge(mm_done, N * (i + 1) + n - 1)
                act.activation(w_hi[:, n % 2, :], w_raw[:, n % 4, :], ACT.Copy).then_inc(hi_done, 1)
        for n in range(2 * KB):
            k, h = n // 2, n % 2
            act.wait_ge(tr_done, n + 1)
            act.activation(xT[:, k, h * HALF:(h + 1) * HALF], acc[:, n % 2, 0:HALF], ACT.Copy).then_inc(xT_done, 1)
            act.activation(xhi[:, k, h * HALF:(h + 1) * HALF], acc[:, n % 2, 0:HALF], ACT.Copy).then_inc(xh_done, 1)
        act.wait_ge(lg_cen, 1)
        act.activation(pr[0:T, :, :], lg[0:T, :, :], ACT.Exp).then_inc(ex_done, 1)

    @block.tensor
    def _(pe):
        pe.sem_inc(mm_done, N)

        def block_of(i, n, first=False, last=False):
            pe.wait_ge(hi_done, N * (i + 1) + n + 1)
            pe.wait_ge(lo_done, N * (i + 1) + n + 1)
            pe.wait_ge(cr_done, N * (i + 1) + n + 1)
            for b in range(B):
                for part, w in enumerate((w_hi, w_lo)):
                    m = pe.matmul(acc[0:T, b, :], catr[:, n % 2, b, :], w[:, n % 2, :],
                                  start=(first and part == 0), stop=(last and part == 1),
                                  skip_group_check=True)
            m.then_inc(mm_done, 1)

        for n in range(N):
            block_of(0, n, first=(n == 0))
        for n in range(N):
            block_of(1, n, last=(n == N - 1))
        pe.wait_ge(norm_done, 1)
        for n in range(2 * KB):
            k, h = n // 2, n % 2
            if n >= 2:
                pe.wait_ge(xh_done, n - 1)
                pe.wait_ge(xl_done, n - 1)
            for b in range(4):
                t = pe.transpose(acc[:, n % 2, b * T:(b + 1) * T], xs[0:T, 4 * h + b, k * P:(k + 1) * P],
                                 ident[0:T, 0:T])
            t.then_inc(tr_done, 1)
        pe.wait_ge(xT_done, 2 * KB)
        pe.wait_ge(wr_in, 16)
        for b in range(B):
            for k in range(KB):
                m = pe.matmul(acc[0:T, 2, b * EX:(b + 1) * EX], xT[:, k, b * T:(b + 1) * T], wr[:, k, :],
                              start=(k == 0), stop=(k == KB - 1))
        m.then_inc(lg_rdy, 1)

    @block.vector
    def _(v):
        v.sem_inc(lo_done, N)
        v.sem_inc(cr_done, N)
        with v.Fori(0, GP // 2) as i:
            for n in range(N):
                r, j = n // NB, n % NB
                v.wait_ge(cat_load[r], 16 * (i + 1))
                v.wait_ge(mm_done, N * (i + 1) + n - 1)
                v.tensor_copy(catr[:, n % 2, :, :], cat[:, r, :, j * T:(j + 1) * T]).then_inc(cr_done, 1)
                v.wait_ge(hi_done, N * (i + 1) + n + 1)
                v.tensor_tensor(w_lo[:, n % 2, :], w_raw[:, n % 4, :], w_hi[:, n % 2, :].bitcast(F32),
                                ALU.subtract).then_inc(lo_done, 1)
        count = [0]

        def link(ins):
            count[0] += 1
            ins.then_inc(dve, 1)
            v.wait_ge(dve, count[0])

        v.wait_ge(mm_done, N * (GP // 2 + 1))
        v.wait_ge(x_in, 16)
        for b in range(B):
            last = v.scalar_tensor_tensor(out=x1[0:T, b, :], in0=acc[0:T, b, :], scalar=proj_scale[0:T, 0:1],
                                          in1=xs[0:T, b, :], op0=ALU.mult, op1=ALU.add)
        link(last)
        for b in range(B):
            last = v.bn_stats(st[0:T, b, :], x1[0:T, b, :])
        link(last)
        for b in range(B):
            last = v.bn_aggr(mv[0:T, b, :], st[0:T, b, :])
        link(last)
        v.tensor_scalar(mv[0:T, :, 1], mv[0:T, :, 1], EPS, None, ALU.add).then_inc(stat_done, 1)
        v.wait_ge(rstd_done, 1)
        for b in range(B):
            last = v.tensor_scalar(xs[0:T, b, :], x1[0:T, b, :], mv[0:T, b, 0:1], rstd[0:T, b:b + 1],
                                   ALU.subtract, ALU.mult)
        last.then_inc(norm_done, 1)
        for n in range(2 * KB):
            k, h = n // 2, n % 2
            v.wait_ge(xh_done, n + 1)
            v.tensor_tensor(xlo[:, k, h * HALF:(h + 1) * HALF], xT[:, k, h * HALF:(h + 1) * HALF],
                            xhi[:, k, h * HALF:(h + 1) * HALF].bitcast(F32), ALU.subtract).then_inc(xl_done, 1)
        v.wait_ge(lg_rdy, 1)
        lp = acc[0:T, 2, 0:B * EX].rearrange("p (b e) -> p b e", e=EX)
        link(v.tensor_reduce(m1[0:T, :], lp, AX, ALU.max))
        v.tensor_tensor(lg[0:T, :, :], lp, m1[0:T, :].unsqueeze(2).to_broadcast([T, B, EX]),
                        ALU.subtract).then_inc(lg_cen, 1)
        v.wait_ge(ex_done, 1)
        link(v.tensor_reduce(m1[0:T, :], pr[0:T, :, :], AX, ALU.add))
        link(v.reciprocal(m1[0:T, :], m1[0:T, :]))
        link(v.tensor_tensor(pr[0:T, :, :], pr[0:T, :, :], m1[0:T, :].unsqueeze(2).to_broadcast([T, B, EX]),
                             ALU.mult))
        for b in range(B):
            last = v.max(top[0:T, b, :], pr[0:T, b, :])
        link(last)
        for b in range(B):
            last = v.max_index(idx[0:T, b, :], top[0:T, b, :], pr[0:T, b, :])
        link(last)
        link(v.tensor_copy(idf[0:T, :, :], idx[0:T, :, :]))
        link(v.tensor_tensor(m1[0:T, :], top[0:T, :, 0], top[0:T, :, 1], ALU.add))
        link(v.reciprocal(m1[0:T, :], m1[0:T, :]))
        link(v.tensor_scalar(m1[0:T, :], m1[0:T, :], gate[0:T, 1:2], None, ALU.mult))
        link(v.tensor_tensor(top[0:T, :, :], top[0:T, :, :], m1[0:T, :].unsqueeze(2).to_broadcast([T, B, EX]),
                             ALU.mult))
        v.wait_ge(iota_done, 1)
        io = iota[0:T, :].unsqueeze(1).to_broadcast([T, B, EX])
        for r, dst in ((0, coef), (1, sel)):
            link(v.tensor_tensor(dst[0:T, :, :], io, idf[0:T, :, r].unsqueeze(2).to_broadcast([T, B, EX]),
                                 ALU.is_equal))
            link(v.tensor_tensor(dst[0:T, :, :], dst[0:T, :, :],
                                 top[0:T, :, r].unsqueeze(2).to_broadcast([T, B, EX]), ALU.mult))
        link(v.tensor_tensor(coef[0:T, :, :], coef[0:T, :, :], sel[0:T, :, :], ALU.add))


def experts(nc, c, sb, ps, sem, Wg, Wu, Wd, x1, xhi, xlo, coef, out):
    raw = [sb(c, f"raw_{n}", [P, KB, FF]) for n in "gud"]
    hi = [sb(c, f"hi_{n}", [P, KB, FF], F32R) for n in "gud"]
    lo = [sb(c, f"lo_{n}", [P, KB, FF], F32R) for n in "gud"]
    sg = sb(c, "sg", [P, 2, HALF])
    hf = sb(c, "hf", [P, 2, HALF])
    hhi = sb(c, "hhi", [P, FB, NT], F32R)
    hlo = sb(c, "hlo", [P, FB, NT], F32R)
    ce = sb(c, "ce", [P, B])
    pg = ps(c, "pg", [P, 2, 512])
    pu = ps(c, "pu", [P, 2, 512])
    pd = ps(c, "pd", [P, 2, 512])

    w_load = [sem(c, f"load_{n}") for n in "gud"]
    h_done = [sem(c, f"hi_done_{n}") for n in "gud"]
    l_done = [sem(c, f"lo_done_{n}") for n in "gud"]
    gu_rdy = sem(c, "gu_rdy")
    sg_done = sem(c, "sg_done")
    hm_done = sem(c, "hm_done")
    hh_done = sem(c, "hh_done")
    hl_done = sem(c, "hl_done")
    dn_rdy = sem(c, "dn_rdy")
    ac_done = sem(c, "ac_done")
    ce_done = sem(c, "ce_done")
    stored = sem(c, "stored")
    block = c.enter_context(nc.Block())
    W = (Wg, Wu, Wd)

    @block.sync
    def _(sp):
        with sp.Fori(0, EX) as e:
            for n in range(3):
                sp.wait_ge(h_done[n], e + 1)
                sp.wait_ge(l_done[n], e + 1)
                sp.dma_start(raw[n][:, :, :], W[n][e].rearrange("(k p) f -> p k f", p=P)
                             ).then_inc(w_load[n], 16)
        for b in range(B):
            sp.wait_ge(ac_done, 8 * EX + b + 1)
            sp.dma_start(out[b], x1[0:T, b, :]).then_inc(stored, 16)
        sp.wait_ge(stored, 16 * B)

    @block.scalar
    def _(act):
        for n in range(3):
            act.sem_inc(h_done[n], 1)
        act.sem_inc(sg_done, 8)
        act.sem_inc(hh_done, 8)

        def split(e, n):
            act.wait_ge(w_load[n], 16 * (e + 1))
            if n < 2:
                act.wait_ge(gu_rdy, 8 * e + 8)
            else:
                act.wait_ge(dn_rdy, 8 * e + 8)
            act.activation(flat(hi[n][:, :, :]), flat(raw[n][:, :, :]), ACT.Copy).then_inc(h_done[n], 1)

        def silu(e, m):
            act.wait_ge(gu_rdy, 8 * (e + 1) + m + 1)
            act.wait_ge(hm_done, 8 * (e + 1) + m - 1)
            act.activation(sg[:, m % 2, :], pg[:, m % 2, 0:HALF], ACT.Silu).then_inc(sg_done, 1)

        def high(e, m):
            act.wait_ge(hm_done, 8 * (e + 1) + m + 1)
            act.wait_ge(dn_rdy, 8 * e + 8)
            act.activation(hhi[:, m % FB, m // FB * HALF:(m // FB + 1) * HALF], hf[:, m % 2, :],
                           ACT.Copy).then_inc(hh_done, 1)

        def expert(e, last=False):
            silu(e, 0)
            split(e, 2)
            for m in range(1, 8):
                high(e, m - 1)
                silu(e, m)
            high(e, 7)
            if not last:
                split(e + 1, 0)
                split(e + 1, 1)

        split(0, 0)
        split(0, 1)
        with act.Fori(0, EX - 1) as e:
            expert(e)
        expert(EX - 1, last=True)

    @block.tensor
    def _(pe):
        pe.sem_inc(gu_rdy, 8)
        pe.sem_inc(dn_rdy, 8)
        with pe.Fori(0, EX) as e:
            for m in range(8):
                f, h = m % FB, m // FB
                if m == 0:
                    for n in range(2):
                        pe.wait_ge(h_done[n], e + 2)
                        pe.wait_ge(l_done[n], e + 2)
                pe.wait_ge(hm_done, 8 * (e + 1) + m - 1)
                for n, bank in ((0, pg), (1, pu)):
                    for i in range(3 * KB):
                        k = i // 3
                        w, a = ((hi, xhi), (hi, xlo), (lo, xhi))[i % 3]
                        mm = pe.matmul(bank[:, m % 2, 0:HALF], w[n][:, k, f * P:(f + 1) * P],
                                       a[:, k, h * HALF:(h + 1) * HALF], start=(i == 0), stop=(i == 3 * KB - 1))
                mm.then_inc(gu_rdy, 1)
            pe.wait_ge(h_done[2], e + 2)
            pe.wait_ge(l_done[2], e + 2)
            for b in range(B):
                if b % 4 == 0:
                    pe.wait_ge(hl_done, 8 * (e + 1) + 4 + b)
                pe.wait_ge(ac_done, 8 * (e + 1) + b - 1)
                for i in range(3 * FB):
                    k = i // 3
                    a, w = ((hhi, hi), (hhi, lo), (hlo, hi))[i % 3]
                    mm = pe.matmul(pd[0:T, b % 2, :], a[:, k, b * T:(b + 1) * T], w[2][:, k, :],
                                   start=(i == 0), stop=(i == 3 * FB - 1))
                mm.then_inc(dn_rdy, 1)

    @block.vector
    def _(v):
        for n in range(3):
            v.sem_inc(l_done[n], 1)
        v.sem_inc(hm_done, 8)
        v.sem_inc(hl_done, 8)
        v.sem_inc(ac_done, 8)

        def split(e, n):
            v.wait_ge(h_done[n], e + 2)
            v.tensor_tensor(flat(lo[n][:, :, :]), flat(raw[n][:, :, :]), flat(hi[n][:, :, :]).bitcast(F32),
                            ALU.subtract).then_inc(l_done[n], 1)

        def product(e, m):
            v.wait_ge(sg_done, 8 * (e + 1) + m + 1)
            v.wait_ge(hh_done, 8 * (e + 1) + m - 1)
            v.tensor_tensor(hf[:, m % 2, :], sg[:, m % 2, :], pu[:, m % 2, 0:HALF], ALU.mult).then_inc(hm_done, 1)

        def low(e, m):
            v.wait_ge(hh_done, 8 * (e + 1) + m + 1)
            cols = slice(m // FB * HALF, (m // FB + 1) * HALF)
            v.tensor_tensor(hlo[:, m % FB, cols], hf[:, m % 2, :], hhi[:, m % FB, cols].bitcast(F32),
                            ALU.subtract).then_inc(hl_done, 1)

        def add(e, b):
            v.wait_ge(dn_rdy, 8 * (e + 1) + b + 1)
            if b == 0:
                v.wait_ge(ce_done, e + 1)
            v.scalar_tensor_tensor(out=x1[0:T, b, :], in0=pd[0:T, b % 2, :], scalar=ce[0:T, b:b + 1],
                                   in1=x1[0:T, b, :], op0=ALU.mult, op1=ALU.add).then_inc(ac_done, 1)

        def expert(e, last=False):
            v.wait_ge(ac_done, 8 * e + 8)
            v.tensor_copy(ce[0:T, :], coef[0:T, :, bass.ds(e, 1)].rearrange("p b e -> p (b e)")
                          ).then_inc(ce_done, 1)
            product(e, 0)
            split(e, 2)
            for m in range(1, 8):
                low(e, m - 1)
                product(e, m)
            low(e, 7)
            add(e, 0)
            add(e, 1)
            if not last:
                split(e + 1, 0)
            add(e, 2)
            add(e, 3)
            if not last:
                split(e + 1, 1)
            for b in range(4, B):
                add(e, b)

        split(0, 0)
        split(0, 1)
        with v.Fori(0, EX - 1) as e:
            expert(e)
        expert(EX - 1, last=True)


def kernel(**inputs):
    import numpy as np
    import concourse.bacc as bacc
    from concourse.bass_utils import run_bass_kernel_spmd

    a = {k: np.asarray(v) for k, v in inputs.items()}
    L = "L0_xattn_"

    def channels(v):
        return v.reshape(KB, P).T

    vecs = np.concatenate(
        [channels(a[L + n]) for n in ("ln_w", "ln_b", "q_in_scale", "qx_in_scale", "k_in_scale", "v_in_scale")]
        + [a[L + n].reshape(P, 1) for n in ("qln_w", "qln_b", "kln_w", "kln_b",
                                            "qxln_w", "qxln_b", "kxln_w", "kxln_b")], axis=1)
    scalars = np.array([a[L + n].reshape(()) for n in ("wq_scale", "wqx_scale", "wk_scale", "wv_scale",
                                                       "proj_in_scale", "proj_w_scale")]
                       + [a["g_xattn"].reshape(()), a["g_ffn"].reshape(())])
    kv = a[L + "w_kv_x"]
    parts = [(a[L + "wq"], 512), (a[L + "wqx"], 512), (a[L + "wk"], 256), (kv[:G * HD], 256),
             (kv[G * HD:], 256), (a[L + "wv"], 256)]
    w_in = np.concatenate([w.reshape(GP, n, KB, P).transpose(0, 3, 2, 1) for w, n in parts], axis=3)
    order = (1, 2, 0, 3)
    wproj = a[L + "wproj"].T.reshape(2, GP, 2, HPG, P, D).transpose(*order, 4, 5).reshape(GP, 8, P, D)
    smooth = a[L + "proj_smooth"].reshape(2, GP, 2, HPG, P).transpose(*order, 4).reshape(GP, 8, P)
    ctxT = a["ctx_2048"].reshape(B, NC, CT, KB, P).transpose(0, 1, 4, 3, 2)
    arrays = {
        "x": a["x"], "ctxT": ctxT, "vecs": vecs, "scalars": scalars,
        "smooth": smooth.transpose(2, 0, 1), "w_in": w_in, "wproj": wproj,
        "Wr": a["L0_ffn_Wr"], "Wg": a["L0_ffn_Wg"], "Wu": a["L0_ffn_Wu"], "Wd": a["L0_ffn_Wd"],
    }
    nc = bacc.Bacc("TRN2", target_bir_lowering=False, num_devices=1)
    feed, args = {}, []
    for name, v in arrays.items():
        v = np.ascontiguousarray(v)
        feed[f"in_{name}"] = v
        args.append(nc.dram_tensor(f"in_{name}", v.shape, mybir.dt.from_np(v.dtype), kind="ExternalInput").ap())
    o = nc.dram_tensor("out_0", (B, T, D), F32, kind="ExternalOutput").ap()
    transformer_block(nc, *args, o)
    r = run_bass_kernel_spmd(nc, [feed], core_ids=[0])
    return r.results[0]["out_0"]
```

```python
from contextlib import ExitStack

import concourse.bass as bass
from concourse import mybir

F32 = mybir.dt.float32
F32R = mybir.dt.float32r
BF16 = mybir.dt.bfloat16
U16 = mybir.dt.uint16
U32 = mybir.dt.uint32
ALU = mybir.AluOpType
ACT = mybir.ActivationFunctionType
AX = mybir.AxisListType.X

P = 128
B, T, D = 8, 112, 512
TC, NC = 375, 3
CT = TC // NC
KB = D // P
NH, G, HD = 16, 8, 128
HPG = NH // G
GP = 4
HP = NH // GP
NT = B * T
EX, FF = 8, 512
FB = FF // P
HALF = NT // 2
EPS = 1e-5
SCALE = float(HD) ** -0.5
FP8_MAX = 448.0

CQ, CQX, CK, CKX, CVX, CV = 0, 512, 1024, 1280, 1536, 1792
WC = 2048
LNC = 1536

V_LNW, V_LNB, V_SQ, V_SQX, V_SK, V_SV = 0, 4, 8, 12, 16, 20
V_QW, V_QB, V_KW, V_KB, V_QXW, V_QXB, V_KXW, V_KXB = range(24, 32)
NV = 32
S_WQ, S_WQX, S_WK, S_WV, S_PIN, S_PW, S_GX, S_GF = range(8)


def transformer_block(nc, x, ctxT, vecs, scalars, smooth, w_in, wproj, Wr, Wg, Wu, Wd, out):
    catd = nc.dram_tensor("cat_scratch", (GP * B, P, 8 * T), BF16)
    cat_w = catd.ap() if hasattr(catd, "ap") else catd
    with ExitStack() as top:
        def sb(ctx, name, shape, dt=F32):
            return ctx.enter_context(nc.sbuf_tensor(name, shape, dt))

        def ps(ctx, name, shape, dt=F32):
            return ctx.enter_context(nc.psum_tensor(name, shape, dt))

        def sem(ctx, name):
            return ctx.enter_context(nc.semaphore(name))

        vec = sb(top, "vec", [P, NV])
        scal = sb(top, "scal", [P, 8])
        gate = sb(top, "gate", [P, 2])
        proj_scale = sb(top, "proj_scale", [P, 1])
        ident = sb(top, "ident", [P, P])
        mhalf = sb(top, "mhalf", [P, 16])
        epst = sb(top, "epst", [P, 16])

        with ExitStack() as c:
            xq = sb(c, "xq", [P, 4, KB, NT], BF16)
            smi = sb(c, "smi", [P, GP, 8])
            wsc = sb(c, "wsc", [P, 4, KB])
            wmul = sb(c, "wmul", [P, KB, LNC // HD])
            with ExitStack() as c0:
                quantise_inputs(nc, c0, sb, ps, sem, x, vecs, scalars, smooth, vec, scal, gate,
                                proj_scale, ident, mhalf, epst, xq, smi, wsc, wmul)
            with ExitStack() as c1:
                attention(nc, c1, sb, ps, sem, ctxT, w_in, cat_w, vec, ident, mhalf, epst, xq, smi, wsc, wmul)
        with ExitStack() as c:
            x1 = sb(c, "x1", [P, B, D])
            xT = sb(c, "xT", [P, KB, NT])
            xhi = sb(c, "xhi", [P, KB, NT], F32R)
            xlo = sb(c, "xlo", [P, KB, NT], F32R)
            coef = sb(c, "coef", [P, B, EX])
            with ExitStack() as c2:
                projection(nc, c2, sb, ps, sem, x, wproj, cat_w, Wr, ident, mhalf, gate, proj_scale,
                           x1, xT, xhi, xlo, coef)
            with ExitStack() as c3:
                experts(nc, c3, sb, ps, sem, Wg, Wu, Wd, x1, xhi, xlo, coef, out)


def quantise_inputs(nc, c, sb, ps, sem, x, vecs, scalars, smooth, vec, scal, gate, proj_scale,
                    ident, mhalf, epst, xq, smi, wsc, wmul):
    xs = sb(c, "xs", [P, B, D])
    st = sb(c, "st", [P, B, 6])
    mv = sb(c, "mv", [P, B, 2])
    mv2 = sb(c, "mv2", [P, B, 2])
    rstd = sb(c, "rstd", [P, 2, B])
    hT = sb(c, "hT", [P, KB, NT])
    inv = sb(c, "inv", [P, 4, KB])
    smr = sb(c, "smr", [P, GP, 8])
    yq = sb(c, "yq", [P, 2, KB, NT], BF16)
    ye = sb(c, "ye", [P, KB, NT], BF16)
    ysum = sb(c, "ysum", [P, KB, NT])
    pt = ps(c, "pt", [P, 2, 512])

    vec_in = sem(c, "vec_in")
    x_in = [sem(c, f"x_in{b}") for b in range(B)]
    const_done = sem(c, "const_done")
    pool_self = sem(c, "pool_self")
    stat_done = sem(c, "stat_done")
    rstd_done = sem(c, "rstd_done")
    dve = sem(c, "dve_chain0")
    norm_done = sem(c, "norm_done")
    tr_done = sem(c, "tr_done")
    hT_done = sem(c, "hT_done")
    scal_done = sem(c, "scal_done")
    inv_done = sem(c, "inv_done")
    y_done = sem(c, "y_done")
    round_done = sem(c, "round_done")
    block = c.enter_context(nc.Block())

    @block.sync
    def _(sp):
        sp.dma_start(vec[:, :], vecs).then_inc(vec_in, 16)
        sp.dma_start(scal[:, :], scalars.partition_broadcast(P)).then_inc(vec_in, 16)
        sp.dma_start(smr[:, :, :], smooth).then_inc(vec_in, 16)
        for b in range(B):
            sp.dma_start(xs[0:T, b, :], x[b]).then_inc(x_in[b], 16)

    @block.gpsimd
    def _(pool):
        pool.memset(ident[:, :], 0.0).then_inc(pool_self, 1)
        pool.memset(mhalf[:, :], -0.5).then_inc(pool_self, 1)
        pool.memset(epst[:, :], EPS).then_inc(pool_self, 1)
        pool.wait_ge(pool_self, 3)
        pool.affine_select(out=ident[:, :], in_=ident[:, :], compare_op=ALU.not_equal, fill=1.0,
                           base=0, pattern=[[-1, P]], channel_multiplier=1).then_inc(const_done, 1)
        for n, m in enumerate((mv, mv2)):
            pool.wait_ge(stat_done, n + 1)
            pool.tensor_tensor(rstd[0:T, n, :], m[0:T, :, 1], mhalf[0:T, 0:B],
                               ALU.pow).then_inc(rstd_done, 1)

    @block.scalar
    def _(act):
        act.wait_ge(vec_in, 48)
        act.activation(gate[:, :], scal[:, S_GX:S_GF + 1], ACT.Tanh).then_inc(scal_done, 1)
        for n in range(2 * KB):
            k, h = n // 2, n % 2
            act.wait_ge(tr_done, n + 1)
            act.activation(hT[:, k, h * HALF:(h + 1) * HALF], pt[:, n % 2, 0:HALF], ACT.Identity,
                           bias=vec[:, V_LNB + k:V_LNB + k + 1],
                           scale=vec[:, V_LNW + k:V_LNW + k + 1]).then_inc(hT_done, 1)
        act.wait_ge(hT_done, 2 * KB)
        act.wait_ge(inv_done, 1)
        for n in range(4):
            if n >= 2:
                act.wait_ge(round_done, n - 1)
            for k in range(KB):
                last = act.activation(yq[:, n % 2, k, :], hT[:, k, :], ACT.Copy, scale=inv[:, n, k:k + 1])
            last.then_inc(y_done, 1)

    @block.tensor
    def _(pe):
        pe.wait_ge(const_done, 1)
        pe.wait_ge(norm_done, 1)
        for n in range(2 * KB):
            k, h = n // 2, n % 2
            if n >= 2:
                pe.wait_ge(hT_done, n - 1)
            for b in range(4):
                t = pe.transpose(pt[:, n % 2, b * T:(b + 1) * T], xs[0:T, 4 * h + b, k * P:(k + 1) * P],
                                 ident[0:T, 0:T])
            t.then_inc(tr_done, 1)

    @block.vector
    def _(v):
        count = [0]

        def link(ins):
            count[0] += 1
            ins.then_inc(dve, 1)
            v.wait_ge(dve, count[0])

        for b in range(B):
            v.wait_ge(x_in[b], 16)
            last = v.bn_stats(st[0:T, b, :], xs[0:T, b, :])
        link(last)
        for b in range(B):
            last = v.bn_aggr(mv[0:T, b, :], st[0:T, b, :])
        link(last)
        v.tensor_scalar(mv[0:T, :, 1], mv[0:T, :, 1], EPS, None, ALU.add).then_inc(stat_done, 1)
        v.wait_ge(vec_in, 48)
        v.reciprocal(inv[:, :, :].rearrange("p a b -> p (a b)"), vec[:, V_SQ:V_SV + KB]).then_inc(inv_done, 1)
        link(v.reciprocal(smi[:, :, :], smr[:, :, :]))
        for n in range(4):
            last = v.tensor_scalar(wsc[:, n, :], vec[:, V_SQ + 4 * n:V_SQ + 4 * n + 4],
                                   scal[:, S_WQ + n:S_WQ + n + 1], None, ALU.mult)
        link(last)
        for n, (lo, hi) in enumerate(((0, 4), (4, 8), (8, 10))):
            last = v.tensor_scalar(wmul[:, :, lo:hi], wsc[:, n, :].unsqueeze(2).to_broadcast([P, KB, hi - lo]),
                                   1.0 / HD, None, ALU.mult)
        v.memset(wmul[:, :, 10:12], 1.0 / HD)
        for col in (V_KW, V_KB, V_KXW, V_KXB):
            last = v.tensor_scalar(vec[:, col:col + 1], vec[:, col:col + 1], SCALE, None, ALU.mult)
        link(last)
        link(v.tensor_tensor(proj_scale[:, :], scal[:, S_PIN:S_PIN + 1], scal[:, S_PW:S_PW + 1], ALU.mult))
        v.wait_ge(scal_done, 1)
        link(v.tensor_tensor(proj_scale[:, :], proj_scale[:, :], gate[:, 0:1], ALU.mult))
        v.wait_ge(rstd_done, 1)
        for b in range(B):
            last = v.tensor_scalar(xs[0:T, b, :], xs[0:T, b, :], mv[0:T, b, 0:1], rstd[0:T, 0, b:b + 1],
                                   ALU.subtract, ALU.mult)
        link(last)
        for b in range(B):
            last = v.bn_stats(st[0:T, b, :], xs[0:T, b, :])
        link(last)
        for b in range(B):
            last = v.bn_aggr(mv2[0:T, b, :], st[0:T, b, :])
        link(last)
        v.tensor_scalar(mv2[0:T, :, 1], mv2[0:T, :, 1], EPS, None, ALU.add).then_inc(stat_done, 1)
        v.wait_ge(rstd_done, 2)
        for b in range(B):
            last = v.tensor_scalar(xs[0:T, b, :], xs[0:T, b, :], mv2[0:T, b, 0:1], rstd[0:T, 1, b:b + 1],
                                   ALU.subtract, ALU.mult)
        last.then_inc(norm_done, 1)
        for n in range(4):
            v.wait_ge(y_done, n + 1)
            round_fp8(v, link, flat(xq[:, n, :, :]), flat(yq[:, n % 2, :, :]), flat(ye[:, :, :]),
                      flat(ysum[:, :, :])).then_inc(round_done, 1)


def flat(ap):
    return ap.rearrange("p a b -> p (a b)")


def round_fp8(v, link, out, y, e, total):
    link(v.tensor_scalar(y, y, FP8_MAX, -FP8_MAX, ALU.min, ALU.max))
    link(v.tensor_scalar(e.bitcast(U16), y.bitcast(U16), 0x7F80, None, ALU.bitwise_and))
    link(v.tensor_scalar(e, e, 2.0 ** -6, 1.5 * 2.0 ** 20, ALU.max, ALU.mult))
    link(v.tensor_tensor(total, y, e, ALU.add))
    return v.tensor_tensor(out, total, e, ALU.subtract)


def attention(nc, c, sb, ps, sem, ctxT, w_in, catd, vec, ident, mhalf, epst, xq, smi, wsc, wmul):
    w_raw = sb(c, "w_raw", [P, KB, WC])
    w_hi = sb(c, "w_hi", [P, KB, WC], F32R)
    w_lo = sb(c, "w_lo", [P, KB, WC], F32R)
    w_mean = sb(c, "w_mean", [P, KB, LNC // HD])
    smg = sb(c, "smg", [P, 8])
    c_raw = sb(c, "c_raw", [P, NC, KB, CT])
    c_hi = sb(c, "c_hi", [P, NC, KB, CT], F32R)
    c_lo = sb(c, "c_lo", [P, NC, KB, CT], F32R)
    xqs = sb(c, "xqs", [P, 4, KB, T], F32R)
    nq = sb(c, "nq", [P, 512])
    nqx = sb(c, "nqx", [P, 512])
    nk = sb(c, "nk", [P, 256])
    nkx = sb(c, "nkx", [P, NC, 256])
    val = sb(c, "val", [P, 2, 256])
    valx = sb(c, "valx", [P, 2, NC, 256])
    sq = sb(c, "sq", [P, 2, 512])
    ss = sb(c, "ss", [P, 16])
    va = sb(c, "va", [P, 16])
    rs = sb(c, "rs", [P, 16])
    qT = sb(c, "qT", [P, HP * T])
    qxT = sb(c, "qxT", [P, HP * T])
    kT = sb(c, "kT", [P, 2 * T])
    kxT = sb(c, "kxT", [P, 2, TC])
    nmax = sb(c, "nmax", [P, 8])
    lsum = sb(c, "lsum", [P, 8])
    linv = sb(c, "linv", [P, 8])
    pself = sb(c, "pself", [P, HP, T])
    pcross = sb(c, "pcross", [P, HP, TC])
    pselfT = sb(c, "pselfT", [P, HP, T])
    pcrossT = sb(c, "pcrossT", [P, NC, HP, T])
    yb = sb(c, "yb", [P, 8 * T], BF16)
    ye = sb(c, "ye1", [P, 8 * T], BF16)
    ysum = sb(c, "ysum1", [P, 8 * T])
    cat = sb(c, "cat", [P, 8 * T], BF16)

    p_proj = ps(c, "p_proj", [P, 2, 512])
    p_tr = ps(c, "p_tr", [P, 2, 512])
    p_self = ps(c, "p_self", [P, 512])
    p_cross = ps(c, "p_cross", [P, 2, 512])
    p_out = ps(c, "p_out", [P, 512])

    w_in_done = sem(c, "w_in_done")
    w_seen = sem(c, "w_seen")
    c_in_done = [sem(c, f"c_in{k}") for k in range(NC)]
    w_cen = sem(c, "w_cen")
    wh_done = sem(c, "wh_done")
    wl_done = [sem(c, f"wl_done{k}") for k in range(KB)]
    ch_done = sem(c, "ch_done")
    cl_done = sem(c, "cl_done")
    xqs_done = sem(c, "xqs_done")
    pj_rdy = sem(c, "pj_rdy")
    pj_done = sem(c, "pj_done")
    rd_done = sem(c, "rd_done")
    va_done = sem(c, "va_done")
    rs_done = sem(c, "rs_done")
    ln_done = sem(c, "ln_done")
    tr_rdy = sem(c, "tr_rdy")
    t_done = sem(c, "t_done")
    pt_done = sem(c, "pt_done")
    ss_rdy = sem(c, "ss_rdy")
    ms_done = sem(c, "ms_done")
    es_done = sem(c, "es_done")
    ns_done = sem(c, "ns_done")
    sx_rdy = sem(c, "sx_rdy")
    mx_done = sem(c, "mx_done")
    ex_done = sem(c, "ex_done")
    nx_done = sem(c, "nx_done")
    ou_rdy = sem(c, "ou_rdy")
    ya_done = sem(c, "ya_done")
    ct_done = sem(c, "ct_done")
    cat_out = sem(c, "cat_out")
    dv = sem(c, "dve_chain1")
    chp = sem(c, "dve_chain_w")
    block = c.enter_context(nc.Block())

    def passes(eng, prepare, step):
        with eng.Fori(0, GP) as gp:
            prepare(gp)
            s0 = gp * B
            step(gp, s0, 0, None)
            with eng.Fori(0, 3) as i:
                s = s0 + 2 * i
                step(gp, s + 1, 1, s)
                step(gp, s + 2, 0, s + 1)
            step(gp, s0 + 7, 1, s0 + 6)
            step(gp, None, 0, s0 + 7)

    @block.sync
    def _(sp):
        def load_w(gp, first=False):
            for k in range(KB):
                if not first:
                    sp.wait_ge(wl_done[k], gp + 1)
                    sp.wait_ge(wh_done, 4 * gp + k + 1)
                sp.dma_start(w_raw[:, k, :], w_in[gp, :, k, :]).then_inc(w_in_done, 16)

        def load_c(s, b, k):
            sp.wait_ge(ch_done, 3 * s + k + 1)
            sp.wait_ge(cl_done, 3 * s + k + 1)
            sp.dma_start(c_raw[:, k, :, :], ctxT[b, k]).then_inc(c_in_done[k], 16)

        def store(st):
            sp.wait_ge(ct_done, st + 1)
            sp.dma_start(catd[st], cat[:, :]).then_inc(cat_out, 16)

        load_w(0, first=True)
        for gp in range(GP):
            s0 = gp * B
            for b in range(2):
                for k in range(NC):
                    load_c(s0 + b, b, k)
                if gp > 0:
                    store(s0 + b - 2)
            if gp + 1 < GP:
                load_w(gp + 1)
            else:
                sp.sem_inc(w_in_done, 16 * KB)
            with sp.Fori(2, B) as b:
                for k in range(NC):
                    load_c(s0 + b, b, k)
                store(s0 + b - 2)
        store(GP * B - 2)
        store(GP * B - 1)
        sp.wait_ge(cat_out, 16 * GP * B)

    @block.gpsimd
    def _(pool):
        pool.sem_inc(cl_done, 3)
        pool.sem_inc(wl_done[KB - 1], 1)
        pool.sem_inc(va_done, 6)
        pool.sem_inc(rs_done, 6)

        def rstd(s, j):
            rows, lo, hi = STAT[j]
            pool.wait_ge(rd_done, 6 * (s + 1) + j + 1)
            pool.tensor_tensor(va[0:rows, lo:hi], ss[0:rows, lo:hi], epst[0:rows, lo:hi],
                               ALU.add).then_inc(va_done, 1)
            pool.wait_ge(va_done, 6 * (s + 1) + j + 1)
            pool.wait_ge(ln_done, 6 * s + j + 1)
            pool.tensor_tensor(rs[0:rows, lo:hi], va[0:rows, lo:hi], mhalf[0:rows, lo:hi],
                               ALU.pow).then_inc(rs_done, 1)

        def c_low(s, k):
            pool.wait_ge(ch_done, 3 * (s + 1) + k + 1)
            pool.wait_ge(pj_rdy, 6 * s + 4 + k)
            pool.tensor_tensor(flat(c_lo[:, k, :, :]), flat(c_raw[:, k, :, :]),
                               flat(c_hi[:, k, :, :]).bitcast(F32), ALU.subtract).then_inc(cl_done, 1)

        def prepare(gp):
            k = KB - 1
            pool.wait_ge(wh_done, 4 * (gp + 1) + k + 1)
            pool.tensor_tensor(w_lo[:, k, :], w_raw[:, k, :], w_hi[:, k, :].bitcast(F32),
                               ALU.subtract).then_inc(wl_done[k], 1)

        def step(gp, s, par, t):
            if s is None:
                return
            for j in range(3):
                c_low(s, j)
                rstd(s, j)
            for j in range(3, 6):
                rstd(s, j)

        passes(pool, prepare, step)

    @block.scalar
    def _(act):
        act.sem_inc(ch_done, 3)
        act.sem_inc(pj_done, 6)
        act.sem_inc(t_done, 5)
        act.sem_inc(es_done, 1)
        act.sem_inc(ex_done, 4)
        act.sem_inc(wh_done, 4)

        def prepare(gp):
            act.wait_ge(pj_rdy, 6 * B * gp + 6)
            for k in range(KB):
                act.wait_ge(w_cen, 4 * gp + k + 1)
                act.activation(w_hi[:, k, :], w_raw[:, k, :], ACT.Copy).then_inc(wh_done, 1)

        def c_high(s, k):
            act.wait_ge(c_in_done[k], 16 * (s + 1))
            act.wait_ge(pj_rdy, 6 * s + 4 + k)
            act.activation(flat(c_hi[:, k, :, :]), flat(c_raw[:, k, :, :]), ACT.Copy).then_inc(ch_done, 1)

        def take(s, j, par):
            bank = p_proj[:, j % 2, :]
            act.wait_ge(pj_rdy, 6 * (s + 1) + j + 1)
            act.wait_ge(tr_rdy, 10 * s + (j + 1 if j < 3 else 5))
            if j < 2:
                act.activation((nq, nqx)[j][0:T, :], bank[0:T, :], ACT.Copy)
                n, rows = 512, T
            elif j == 2:
                act.wait_ge(ou_rdy, 2 * s)
                act.activation(nk[0:T, :], bank[0:T, 0:256], ACT.Copy)
                act.activation(val[0:T, par, :], bank[0:T, 256:512], ACT.Copy)
                n, rows = 256, T
            else:
                act.activation(nkx[0:CT, j - 3, :], bank[0:CT, 0:256], ACT.Copy)
                act.activation(valx[0:CT, par, j - 3, :], bank[0:CT, 256:512], ACT.Copy)
                n, rows = 256, CT
            act.wait_ge(rd_done, 6 * (s + 1) + j - 1)
            act.activation(sq[0:rows, j % 2, 0:n], bank[0:rows, 0:n], ACT.Square,
                           scale=float(HD) ** -0.5).then_inc(pj_done, 1)

        def turned(t, n):
            act.wait_ge(tr_rdy, 10 * (t + 1) + n + 1)
            if n in (0, 2):
                act.wait_ge(ss_rdy, t + 1)
            else:
                act.wait_ge(sx_rdy, 4 * t + 4)
            dst = (qT[:, :], qxT[:, :], kT[:, :], kxT[:, 0, :], kxT[:, 1, :])[n]
            w, b = ((V_QW, V_QB), (V_QXW, V_QXB), (V_KW, V_KB), (V_KXW, V_KXB), (V_KXW, V_KXB))[n]
            act.activation(dst, p_tr[:, n % 2, 0:TURNED[n]], ACT.Identity, bias=vec[:, b:b + 1],
                           scale=vec[:, w:w + 1]).then_inc(t_done, 1)

        def exp_self(t):
            act.wait_ge(ms_done, t + 2)
            act.wait_ge(tr_rdy, 10 * t + 6)
            act.wait_ge(ns_done, t + 1)
            for h in range(HP):
                last = act.activation(pself[0:T, h, :], p_self[0:T, h * T:(h + 1) * T], ACT.Exp,
                                      bias=nmax[0:T, h:h + 1], accum_out=lsum[0:T, h:h + 1])
            last.then_inc(es_done, 1)

        def exp_cross(t, h):
            act.wait_ge(mx_done, 4 * (t + 1) + h + 1)
            act.wait_ge(tr_rdy, 10 * t + 7 + h)
            act.wait_ge(nx_done, 4 * t + h + 1)
            act.activation(pcross[0:T, h, :], p_cross[0:T, h % 2, 0:TC], ACT.Exp,
                           bias=nmax[0:T, 4 + h:5 + h], accum_out=lsum[0:T, 4 + h:5 + h]).then_inc(ex_done, 1)

        def step(gp, s, par, t):
            A, Q = s is not None, t is not None
            if Q: turned(t, 0)
            if Q: turned(t, 1)
            if A: take(s, 0, par)
            if A: c_high(s, 0)
            if Q: turned(t, 2)
            if Q: turned(t, 3)
            if A: take(s, 1, par)
            if Q: exp_self(t)
            if Q: turned(t, 4)
            if A: c_high(s, 1)
            if Q: exp_cross(t, 0)
            if Q: exp_cross(t, 1)
            if A: take(s, 2, par)
            if A: c_high(s, 2)
            if Q: exp_cross(t, 2)
            if Q: exp_cross(t, 3)
            if A: take(s, 3, par)
            if A: take(s, 4, par)
            if A: take(s, 5, par)

        passes(act, prepare, step)

    @block.tensor
    def _(pe):
        pe.sem_inc(pj_rdy, 6)
        pe.sem_inc(tr_rdy, 10)
        pe.sem_inc(ss_rdy, 1)
        pe.sem_inc(sx_rdy, 4)
        pe.sem_inc(ou_rdy, 2)

        def project(s, j, gp=None):
            pe.wait_ge(pj_done, 6 * (s + 1) + j - 1)
            bank = p_proj[:, j % 2, :]
            if j == 0:
                pe.wait_ge(xqs_done, s + 1)
            if j < 3:
                for n, o, lo, w in (((0, 0, CQ, 512),), ((1, 0, CQX, 512),),
                                    ((2, 0, CK, 256), (3, 256, CV, 256)))[j]:
                    for i in range(2 * KB):
                        k = i // 2
                        if gp is not None and i % 2 == 0:
                            pe.wait_ge(wh_done, 4 * (gp + 1) + k + 1)
                            pe.wait_ge(wl_done[k], gp + 2)
                        m = pe.matmul(bank[0:T, o:o + w], xqs[:, n, k, :], (w_hi, w_lo)[i % 2][:, k, lo:lo + w],
                                      start=(i == 0), stop=(i == 2 * KB - 1))
            else:
                ch = j - 3
                pe.wait_ge(ch_done, 3 * (s + 1) + ch + 1)
                pe.wait_ge(cl_done, 3 * (s + 1) + ch + 1)
                for i in range(3 * KB):
                    k = i // 3
                    a, w = ((c_hi, w_hi), (c_hi, w_lo), (c_lo, w_hi))[i % 3]
                    m = pe.matmul(bank[0:CT, :], a[:, ch, k, :], w[:, k, CKX:CV],
                                  start=(i == 0), stop=(i == 3 * KB - 1))
            m.then_inc(pj_rdy, 1)

        def bank_free(t, n):
            if n < 2:
                pe.wait_ge(pt_done, 5 * t + 4 + n)
            elif n < 7:
                pe.wait_ge(t_done, 5 * (t + 1) + n - 1)
            else:
                pe.wait_ge(pt_done, 5 * (t + 1) + n - 6)

        def turn(t, n):
            pe.wait_ge(ln_done, 6 * (t + 1) + (1, 2, 3, 6, 6)[n])
            bank_free(t, n)
            if n < 3:
                src = (nq, nqx, nk)[n]
                for h in range((4, 4, 2)[n]):
                    m = pe.transpose(p_tr[:, n % 2, h * T:(h + 1) * T], src[0:T, h * P:(h + 1) * P],
                                     ident[0:T, 0:T])
            else:
                for k in range(NC):
                    m = pe.transpose(p_tr[:, n % 2, k * CT:(k + 1) * CT],
                                     nkx[0:CT, k, (n - 3) * P:(n - 2) * P], ident[0:CT, 0:CT])
            m.then_inc(tr_rdy, 1)

        def score_self(t):
            pe.wait_ge(t_done, 5 * (t + 1) + 3)
            pe.wait_ge(es_done, t + 1)
            for h in range(HP):
                m = pe.matmul(p_self[0:T, h * T:(h + 1) * T], qT[:, h * T:(h + 1) * T],
                              kT[:, h // HPG * T:(h // HPG + 1) * T], start=True, stop=True)
            m.then_inc(ss_rdy, 1)

        def score_cross(t, h):
            pe.wait_ge(t_done, 5 * (t + 1) + 4 + h // HPG)
            pe.wait_ge(ex_done, 4 * (t + 1) + h - 1)
            pe.matmul(p_cross[0:T, h % 2, 0:TC], qxT[:, h * T:(h + 1) * T], kxT[:, h // HPG, :],
                      start=True, stop=True).then_inc(sx_rdy, 1)

        def turn_self(t):
            pe.wait_ge(ns_done, t + 2)
            bank_free(t, 5)
            for h in range(HP):
                m = pe.transpose(p_tr[0:T, 1, h * T:(h + 1) * T], pself[0:T, h, :], ident[0:T, 0:T])
            m.then_inc(tr_rdy, 1)

        def turn_cross(t, h):
            pe.wait_ge(nx_done, 4 * (t + 1) + h + 1)
            bank_free(t, 6 + h)
            for k in range(NC):
                m = pe.transpose(p_tr[0:CT, h % 2, k * T:(k + 1) * T], pcross[0:T, h, k * CT:(k + 1) * CT],
                                 ident[0:T, 0:T])
            m.then_inc(tr_rdy, 1)

        def outputs(t, g, par):
            pe.wait_ge(pt_done, 5 * (t + 1) + (3, 5)[g])
            pe.wait_ge(pj_done, 6 * (t + 1) + 6)
            pe.wait_ge(ya_done, 2 * (t + 1) + g)
            pe.matmul(p_out[:, 0:HPG * T], val[0:T, par, g * P:(g + 1) * P],
                      flat(pselfT[0:T, HPG * g:HPG * (g + 1), :]), start=True, stop=True)
            for k in range(NC):
                m = pe.matmul(p_out[:, HPG * T:2 * HPG * T], valx[0:CT, par, k, g * P:(g + 1) * P],
                              flat(pcrossT[0:CT, k, HPG * g:HPG * (g + 1), :]),
                              start=(k == 0), stop=(k == NC - 1))
            m.then_inc(ou_rdy, 1)

        def step(gp, s, par, t):
            A, Q = s is not None, t is not None
            if A: project(s, 0, None if Q else gp)
            if Q: turn(t, 0)
            if Q: turn(t, 1)
            if A: project(s, 1)
            if Q: turn(t, 2)
            if Q: turn(t, 3)
            if A: project(s, 2)
            if Q: score_self(t)
            if Q: score_cross(t, 0)
            if Q: score_cross(t, 1)
            if Q: turn(t, 4)
            if A: project(s, 3)
            if Q: turn_self(t)
            if Q: turn_cross(t, 0)
            if Q: score_cross(t, 2)
            if Q: turn_cross(t, 1)
            if Q: score_cross(t, 3)
            if A: project(s, 4)
            if Q: outputs(t, 0, 1 - par)
            if Q: turn_cross(t, 2)
            if Q: turn_cross(t, 3)
            if A: project(s, 5)
            if Q: outputs(t, 1, 1 - par)

        passes(pe, lambda gp: None, step)

    @block.vector
    def _(v):
        v.sem_inc(rd_done, 6)
        v.sem_inc(ln_done, 6)
        v.sem_inc(pt_done, 5)
        v.sem_inc(ms_done, 1)
        v.sem_inc(ns_done, 1)
        v.sem_inc(mx_done, 4)
        v.sem_inc(nx_done, 4)
        v.sem_inc(ya_done, 2)
        for k in range(KB - 1):
            v.sem_inc(wl_done[k], 1)
        CH, CHP = 9, 8
        SEG = ((CQ, CQX, 0, 4), (CQX, CK, 4, 8), (CK, CKX, 8, 10))

        def centre(g, k):
            raw = w_raw[:, k, :]
            heads = raw[:, 0:LNC].rearrange("p (h d) -> p h d", d=HD)
            v.tensor_reduce(w_mean[:, k, :], heads, AX, ALU.add).then_inc(chp, 1)
            v.wait_ge(chp, CHP * g + 2 * k + 1)
            v.tensor_tensor(w_mean[:, k, :], w_mean[:, k, :], wmul[:, k, :], ALU.mult).then_inc(chp, 1)
            v.wait_ge(chp, CHP * g + 2 * k + 2)
            for n, (lo, hi, h0, h1) in enumerate(SEG):
                mean = w_mean[:, k, h0:h1].unsqueeze(2).to_broadcast([P, h1 - h0, HD])
                v.scalar_tensor_tensor(out=heads[:, h0:h1, :], in0=heads[:, h0:h1, :],
                                       scalar=wsc[:, n, k:k + 1], in1=mean, op0=ALU.mult, op1=ALU.subtract)
            v.tensor_tensor(heads[:, 10:12, :], heads[:, 10:12, :],
                            w_mean[:, k, 10:12].unsqueeze(2).to_broadcast([P, 2, HD]), ALU.subtract)
            v.tensor_scalar(raw[:, CV:WC], raw[:, CV:WC], wsc[:, 3, k:k + 1], None,
                            ALU.mult).then_inc(w_cen, 1)

        def loaded(g):
            v.wait_ge(w_in_done, 16 * KB * (g + 1))
            v.sem_inc(w_seen, 1)

        def prepare(gp):
            v.wait_ge(ya_done, 2 * B * gp + 2)
            v.tensor_copy(smg[:, :], smi[:, gp, :])
            for k in range(KB - 1):
                v.wait_ge(wh_done, 4 * (gp + 1) + k + 1)
                v.wait_ge(pj_rdy, 6 * B * gp + 6)
                v.tensor_tensor(w_lo[:, k, :], w_raw[:, k, :], w_hi[:, k, :].bitcast(F32),
                                ALU.subtract).then_inc(wl_done[k], 1)

        def inputs(s, b):
            v.wait_ge(pj_rdy, 6 * s + 3)
            for n in range(4):
                last = v.tensor_copy(xqs[:, n, :, :], xq[:, n, :, bass.ds(b * T, T)])
            last.then_inc(xqs_done, 1)

        def sums(s, j):
            rows, lo, hi = STAT[j]
            v.wait_ge(pj_done, 6 * (s + 1) + j + 1)
            v.wait_ge(va_done, 6 * s + j + 1)
            v.tensor_reduce(ss[0:rows, lo:hi],
                            sq[0:rows, j % 2, 0:(hi - lo) * HD].rearrange("p (h d) -> p h d", d=HD),
                            AX, ALU.add).then_inc(rd_done, 1)

        def scale(s, j):
            rows, lo, hi = STAT[j]
            v.wait_ge(rs_done, 6 * (s + 1) + j + 1)
            buf = (nq[0:T, :], nqx[0:T, :], nk[0:T, :], nkx[0:CT, 0, :], nkx[0:CT, 1, :], nkx[0:CT, 2, :])[j]
            buf = buf.rearrange("p (h d) -> p h d", d=HD)
            v.tensor_tensor(buf, buf, rs[0:rows, lo:hi].unsqueeze(2).to_broadcast([rows, hi - lo, HD]),
                            ALU.mult).then_inc(ln_done, 1)

        def max_self(t):
            v.wait_ge(ss_rdy, t + 2)
            v.wait_ge(es_done, t + 1)
            v.tensor_reduce(nmax[0:T, 0:HP], p_self[0:T, 0:HP * T].rearrange("p (h d) -> p h d", d=T),
                            AX, ALU.max, negate=True).then_inc(ms_done, 1)

        def norm_self(t):
            v.wait_ge(es_done, t + 2)
            v.wait_ge(tr_rdy, 10 * t + 6)
            v.reciprocal(linv[0:T, 0:HP], lsum[0:T, 0:HP]).then_inc(dv, 1)
            v.wait_ge(dv, CH * t + 1)
            v.tensor_tensor(pself[0:T, :, :], pself[0:T, :, :],
                            linv[0:T, 0:HP].unsqueeze(2).to_broadcast([T, HP, T]), ALU.mult).then_inc(ns_done, 1)

        def max_cross(t, h):
            v.wait_ge(sx_rdy, 4 * (t + 1) + h + 1)
            v.wait_ge(ex_done, 4 * t + h + 1)
            v.tensor_reduce(nmax[0:T, 4 + h:5 + h], p_cross[0:T, h % 2, 0:TC], AX, ALU.max,
                            negate=True).then_inc(mx_done, 1)

        def norm_cross(t, h):
            v.wait_ge(ex_done, 4 * (t + 1) + h + 1)
            v.reciprocal(linv[0:T, 4 + h:5 + h], lsum[0:T, 4 + h:5 + h]).then_inc(dv, 1)
            v.wait_ge(dv, CH * t + 2 + h)
            v.tensor_scalar(pcross[0:T, h, :], pcross[0:T, h, :], linv[0:T, 4 + h:5 + h], None,
                            ALU.mult).then_inc(nx_done, 1)

        def take_self(t):
            v.wait_ge(tr_rdy, 10 * (t + 1) + 6)
            v.wait_ge(ou_rdy, 2 * t + 2)
            v.tensor_copy(flat(pselfT[0:T, :, :]), p_tr[0:T, 1, 0:HP * T]).then_inc(pt_done, 1)

        def take_cross(t, h):
            v.wait_ge(tr_rdy, 10 * (t + 1) + 7 + h)
            v.wait_ge(ou_rdy, 2 * t + 2)
            v.tensor_copy(pcrossT[0:CT, :, h, :],
                          p_tr[0:CT, h % 2, 0:NC * T].rearrange("p (k t) -> p k t", k=NC)).then_inc(pt_done, 1)

        def smoothed(t, g):
            v.wait_ge(ou_rdy, 2 * (t + 1) + g + 1)
            v.tensor_tensor(yb[:, g * 4 * T:(g + 1) * 4 * T].rearrange("p (a t) -> p a t", t=T),
                            p_out[:, 0:4 * T].rearrange("p (a t) -> p a t", t=T),
                            smg[:, 4 * g:4 * g + 4].unsqueeze(2).to_broadcast([P, 4, T]),
                            ALU.mult).then_inc(ya_done, 1)

        def rounded(t):
            v.wait_ge(ya_done, 2 * (t + 1) + 2)
            v.tensor_scalar(yb[:, :], yb[:, :], FP8_MAX, -FP8_MAX, ALU.min, ALU.max).then_inc(dv, 1)
            v.wait_ge(dv, CH * t + 6)
            v.tensor_scalar(ye[:, :].bitcast(U16), yb[:, :].bitcast(U16), 0x7F80, None,
                            ALU.bitwise_and).then_inc(dv, 1)
            v.wait_ge(dv, CH * t + 7)
            v.tensor_scalar(ye[:, :], ye[:, :], 2.0 ** -6, 1.5 * 2.0 ** 20, ALU.max, ALU.mult).then_inc(dv, 1)
            v.wait_ge(dv, CH * t + 8)
            v.tensor_tensor(ysum[:, :], yb[:, :], ye[:, :], ALU.add).then_inc(dv, 1)
            v.wait_ge(dv, CH * t + 9)
            v.wait_ge(cat_out, 16 * t)
            v.tensor_tensor(cat[:, :], ysum[:, :], ye[:, :], ALU.subtract).then_inc(ct_done, 1)

        def step(s, t, b_next, g=None, blocks=()):
            A, Q = s is not None, t is not None
            if A: sums(s, 0)
            if A: sums(s, 1)
            if Q: max_self(t)
            if A: scale(s, 0)
            if Q: norm_self(t)
            if Q: max_cross(t, 0)
            if Q: max_cross(t, 1)
            if Q: norm_cross(t, 0)
            if Q: norm_cross(t, 1)
            if Q: take_self(t)
            if A: sums(s, 2)
            if Q: take_cross(t, 0)
            if Q: max_cross(t, 2)
            if A: scale(s, 1)
            if Q: take_cross(t, 1)
            if Q: max_cross(t, 3)
            if A: scale(s, 2)
            if A and b_next is not None: inputs(s + 1, b_next)
            if Q: norm_cross(t, 2)
            if Q: norm_cross(t, 3)
            if A: sums(s, 3)
            if Q: smoothed(t, 0)
            if Q: take_cross(t, 2)
            if Q: take_cross(t, 3)
            if A: scale(s, 3)
            if A: sums(s, 4)
            if Q: smoothed(t, 1)
            if A: scale(s, 4)
            for k in blocks:
                centre(g, k)
            if A: sums(s, 5)
            if A: scale(s, 5)
            if Q: rounded(t)

        loaded(0)
        for k in range(KB):
            centre(0, k)
        with v.Fori(0, GP) as gp:
            prepare(gp)
            s0 = gp * B
            inputs(s0, 0)
            step(s0, None, 1)
            with v.Fori(0, 3) as i:
                s = s0 + 2 * i
                step(s + 1, s, 2 * i + 2)
                step(s + 2, s + 1, 2 * i + 3)
            loaded(gp + 1)
            step(s0 + 7, s0 + 6, None, gp + 1, (0, 1))
            step(None, s0 + 7, None, gp + 1, (2, 3))


STAT = ((T, 0, 4), (T, 4, 8), (T, 8, 10), (CT, 10, 12), (CT, 12, 14), (CT, 14, 16))
TURNED = (HP * T, HP * T, 2 * T, TC, TC)


def projection(nc, c, sb, ps, sem, x, wproj, catd, Wr, ident, mhalf, gate, proj_scale,
               x1, xT, xhi, xlo, coef):
    NB = 8
    w_raw = sb(c, "p_raw", [P, 4, D])
    w_hi = sb(c, "p_hi", [P, 2, D], F32R)
    w_lo = sb(c, "p_lo", [P, 2, D], F32R)
    cat = sb(c, "p_cat", [P, 2, B, NB * T], BF16)
    catr = sb(c, "p_catr", [P, 2, B, T], F32R)
    xs = sb(c, "xs1", [P, B, D])
    st = sb(c, "st1", [P, B, 6])
    mv = sb(c, "mv1", [P, B, 2])
    rstd = sb(c, "rstd1", [P, B])
    wr = sb(c, "wr", [P, KB, EX])
    lg = sb(c, "lg", [P, B, EX])
    pr = sb(c, "pr", [P, B, EX])
    m1 = sb(c, "m1", [P, B])
    top = sb(c, "top", [P, B, EX])
    idx = sb(c, "idx", [P, B, EX], U32)
    idf = sb(c, "idf", [P, B, EX])
    iota = sb(c, "iota", [P, EX])
    sel = sb(c, "sel", [P, B, EX])
    acc = ps(c, "p_acc", [P, B, D])

    x_in = sem(c, "x_in_p")
    wr_in = sem(c, "wr_in")
    w_load = [sem(c, f"pw_load{r}") for r in range(4)]
    cat_load = [sem(c, f"cat_load{r}") for r in range(2)]
    hi_done = sem(c, "ph_done")
    lo_done = sem(c, "pl_done")
    cr_done = sem(c, "cr_done")
    mm_done = sem(c, "pm_done")
    dve = sem(c, "dve_chain2")
    stat_done = sem(c, "stat_done1")
    rstd_done = sem(c, "rstd_done1")
    iota_done = sem(c, "iota_done")
    norm_done = sem(c, "norm_done1")
    tr_done = sem(c, "tr_done1")
    xT_done = sem(c, "xT_done")
    xh_done = sem(c, "xh_done")
    xl_done = sem(c, "xl_done")
    lg_rdy = sem(c, "lg_rdy")
    lg_cen = sem(c, "lg_cen")
    ex_done = sem(c, "lg_exp")
    block = c.enter_context(nc.Block())
    N = 2 * NB

    @block.sync
    def _(sp):
        sp.dma_start(xs[0:T, :, :], x.rearrange("b t d -> t b d")).then_inc(x_in, 16)
        sp.dma_start(wr[:, :, :], Wr.rearrange("(k p) e -> p k e", p=P)).then_inc(wr_in, 16)
        with sp.Fori(0, GP // 2) as i:
            for n in range(N):
                if n % NB == 0:
                    r = n // NB
                    sp.wait_ge(cr_done, N * i + NB * (r + 1))
                    sp.dma_start(cat[:, r, :, :], catd[bass.ds((2 * i + r) * B, B)].rearrange("b p n -> p b n")
                                 ).then_inc(cat_load[r], 16)
                sp.wait_ge(hi_done, N * (i + 1) + n - 3)
                sp.wait_ge(lo_done, N * (i + 1) + n - 3)
                sp.dma_start(w_raw[:, n % 4, :], wproj[2 * i + n // NB, n % NB]).then_inc(w_load[n % 4], 16)

    @block.gpsimd
    def _(pool):
        pool.iota(iota[:, :], pattern=[[1, EX]], base=0, channel_multiplier=0,
                  allow_small_or_imprecise_dtypes=True).then_inc(iota_done, 1)
        pool.wait_ge(stat_done, 1)
        pool.tensor_tensor(rstd[0:T, :], mv[0:T, :, 1], mhalf[0:T, 0:B], ALU.pow).then_inc(rstd_done, 1)

    @block.scalar
    def _(act):
        act.sem_inc(hi_done, N)
        with act.Fori(0, GP // 2) as i:
            for n in range(N):
                act.wait_ge(w_load[n % 4], 64 * i + 16 * (n // 4 + 1))
                act.wait_ge(mm_done, N * (i + 1) + n - 1)
                act.activation(w_hi[:, n % 2, :], w_raw[:, n % 4, :], ACT.Copy).then_inc(hi_done, 1)
        for n in range(2 * KB):
            k, h = n // 2, n % 2
            act.wait_ge(tr_done, n + 1)
            act.activation(xT[:, k, h * HALF:(h + 1) * HALF], acc[:, n % 2, 0:HALF], ACT.Copy).then_inc(xT_done, 1)
            act.activation(xhi[:, k, h * HALF:(h + 1) * HALF], acc[:, n % 2, 0:HALF], ACT.Copy).then_inc(xh_done, 1)
        act.wait_ge(lg_cen, 1)
        act.activation(pr[0:T, :, :], lg[0:T, :, :], ACT.Exp).then_inc(ex_done, 1)

    @block.tensor
    def _(pe):
        pe.sem_inc(mm_done, N)

        def block_of(i, n, first=False, last=False):
            pe.wait_ge(hi_done, N * (i + 1) + n + 1)
            pe.wait_ge(lo_done, N * (i + 1) + n + 1)
            pe.wait_ge(cr_done, N * (i + 1) + n + 1)
            for b in range(B):
                for part, w in enumerate((w_hi, w_lo)):
                    m = pe.matmul(acc[0:T, b, :], catr[:, n % 2, b, :], w[:, n % 2, :],
                                  start=(first and part == 0), stop=(last and part == 1),
                                  skip_group_check=True)
            m.then_inc(mm_done, 1)

        for n in range(N):
            block_of(0, n, first=(n == 0))
        for n in range(N):
            block_of(1, n, last=(n == N - 1))
        pe.wait_ge(norm_done, 1)
        for n in range(2 * KB):
            k, h = n // 2, n % 2
            if n >= 2:
                pe.wait_ge(xh_done, n - 1)
                pe.wait_ge(xl_done, n - 1)
            for b in range(4):
                t = pe.transpose(acc[:, n % 2, b * T:(b + 1) * T], xs[0:T, 4 * h + b, k * P:(k + 1) * P],
                                 ident[0:T, 0:T])
            t.then_inc(tr_done, 1)
        pe.wait_ge(xT_done, 2 * KB)
        pe.wait_ge(wr_in, 16)
        for b in range(B):
            for k in range(KB):
                m = pe.matmul(acc[0:T, 2, b * EX:(b + 1) * EX], xT[:, k, b * T:(b + 1) * T], wr[:, k, :],
                              start=(k == 0), stop=(k == KB - 1))
        m.then_inc(lg_rdy, 1)

    @block.vector
    def _(v):
        v.sem_inc(lo_done, N)
        v.sem_inc(cr_done, N)
        with v.Fori(0, GP // 2) as i:
            for n in range(N):
                r, j = n // NB, n % NB
                v.wait_ge(cat_load[r], 16 * (i + 1))
                v.wait_ge(mm_done, N * (i + 1) + n - 1)
                v.tensor_copy(catr[:, n % 2, :, :], cat[:, r, :, j * T:(j + 1) * T]).then_inc(cr_done, 1)
                v.wait_ge(hi_done, N * (i + 1) + n + 1)
                v.tensor_tensor(w_lo[:, n % 2, :], w_raw[:, n % 4, :], w_hi[:, n % 2, :].bitcast(F32),
                                ALU.subtract).then_inc(lo_done, 1)
        count = [0]

        def link(ins):
            count[0] += 1
            ins.then_inc(dve, 1)
            v.wait_ge(dve, count[0])

        v.wait_ge(mm_done, N * (GP // 2 + 1))
        v.wait_ge(x_in, 16)
        for b in range(B):
            last = v.scalar_tensor_tensor(out=x1[0:T, b, :], in0=acc[0:T, b, :], scalar=proj_scale[0:T, 0:1],
                                          in1=xs[0:T, b, :], op0=ALU.mult, op1=ALU.add)
        link(last)
        for b in range(B):
            last = v.bn_stats(st[0:T, b, :], x1[0:T, b, :])
        link(last)
        for b in range(B):
            last = v.bn_aggr(mv[0:T, b, :], st[0:T, b, :])
        link(last)
        v.tensor_scalar(mv[0:T, :, 1], mv[0:T, :, 1], EPS, None, ALU.add).then_inc(stat_done, 1)
        v.wait_ge(rstd_done, 1)
        for b in range(B):
            last = v.tensor_scalar(xs[0:T, b, :], x1[0:T, b, :], mv[0:T, b, 0:1], rstd[0:T, b:b + 1],
                                   ALU.subtract, ALU.mult)
        last.then_inc(norm_done, 1)
        for n in range(2 * KB):
            k, h = n // 2, n % 2
            v.wait_ge(xh_done, n + 1)
            v.tensor_tensor(xlo[:, k, h * HALF:(h + 1) * HALF], xT[:, k, h * HALF:(h + 1) * HALF],
                            xhi[:, k, h * HALF:(h + 1) * HALF].bitcast(F32), ALU.subtract).then_inc(xl_done, 1)
        v.wait_ge(lg_rdy, 1)
        lp = acc[0:T, 2, 0:B * EX].rearrange("p (b e) -> p b e", e=EX)
        link(v.tensor_reduce(m1[0:T, :], lp, AX, ALU.max))
        v.tensor_tensor(lg[0:T, :, :], lp, m1[0:T, :].unsqueeze(2).to_broadcast([T, B, EX]),
                        ALU.subtract).then_inc(lg_cen, 1)
        v.wait_ge(ex_done, 1)
        link(v.tensor_reduce(m1[0:T, :], pr[0:T, :, :], AX, ALU.add))
        link(v.reciprocal(m1[0:T, :], m1[0:T, :]))
        link(v.tensor_tensor(pr[0:T, :, :], pr[0:T, :, :], m1[0:T, :].unsqueeze(2).to_broadcast([T, B, EX]),
                             ALU.mult))
        for b in range(B):
            last = v.max(top[0:T, b, :], pr[0:T, b, :])
        link(last)
        for b in range(B):
            last = v.max_index(idx[0:T, b, :], top[0:T, b, :], pr[0:T, b, :])
        link(last)
        link(v.tensor_copy(idf[0:T, :, :], idx[0:T, :, :]))
        link(v.tensor_tensor(m1[0:T, :], top[0:T, :, 0], top[0:T, :, 1], ALU.add))
        link(v.reciprocal(m1[0:T, :], m1[0:T, :]))
        link(v.tensor_scalar(m1[0:T, :], m1[0:T, :], gate[0:T, 1:2], None, ALU.mult))
        link(v.tensor_tensor(top[0:T, :, :], top[0:T, :, :], m1[0:T, :].unsqueeze(2).to_broadcast([T, B, EX]),
                             ALU.mult))
        v.wait_ge(iota_done, 1)
        io = iota[0:T, :].unsqueeze(1).to_broadcast([T, B, EX])
        for r, dst in ((0, coef), (1, sel)):
            link(v.tensor_tensor(dst[0:T, :, :], io, idf[0:T, :, r].unsqueeze(2).to_broadcast([T, B, EX]),
                                 ALU.is_equal))
            link(v.tensor_tensor(dst[0:T, :, :], dst[0:T, :, :],
                                 top[0:T, :, r].unsqueeze(2).to_broadcast([T, B, EX]), ALU.mult))
        link(v.tensor_tensor(coef[0:T, :, :], coef[0:T, :, :], sel[0:T, :, :], ALU.add))


def experts(nc, c, sb, ps, sem, Wg, Wu, Wd, x1, xhi, xlo, coef, out):
    raw = [sb(c, f"raw_{n}", [P, KB, FF]) for n in "gud"]
    hi = [sb(c, f"hi_{n}", [P, KB, FF], F32R) for n in "gud"]
    lo = [sb(c, f"lo_{n}", [P, KB, FF], F32R) for n in "gud"]
    sg = sb(c, "sg", [P, 2, HALF])
    hf = sb(c, "hf", [P, 2, HALF])
    hhi = sb(c, "hhi", [P, FB, NT], F32R)
    hlo = sb(c, "hlo", [P, FB, NT], F32R)
    ce = sb(c, "ce", [P, B])
    pg = ps(c, "pg", [P, 2, 512])
    pu = ps(c, "pu", [P, 2, 512])
    pd = ps(c, "pd", [P, 2, 512])

    w_load = [sem(c, f"load_{n}") for n in "gud"]
    h_done = [sem(c, f"hi_done_{n}") for n in "gud"]
    l_done = [sem(c, f"lo_done_{n}") for n in "gud"]
    gu_rdy = sem(c, "gu_rdy")
    sg_done = sem(c, "sg_done")
    hm_done = sem(c, "hm_done")
    hh_done = sem(c, "hh_done")
    hl_done = sem(c, "hl_done")
    dn_rdy = sem(c, "dn_rdy")
    ac_done = sem(c, "ac_done")
    ce_done = sem(c, "ce_done")
    stored = sem(c, "stored")
    block = c.enter_context(nc.Block())
    W = (Wg, Wu, Wd)

    @block.sync
    def _(sp):
        with sp.Fori(0, EX) as e:
            for n in range(3):
                sp.wait_ge(h_done[n], e + 1)
                sp.wait_ge(l_done[n], e + 1)
                sp.dma_start(raw[n][:, :, :], W[n][e].rearrange("(k p) f -> p k f", p=P)
                             ).then_inc(w_load[n], 16)
        for b in range(B):
            sp.wait_ge(ac_done, 8 * EX + b + 1)
            sp.dma_start(out[b], x1[0:T, b, :]).then_inc(stored, 16)
        sp.wait_ge(stored, 16 * B)

    @block.scalar
    def _(act):
        for n in range(3):
            act.sem_inc(h_done[n], 1)
        act.sem_inc(sg_done, 8)
        act.sem_inc(hh_done, 8)

        def split(e, n):
            act.wait_ge(w_load[n], 16 * (e + 1))
            if n < 2:
                act.wait_ge(gu_rdy, 8 * e + 8)
            else:
                act.wait_ge(dn_rdy, 8 * e + 8)
            act.activation(flat(hi[n][:, :, :]), flat(raw[n][:, :, :]), ACT.Copy).then_inc(h_done[n], 1)

        def silu(e, m):
            act.wait_ge(gu_rdy, 8 * (e + 1) + m + 1)
            act.wait_ge(hm_done, 8 * (e + 1) + m - 1)
            act.activation(sg[:, m % 2, :], pg[:, m % 2, 0:HALF], ACT.Silu).then_inc(sg_done, 1)

        def high(e, m):
            act.wait_ge(hm_done, 8 * (e + 1) + m + 1)
            act.wait_ge(dn_rdy, 8 * e + 8)
            act.activation(hhi[:, m % FB, m // FB * HALF:(m // FB + 1) * HALF], hf[:, m % 2, :],
                           ACT.Copy).then_inc(hh_done, 1)

        def expert(e, last=False):
            silu(e, 0)
            split(e, 2)
            for m in range(1, 8):
                high(e, m - 1)
                silu(e, m)
            high(e, 7)
            if not last:
                split(e + 1, 0)
                split(e + 1, 1)

        split(0, 0)
        split(0, 1)
        with act.Fori(0, EX - 1) as e:
            expert(e)
        expert(EX - 1, last=True)

    @block.tensor
    def _(pe):
        pe.sem_inc(gu_rdy, 8)
        pe.sem_inc(dn_rdy, 8)
        with pe.Fori(0, EX) as e:
            for m in range(8):
                f, h = m % FB, m // FB
                if m == 0:
                    for n in range(2):
                        pe.wait_ge(h_done[n], e + 2)
                        pe.wait_ge(l_done[n], e + 2)
                pe.wait_ge(hm_done, 8 * (e + 1) + m - 1)
                for n, bank in ((0, pg), (1, pu)):
                    for i in range(3 * KB):
                        k = i // 3
                        w, a = ((hi, xhi), (hi, xlo), (lo, xhi))[i % 3]
                        mm = pe.matmul(bank[:, m % 2, 0:HALF], w[n][:, k, f * P:(f + 1) * P],
                                       a[:, k, h * HALF:(h + 1) * HALF], start=(i == 0), stop=(i == 3 * KB - 1))
                mm.then_inc(gu_rdy, 1)
            pe.wait_ge(h_done[2], e + 2)
            pe.wait_ge(l_done[2], e + 2)
            for b in range(B):
                if b % 4 == 0:
                    pe.wait_ge(hl_done, 8 * (e + 1) + 4 + b)
                pe.wait_ge(ac_done, 8 * (e + 1) + b - 1)
                for i in range(3 * FB):
                    k = i // 3
                    a, w = ((hhi, hi), (hhi, lo), (hlo, hi))[i % 3]
                    mm = pe.matmul(pd[0:T, b % 2, :], a[:, k, b * T:(b + 1) * T], w[2][:, k, :],
                                   start=(i == 0), stop=(i == 3 * FB - 1))
                mm.then_inc(dn_rdy, 1)

    @block.vector
    def _(v):
        for n in range(3):
            v.sem_inc(l_done[n], 1)
        v.sem_inc(hm_done, 8)
        v.sem_inc(hl_done, 8)
        v.sem_inc(ac_done, 8)

        def split(e, n):
            v.wait_ge(h_done[n], e + 2)
            v.tensor_tensor(flat(lo[n][:, :, :]), flat(raw[n][:, :, :]), flat(hi[n][:, :, :]).bitcast(F32),
                            ALU.subtract).then_inc(l_done[n], 1)

        def product(e, m):
            v.wait_ge(sg_done, 8 * (e + 1) + m + 1)
            v.wait_ge(hh_done, 8 * (e + 1) + m - 1)
            v.tensor_tensor(hf[:, m % 2, :], sg[:, m % 2, :], pu[:, m % 2, 0:HALF], ALU.mult).then_inc(hm_done, 1)

        def low(e, m):
            v.wait_ge(hh_done, 8 * (e + 1) + m + 1)
            cols = slice(m // FB * HALF, (m // FB + 1) * HALF)
            v.tensor_tensor(hlo[:, m % FB, cols], hf[:, m % 2, :], hhi[:, m % FB, cols].bitcast(F32),
                            ALU.subtract).then_inc(hl_done, 1)

        def add(e, b):
            v.wait_ge(dn_rdy, 8 * (e + 1) + b + 1)
            if b == 0:
                v.wait_ge(ce_done, e + 1)
            v.scalar_tensor_tensor(out=x1[0:T, b, :], in0=pd[0:T, b % 2, :], scalar=ce[0:T, b:b + 1],
                                   in1=x1[0:T, b, :], op0=ALU.mult, op1=ALU.add).then_inc(ac_done, 1)

        def expert(e, last=False):
            v.wait_ge(ac_done, 8 * e + 8)
            v.tensor_copy(ce[0:T, :], coef[0:T, :, bass.ds(e, 1)].rearrange("p b e -> p (b e)")
                          ).then_inc(ce_done, 1)
            product(e, 0)
            split(e, 2)
            for m in range(1, 8):
                low(e, m - 1)
                product(e, m)
            low(e, 7)
            add(e, 0)
            add(e, 1)
            if not last:
                split(e + 1, 0)
            add(e, 2)
            add(e, 3)
            if not last:
                split(e + 1, 1)
            for b in range(4, B):
                add(e, b)

        split(0, 0)
        split(0, 1)
        with v.Fori(0, EX - 1) as e:
            expert(e)
        expert(EX - 1, last=True)


def kernel(**inputs):
    import numpy as np
    import concourse.bacc as bacc
    from concourse.bass_utils import run_bass_kernel_spmd

    a = {k: np.asarray(v) for k, v in inputs.items()}
    L = "L0_xattn_"

    def channels(v):
        return v.reshape(KB, P).T

    vecs = np.concatenate(
        [channels(a[L + n]) for n in ("ln_w", "ln_b", "q_in_scale", "qx_in_scale", "k_in_scale", "v_in_scale")]
        + [a[L + n].reshape(P, 1) for n in ("qln_w", "qln_b", "kln_w", "kln_b",
                                            "qxln_w", "qxln_b", "kxln_w", "kxln_b")], axis=1)
    scalars = np.array([a[L + n].reshape(()) for n in ("wq_scale", "wqx_scale", "wk_scale", "wv_scale",
                                                       "proj_in_scale", "proj_w_scale")]
                       + [a["g_xattn"].reshape(()), a["g_ffn"].reshape(())])
    kv = a[L + "w_kv_x"]
    parts = [(a[L + "wq"], 512), (a[L + "wqx"], 512), (a[L + "wk"], 256), (kv[:G * HD], 256),
             (kv[G * HD:], 256), (a[L + "wv"], 256)]
    w_in = np.concatenate([w.reshape(GP, n, KB, P).transpose(0, 3, 2, 1) for w, n in parts], axis=3)
    order = (1, 2, 0, 3)
    wproj = a[L + "wproj"].T.reshape(2, GP, 2, HPG, P, D).transpose(*order, 4, 5).reshape(GP, 8, P, D)
    smooth = a[L + "proj_smooth"].reshape(2, GP, 2, HPG, P).transpose(*order, 4).reshape(GP, 8, P)
    ctxT = a["ctx_2048"].reshape(B, NC, CT, KB, P).transpose(0, 1, 4, 3, 2)
    arrays = {
        "x": a["x"], "ctxT": ctxT, "vecs": vecs, "scalars": scalars,
        "smooth": smooth.transpose(2, 0, 1), "w_in": w_in, "wproj": wproj,
        "Wr": a["L0_ffn_Wr"], "Wg": a["L0_ffn_Wg"], "Wu": a["L0_ffn_Wu"], "Wd": a["L0_ffn_Wd"],
    }
    nc = bacc.Bacc("TRN2", target_bir_lowering=False, num_devices=1)
    feed, args = {}, []
    for name, v in arrays.items():
        v = np.ascontiguousarray(v)
        feed[f"in_{name}"] = v
        args.append(nc.dram_tensor(f"in_{name}", v.shape, mybir.dt.from_np(v.dtype), kind="ExternalInput").ap())
    o = nc.dram_tensor("out_0", (B, T, D), F32, kind="ExternalOutput").ap()
    transformer_block(nc, *args, o)
    r = run_bass_kernel_spmd(nc, [feed], core_ids=[0])
    return r.results[0]["out_0"]
```

```python
from contextlib import ExitStack

import concourse.bass as bass
from concourse import mybir

F32 = mybir.dt.float32
F32R = mybir.dt.float32r
BF16 = mybir.dt.bfloat16
U16 = mybir.dt.uint16
U32 = mybir.dt.uint32
ALU = mybir.AluOpType
ACT = mybir.ActivationFunctionType
AX = mybir.AxisListType.X

P = 128
B, T, D = 8, 112, 512
TC, NC = 375, 3
CT = TC // NC
KB = D // P
NH, G, HD = 16, 8, 128
HPG = NH // G
GP = 4
HP = NH // GP
NT = B * T
EX, FF = 8, 512
FB = FF // P
HALF = NT // 2
TJ = NT // P
GROUP = ((0, 4), (4, TJ))
EPS = 1e-5
SCALE = float(HD) ** -0.5
FP8_MAX = 448.0

CQ, CQX, CK, CKX, CVX, CV = 0, 512, 1024, 1280, 1536, 1792
WC = 2048
LNC = 1536

V_LNW, V_LNB, V_SQ, V_SQX, V_SK, V_SV = 0, 4, 8, 12, 16, 20
V_QW, V_QB, V_KW, V_KB, V_QXW, V_QXB, V_KXW, V_KXB = range(24, 32)
NV = 32
S_WQ, S_WQX, S_WK, S_WV, S_PIN, S_PW, S_GX, S_GF = range(8)


def transformer_block(nc, x, ctxT, vecs, scalars, smooth, w_in, wproj, Wr, Wg, Wu, Wd, out):
    catd = nc.dram_tensor("cat_scratch", (GP * B, P, 8 * T), BF16)
    cat_w = catd.ap() if hasattr(catd, "ap") else catd
    with ExitStack() as top:
        def sb(ctx, name, shape, dt=F32):
            return ctx.enter_context(nc.sbuf_tensor(name, shape, dt))

        def ps(ctx, name, shape, dt=F32):
            return ctx.enter_context(nc.psum_tensor(name, shape, dt))

        def sem(ctx, name):
            return ctx.enter_context(nc.semaphore(name))

        vec = sb(top, "vec", [P, NV])
        scal = sb(top, "scal", [P, 8])
        gate = sb(top, "gate", [P, 2])
        proj_scale = sb(top, "proj_scale", [P, 1])
        ident = sb(top, "ident", [P, P])
        mhalf = sb(top, "mhalf", [P, 16])
        epst = sb(top, "epst", [P, 16])

        shared = sb(top, "shared", [P, KB * WC])
        wp_load = [sem(top, f"wp_load{r}") for r in range(4)]
        cat_load = [sem(top, f"cat_load{r}") for r in range(2)]

        with ExitStack() as c:
            xq = sb(c, "xq", [P, 4, KB, NT], BF16)
            smi = sb(c, "smi", [P, GP, 8])
            wsc = sb(c, "wsc", [P, 4, KB])
            wmul = sb(c, "wmul", [P, KB, LNC // HD])
            weights = CentredWeights(c, sb, sem, w_in, shared, wsc, wmul)
            with ExitStack() as c0:
                quantise_inputs(nc, c0, sb, ps, sem, x, vecs, scalars, smooth, vec, scal, gate,
                                proj_scale, ident, mhalf, epst, xq, smi, weights)
            with ExitStack() as c1:
                attention(nc, c1, sb, ps, sem, ctxT, wproj, cat_w, vec, ident, mhalf, epst, xq, smi,
                          weights, shared, wp_load, cat_load)
        with ExitStack() as c:
            x1 = sb(c, "x1", [P, TJ, D])
            xT = sb(c, "xT", [P, KB, NT])
            xhi = sb(c, "xhi", [P, KB, NT], F32R)
            xlo = sb(c, "xlo", [P, KB, NT], F32R)
            ffn = SplitWeights(c, sb, sem)
            with ExitStack() as c2:
                projection(nc, c2, sb, ps, sem, x, wproj, cat_w, (Wg, Wu, Wd), ident, mhalf,
                           proj_scale, x1, xT, xhi, xlo, shared, wp_load, cat_load, ffn)
            with ExitStack() as c3:
                experts(nc, c3, sb, ps, sem, Wr, (Wg, Wu, Wd), gate, x1, xT, xhi, xlo, ffn, out)


class CentredWeights:

    def __init__(self, c, sb, sem, w_in, shared, wsc, wmul):
        self.w_in, self.wsc, self.wmul = w_in, wsc, wmul
        self.raw = shared[:, :].rearrange("p (k n) -> p k n", k=KB)
        self.mean = sb(c, "w_mean", [P, KB, LNC // HD])
        self.in_done = sem(c, "w_in_done")
        self.seen = sem(c, "w_seen")
        self.sum = sem(c, "w_sum")
        self.mu = sem(c, "w_mu")
        self.cen = sem(c, "w_cen")

    def fetch(self, sp, g, k):
        sp.dma_start(self.raw[:, k, :], self.w_in[g, :, k, :]).then_inc(self.in_done, 16)

    def means(self, v, g, k):
        mean = self.mean[:, bass.ds(k, 1), :].rearrange("p a b -> p (a b)")
        v.wait_ge(self.in_done, 16 * KB * (g + 1))
        v.wait_ge(self.cen, 4 * g + k + 1)
        v.sem_inc(self.seen, 1)
        v.tensor_reduce(mean, self.raw[:, bass.ds(k, 1), 0:LNC].rearrange("p a (h d) -> p (a h) d", d=HD),
                        AX, ALU.add).then_inc(self.sum, 1)
        v.wait_ge(self.sum, 4 * g + k + 1)
        v.tensor_tensor(mean, mean, self.wmul[:, bass.ds(k, 1), :].rearrange("p a b -> p (a b)"),
                        ALU.mult).then_inc(self.mu, 1)

    def centre(self, act, g, k, part):
        if part == 0:
            act.wait_ge(self.mu, 4 * g + k + 1)
            act.sem_inc(self.seen, 1)
        block_k = bass.ds(k, 1)
        for h in range(4 * part, 4 * part + 4):
            cols = self.raw[:, block_k, h * HD:(h + 1) * HD].rearrange("p a b -> p (a b)")
            mean = self.mean[:, block_k, h:h + 1].rearrange("p a b -> p (a b)")
            if h < CKX // HD:
                n = 0 if h < CQX // HD else 1 if h < CK // HD else 2
                act.activation(cols, cols, ACT.Identity, bias=mean, scale=self.wsc[:, n, block_k])
            else:
                act.activation(cols, cols, ACT.Identity, bias=mean)
        if part == 2:
            cols = self.raw[:, block_k, CV:WC].rearrange("p a b -> p (a b)")
            act.activation(cols, cols, ACT.Copy, scale=self.wsc[:, 3, block_k]).then_inc(self.cen, 1)


class SplitWeights:

    def __init__(self, c, sb, sem):
        self.raw = [sb(c, f"raw_{n}", [P, KB, FF]) for n in "gud"]
        self.hi = [sb(c, f"hi_{n}", [P, KB, FF], F32R) for n in "gud"]
        self.lo = [sb(c, f"lo_{n}", [P, KB, FF], F32R) for n in "gud"]
        self.load = [sem(c, f"load_{n}") for n in "gud"]
        self.h_done = [sem(c, f"hi_done_{n}") for n in "gud"]
        self.l_done = [sem(c, f"lo_done_{n}") for n in "gud"]

    def fetch(self, sp, W, e, n):
        sp.dma_start(self.raw[n][:, :, :], W[n][e].rearrange("(k p) f -> p k f", p=P)
                     ).then_inc(self.load[n], 16)

    def high(self, act, e, n):
        act.wait_ge(self.load[n], 16 * (e + 1))
        act.activation(flat(self.hi[n][:, :, :]), flat(self.raw[n][:, :, :]), ACT.Copy
                       ).then_inc(self.h_done[n], 1)

    def low(self, v, e, n):
        v.wait_ge(self.h_done[n], e + 2)
        v.tensor_tensor(flat(self.lo[n][:, :, :]), flat(self.raw[n][:, :, :]),
                        flat(self.hi[n][:, :, :]).bitcast(F32), ALU.subtract).then_inc(self.l_done[n], 1)


def quantise_inputs(nc, c, sb, ps, sem, x, vecs, scalars, smooth, vec, scal, gate, proj_scale,
                    ident, mhalf, epst, xq, smi, weights):
    LAG = 3
    NORMS = []
    for j in range(TJ + LAG):
        if j < TJ:
            NORMS.append((0, j))
        if j >= LAG:
            NORMS.append((1, j - LAG))
    N = len(NORMS)
    wsc, wmul = weights.wsc, weights.wmul

    xs = sb(c, "xs", [P, TJ, D])
    st = sb(c, "st", [P, N, 6])
    mv = sb(c, "mv", [P, N, 2])
    rstd = sb(c, "rstd", [P, N])
    shift = sb(c, "shift0", [P, N])
    hT = sb(c, "hT", [P, KB, NT])
    inv = sb(c, "inv", [P, 4, KB])
    smr = sb(c, "smr", [P, GP, 8])
    yq = sb(c, "yq", [P, 2, KB, NT], BF16)
    ye = sb(c, "ye", [P, KB, NT], BF16)
    ysum = sb(c, "ysum", [P, KB, NT], BF16)
    pt = ps(c, "pt", [P, 4, 512])

    vec_in = sem(c, "vec_in")
    x_in = [sem(c, f"x_in{j}") for j in range(TJ)]
    const_done = sem(c, "const_done")
    pool_self = sem(c, "pool_self")
    bn_done = sem(c, "bn_done0")
    ag_done = sem(c, "ag_done0")
    stat_done = sem(c, "stat_done")
    rstd_pow = sem(c, "rstd_pow0")
    rstd_done = sem(c, "rstd_done")
    normed = sem(c, "normed")
    dve = sem(c, "dve_chain0")
    tr_done = sem(c, "tr_done")
    hT_done = sem(c, "hT_done")
    scal_done = sem(c, "scal_done")
    inv_done = sem(c, "inv_done")
    y_done = sem(c, "y_done")
    round_done = sem(c, "round_done")
    block = c.enter_context(nc.Block())

    @block.sync
    def _(sp):
        tokens = x.rearrange("b t d -> (b t) d")
        sp.dma_start(xs[:, 0, :], tokens[0:P, :]).then_inc(x_in[0], 16)
        sp.dma_start(vec[:, :], vecs).then_inc(vec_in, 16)
        sp.dma_start(scal[:, :], scalars.partition_broadcast(P)).then_inc(vec_in, 16)
        sp.dma_start(smr[:, :, :], smooth).then_inc(vec_in, 16)
        for j in range(1, TJ):
            sp.dma_start(xs[:, j, :], tokens[j * P:(j + 1) * P, :]).then_inc(x_in[j], 16)
        for k in range(KB):
            weights.fetch(sp, 0, k)

    @block.gpsimd
    def _(pool):
        pool.memset(ident[:, :], 0.0).then_inc(pool_self, 1)
        pool.memset(mhalf[:, :], -0.5).then_inc(pool_self, 1)
        pool.memset(epst[:, :], EPS).then_inc(pool_self, 1)
        pool.wait_ge(pool_self, 3)
        pool.affine_select(out=ident[:, :], in_=ident[:, :], compare_op=ALU.not_equal, fill=1.0,
                           base=0, pattern=[[-1, P]], channel_multiplier=1).then_inc(const_done, 1)
        for i in range(N):
            one = slice(i, i + 1)
            pool.wait_ge(stat_done, i + 1)
            pool.tensor_tensor(rstd[:, one], mv[:, i, 1:2], mhalf[:, 0:1], ALU.pow).then_inc(rstd_pow, 1)
            pool.wait_ge(rstd_pow, i + 1)
            pool.tensor_tensor(shift[:, one], mv[:, i, 0:1], rstd[:, one], ALU.mult).then_inc(rstd_done, 1)

    @block.scalar
    def _(act):
        act.sem_inc(weights.cen, 4)
        act.wait_ge(vec_in, 48)
        act.activation(gate[:, :], scal[:, S_GX:S_GF + 1], ACT.Tanh).then_inc(scal_done, 1)
        for i, (_, j) in enumerate(NORMS):
            act.wait_ge(rstd_done, i + 1)
            act.activation(xs[:, j, :], xs[:, j, :], ACT.Identity, bias=shift[:, i:i + 1],
                           scale=rstd[:, i:i + 1]).then_inc(normed, 1)
        for n in range(2 * KB):
            k, (lo, hi) = n % KB, GROUP[n // KB]
            act.wait_ge(tr_done, n + 1)
            act.activation(hT[:, k, lo * P:hi * P], pt[:, n % 4, 0:(hi - lo) * P], ACT.Identity,
                           bias=vec[:, V_LNB + k:V_LNB + k + 1],
                           scale=vec[:, V_LNW + k:V_LNW + k + 1]).then_inc(hT_done, 1)
        act.wait_ge(hT_done, 2 * KB)
        act.wait_ge(inv_done, 1)
        for n in range(4):
            if n >= 2:
                act.wait_ge(round_done, n - 1)
            for k in range(KB):
                last = act.activation(yq[:, n % 2, k, :], hT[:, k, :], ACT.Copy, scale=inv[:, n, k:k + 1])
            last.then_inc(y_done, 1)
            if n >= 1:
                for part in range(3):
                    weights.centre(act, 0, n - 1, part)
        for part in range(3):
            weights.centre(act, 0, KB - 1, part)

    @block.tensor
    def _(pe):
        pe.wait_ge(const_done, 1)
        for n in range(2 * KB):
            k, (lo, hi) = n % KB, GROUP[n // KB]
            pe.wait_ge(normed, NORMS.index((1, hi - 1)) + 1)
            if n >= 4:
                pe.wait_ge(hT_done, n - 3)
            for j in range(lo, hi):
                t = pe.transpose(pt[:, n % 4, (j - lo) * P:(j - lo + 1) * P], xs[:, j, k * P:(k + 1) * P],
                                 ident[:, :])
            t.then_inc(tr_done, 1)

    @block.vector
    def _(v):
        count = [0]

        def link(ins):
            count[0] += 1
            ins.then_inc(dve, 1)
            v.wait_ge(dve, count[0])

        def mean_and_variance(i):
            v.wait_ge(bn_done, i + 1)
            v.bn_aggr(mv[:, i, :], st[:, i, :]).then_inc(ag_done, 1)
            v.wait_ge(ag_done, i + 1)
            v.tensor_scalar(mv[:, i, 0:1], mv[:, i, 0:1], -1.0, None, ALU.mult)
            v.tensor_scalar(mv[:, i, 1:2], mv[:, i, 1:2], EPS, None, ALU.add).then_inc(stat_done, 1)

        for i, (n, j) in enumerate(NORMS):
            if n == 0:
                v.wait_ge(x_in[j], 16)
            else:
                v.wait_ge(normed, NORMS.index((0, j)) + 1)
            v.bn_stats(st[:, i, :], xs[:, j, :]).then_inc(bn_done, 1)
            if i > 0:
                mean_and_variance(i - 1)
        mean_and_variance(N - 1)
        v.wait_ge(vec_in, 48)
        v.reciprocal(inv[:, :, :].rearrange("p a b -> p (a b)"), vec[:, V_SQ:V_SV + KB]).then_inc(inv_done, 1)
        link(v.reciprocal(smi[:, :, :], smr[:, :, :]))
        for n in range(4):
            last = v.tensor_scalar(wsc[:, n, :], vec[:, V_SQ + 4 * n:V_SQ + 4 * n + 4],
                                   scal[:, S_WQ + n:S_WQ + n + 1], None, ALU.mult)
        link(last)
        for n, (lo, hi) in enumerate(((0, 4), (4, 8), (8, 10))):
            last = v.tensor_scalar(wmul[:, :, lo:hi], wsc[:, n, :].unsqueeze(2).to_broadcast([P, KB, hi - lo]),
                                   -1.0 / HD, None, ALU.mult)
        v.memset(wmul[:, :, 10:12], -1.0 / HD)
        for col in (V_KW, V_KB, V_KXW, V_KXB):
            last = v.tensor_scalar(vec[:, col:col + 1], vec[:, col:col + 1], SCALE, None, ALU.mult)
        link(last)
        link(v.tensor_tensor(proj_scale[:, :], scal[:, S_PIN:S_PIN + 1], scal[:, S_PW:S_PW + 1], ALU.mult))
        v.wait_ge(scal_done, 1)
        link(v.tensor_tensor(proj_scale[:, :], proj_scale[:, :], gate[:, 0:1], ALU.mult))
        for k in range(KB):
            weights.means(v, 0, k)
        for n in range(4):
            v.wait_ge(y_done, n + 1)
            round_fp8(v, link, flat(xq[:, n, :, :]), flat(yq[:, n % 2, :, :]), flat(ye[:, :, :]),
                      flat(ysum[:, :, :])).then_inc(round_done, 1)


def flat(ap):
    return ap.rearrange("p a b -> p (a b)")


def round_fp8(v, link, out, y, e, total):
    link(v.tensor_scalar(y, y, FP8_MAX, -FP8_MAX, ALU.min, ALU.max))
    link(v.tensor_scalar(e.bitcast(U16), y.bitcast(U16), 0x7F80, None, ALU.bitwise_and))
    link(v.tensor_scalar(e, e, 2.0 ** -6, 1.5 * 2.0 ** 4, ALU.max, ALU.mult))
    link(v.tensor_tensor(total, y, e, ALU.add))
    return v.tensor_tensor(out, total, e, ALU.subtract)


def cat_tile(shared):
    return shared[:, 4 * D:4 * D + B * 4 * T].bitcast(BF16).rearrange("p (b n) -> p b n", b=B)


def attention(nc, c, sb, ps, sem, ctxT, wproj, catd, vec, ident, mhalf, epst, xq, smi,
              weights, shared, wp_load, cat_load):
    w_raw, w_cen = weights.raw, weights.cen
    w_hi = sb(c, "w_hi", [P, KB, WC], F32R)
    w_lo = sb(c, "w_lo", [P, KB, WC], F32R)
    smg = sb(c, "smg", [P, 8])
    c_raw = sb(c, "c_raw", [P, NC, KB, CT])
    c_hi = sb(c, "c_hi", [P, NC, KB, CT], F32R)
    c_lo = sb(c, "c_lo", [P, NC, KB, CT], F32R)
    xqs = sb(c, "xqs", [P, 4, KB, T], F32R)
    nq = sb(c, "nq", [P, 512])
    nqx = sb(c, "nqx", [P, 512])
    nk = sb(c, "nk", [P, 256])
    nkx = sb(c, "nkx", [P, NC, 256])
    val = sb(c, "val", [P, 2, 256])
    valx = sb(c, "valx", [P, 2, NC, 256])
    sq = sb(c, "sq", [P, 2, 512])
    ss = sb(c, "ss", [P, 16])
    va = sb(c, "va", [P, 16])
    rs = sb(c, "rs", [P, 16])
    qT = sb(c, "qT", [P, HP * T])
    qxT = sb(c, "qxT", [P, HP * T])
    kT = sb(c, "kT", [P, 2 * T])
    kxT = sb(c, "kxT", [P, 2, TC])
    nmax = sb(c, "nmax", [P, 8])
    lsum = sb(c, "lsum", [P, 8])
    linv = sb(c, "linv", [P, 8])
    pself = sb(c, "pself", [P, HP, T])
    pcross = sb(c, "pcross", [P, HP, TC])
    pselfT = sb(c, "pselfT", [P, HP, T])
    pcrossT = sb(c, "pcrossT", [P, NC, HP, T])
    yb = sb(c, "yb", [P, 8 * T], BF16)
    ye = sb(c, "ye1", [P, 8 * T], BF16)
    ysum = sb(c, "ysum1", [P, 8 * T], BF16)
    cat = sb(c, "cat", [P, 8 * T], BF16)

    p_proj = ps(c, "p_proj", [P, 2, 512])
    p_tr = ps(c, "p_tr", [P, 2, 512])
    p_self = ps(c, "p_self", [P, 512])
    p_cross = ps(c, "p_cross", [P, 2, 512])
    p_out = ps(c, "p_out", [P, 512])

    c_in_done = [sem(c, f"c_in{k}") for k in range(NC)]
    wh_done = sem(c, "wh_done")
    wl_done = [sem(c, f"wl_done{k}") for k in range(KB)]
    ch_done = sem(c, "ch_done")
    cl_done = sem(c, "cl_done")
    xqs_done = sem(c, "xqs_done")
    pj_rdy = sem(c, "pj_rdy")
    pj_done = sem(c, "pj_done")
    rd_done = sem(c, "rd_done")
    va_done = sem(c, "va_done")
    rs_done = sem(c, "rs_done")
    ln_done = sem(c, "ln_done")
    tr_rdy = sem(c, "tr_rdy")
    t_done = sem(c, "t_done")
    pt_done = sem(c, "pt_done")
    ss_rdy = sem(c, "ss_rdy")
    ms_done = sem(c, "ms_done")
    es_done = sem(c, "es_done")
    ns_done = sem(c, "ns_done")
    sx_rdy = sem(c, "sx_rdy")
    mx_done = sem(c, "mx_done")
    ex_done = sem(c, "ex_done")
    nx_done = sem(c, "nx_done")
    ou_rdy = sem(c, "ou_rdy")
    ya_done = sem(c, "ya_done")
    ct_done = sem(c, "ct_done")
    cat_out = sem(c, "cat_out")
    dv = sem(c, "dve_chain1")
    block = c.enter_context(nc.Block())

    def passes(eng, step):
        step(0, 0, None, 0, True, None)

        def batches(gp):
            s0 = gp * B
            with eng.Fori(0, 3) as i:
                s = s0 + 2 * i
                step(s + 1, 1, s, gp + 1, False, None)
                step(s + 2, 0, s + 1, gp + 1, False, i)
            step(s0 + 7, 1, s0 + 6, gp + 1, False, 3)

        with eng.Fori(0, GP - 1) as gp:
            batches(gp)
            step(gp * B + B, 0, gp * B + 7, gp + 1, True, None)
        s0 = (GP - 1) * B
        with eng.Fori(0, 3) as i:
            s = s0 + 2 * i
            step(s + 1, 1, s, None, False, None)
            step(s + 2, 0, s + 1, None, False, None)
        step(s0 + 7, 1, s0 + 6, None, False, None)
        step(None, 0, s0 + 7, None, False, None)

    @block.sync
    def _(sp):
        def load_w(gp):
            for k in range(KB):
                sp.wait_ge(wl_done[k], gp + 1)
                sp.wait_ge(wh_done, 4 * gp + k + 1)
                weights.fetch(sp, gp, k)

        def load_c(s, b, k):
            sp.wait_ge(ch_done, 3 * s + k + 1)
            sp.wait_ge(cl_done, 3 * s + k + 1)
            sp.dma_start(c_raw[:, k, :, :], ctxT[b, k]).then_inc(c_in_done[k], 16)

        def store(st):
            sp.wait_ge(ct_done, st + 1)
            sp.dma_start(catd[st], cat[:, :]).then_inc(cat_out, 16)

        sp.sem_inc(cat_out, 16)
        for gp in range(GP):
            s0 = gp * B
            for b in range(2):
                for k in range(NC):
                    load_c(s0 + b, b, k)
                if gp > 0:
                    store(s0 + b - 2)
            if gp + 1 < GP:
                load_w(gp + 1)
            else:
                for k in range(KB):
                    sp.wait_ge(wl_done[k], GP + 1)
                    sp.wait_ge(wh_done, 4 * GP + k + 1)
                for n in range(4):
                    sp.dma_start(shared[:, n * D:(n + 1) * D], wproj[0, n]).then_inc(wp_load[n], 16)
                sp.wait_ge(cat_out, 16 * (B + 1))
                sp.dma_start(cat_tile(shared), catd[0:B].rearrange("b p n -> p b n")
                             ).then_inc(cat_load[0], 16)
            with sp.Fori(2, B) as b:
                for k in range(NC):
                    load_c(s0 + b, b, k)
                store(s0 + b - 2)
        store(GP * B - 2)
        store(GP * B - 1)
        sp.wait_ge(cat_out, 16 * (GP * B + 1))

    @block.gpsimd
    def _(pool):
        pool.sem_inc(cl_done, 3)
        pool.sem_inc(wl_done[KB - 1], 1)
        pool.sem_inc(va_done, 6)
        pool.sem_inc(rs_done, 6)

        def rstd(s, j):
            rows, lo, hi = STAT[j]
            pool.wait_ge(rd_done, 6 * (s + 1) + j + 1)
            pool.tensor_tensor(va[0:rows, lo:hi], ss[0:rows, lo:hi], epst[0:rows, lo:hi],
                               ALU.add).then_inc(va_done, 1)
            pool.wait_ge(va_done, 6 * (s + 1) + j + 1)
            pool.wait_ge(ln_done, 6 * s + j + 1)
            pool.tensor_tensor(rs[0:rows, lo:hi], va[0:rows, lo:hi], mhalf[0:rows, lo:hi],
                               ALU.pow).then_inc(rs_done, 1)

        def c_low(s, k):
            pool.wait_ge(ch_done, 3 * (s + 1) + k + 1)
            pool.wait_ge(pj_rdy, 6 * s + 4 + k)
            pool.tensor_tensor(flat(c_lo[:, k, :, :]), flat(c_raw[:, k, :, :]),
                               flat(c_hi[:, k, :, :]).bitcast(F32), ALU.subtract).then_inc(cl_done, 1)

        def w_low(g, k):
            pool.wait_ge(wh_done, 4 * (g + 1) + k + 1)
            pool.tensor_tensor(w_lo[:, k, :], w_raw[:, k, :], w_hi[:, k, :].bitcast(F32),
                               ALU.subtract).then_inc(wl_done[k], 1)

        def step(s, par, t, g, first, k):
            if first:
                if t is not None:
                    w_low(g, 0)
                w_low(g, KB - 1)
            if s is None:
                return
            for j in range(3):
                c_low(s, j)
                rstd(s, j)
            for j in range(3, 6):
                rstd(s, j)

        passes(pool, step)

    @block.scalar
    def _(act):
        act.sem_inc(ch_done, 3)
        act.sem_inc(pj_done, 6)
        act.sem_inc(t_done, 5)
        act.sem_inc(es_done, 1)
        act.sem_inc(ex_done, 4)
        act.sem_inc(wh_done, 4)

        def w_high(g, k):
            act.wait_ge(pj_rdy, 6 * B * g + 6)
            act.wait_ge(w_cen, 4 * (g + 1) + k + 1)
            act.activation(w_hi[:, k, :], w_raw[:, k, :], ACT.Copy).then_inc(wh_done, 1)

        def c_high(s, k):
            act.wait_ge(c_in_done[k], 16 * (s + 1))
            act.wait_ge(pj_rdy, 6 * s + 4 + k)
            act.activation(flat(c_hi[:, k, :, :]), flat(c_raw[:, k, :, :]), ACT.Copy).then_inc(ch_done, 1)

        def take(s, j, par):
            bank = p_proj[:, j % 2, :]
            act.wait_ge(pj_rdy, 6 * (s + 1) + j + 1)
            act.wait_ge(tr_rdy, 10 * s + (j + 1 if j < 3 else 5))
            if j < 2:
                act.activation((nq, nqx)[j][0:T, :], bank[0:T, :], ACT.Copy)
                n, rows = 512, T
            elif j == 2:
                act.wait_ge(ou_rdy, 2 * s)
                act.activation(nk[0:T, :], bank[0:T, 0:256], ACT.Copy)
                act.activation(val[0:T, par, :], bank[0:T, 256:512], ACT.Copy)
                n, rows = 256, T
            else:
                act.activation(nkx[0:CT, j - 3, :], bank[0:CT, 0:256], ACT.Copy)
                act.activation(valx[0:CT, par, j - 3, :], bank[0:CT, 256:512], ACT.Copy)
                n, rows = 256, CT
            act.wait_ge(rd_done, 6 * (s + 1) + j - 1)
            act.activation(sq[0:rows, j % 2, 0:n], bank[0:rows, 0:n], ACT.Square,
                           scale=float(HD) ** -0.5).then_inc(pj_done, 1)

        def turned(t, n):
            act.wait_ge(tr_rdy, 10 * (t + 1) + n + 1)
            if n in (0, 2):
                act.wait_ge(ss_rdy, t + 1)
            else:
                act.wait_ge(sx_rdy, 4 * t + 4)
            dst = (qT[:, :], qxT[:, :], kT[:, :], kxT[:, 0, :], kxT[:, 1, :])[n]
            w, b = ((V_QW, V_QB), (V_QXW, V_QXB), (V_KW, V_KB), (V_KXW, V_KXB), (V_KXW, V_KXB))[n]
            act.activation(dst, p_tr[:, n % 2, 0:TURNED[n]], ACT.Identity, bias=vec[:, b:b + 1],
                           scale=vec[:, w:w + 1]).then_inc(t_done, 1)

        def exp_self(t):
            act.wait_ge(ms_done, t + 2)
            act.wait_ge(tr_rdy, 10 * t + 6)
            act.wait_ge(ns_done, t + 1)
            for h in range(HP):
                last = act.activation(pself[0:T, h, :], p_self[0:T, h * T:(h + 1) * T], ACT.Exp,
                                      bias=nmax[0:T, h:h + 1], accum_out=lsum[0:T, h:h + 1])
            last.then_inc(es_done, 1)

        def exp_cross(t, h):
            act.wait_ge(mx_done, 4 * (t + 1) + h + 1)
            act.wait_ge(tr_rdy, 10 * t + 7 + h)
            act.wait_ge(nx_done, 4 * t + h + 1)
            act.activation(pcross[0:T, h, :], p_cross[0:T, h % 2, 0:TC], ACT.Exp,
                           bias=nmax[0:T, 4 + h:5 + h], accum_out=lsum[0:T, 4 + h:5 + h]).then_inc(ex_done, 1)

        def step(s, par, t, g, first, k):
            A, Q = s is not None and not first, t is not None
            if Q: turned(t, 0)
            if Q: turned(t, 1)
            if first: w_high(g, 0)
            if A: take(s, 0, par)
            if A: c_high(s, 0)
            if Q: turned(t, 2)
            if Q: turned(t, 3)
            if first: w_high(g, 1)
            if A: take(s, 1, par)
            if A: c_high(s, 1)
            if Q: exp_self(t)
            if Q: exp_cross(t, 0)
            if Q: exp_cross(t, 1)
            if Q: turned(t, 4)
            if first: w_high(g, 2)
            if first: w_high(g, 3)
            if A: take(s, 2, par)
            if A: c_high(s, 2)
            if Q: exp_cross(t, 2)
            if Q: exp_cross(t, 3)
            if A: take(s, 3, par)
            if k is not None: weights.centre(act, g, k, 0)
            if A: take(s, 4, par)
            if k is not None: weights.centre(act, g, k, 1)
            if A: take(s, 5, par)
            if k is not None: weights.centre(act, g, k, 2)
            if first:
                for j in range(3):
                    c_high(s, j)
                for j in range(6):
                    take(s, j, par)

        passes(act, step)

    @block.tensor
    def _(pe):
        pe.sem_inc(pj_rdy, 6)
        pe.sem_inc(tr_rdy, 10)
        pe.sem_inc(ss_rdy, 1)
        pe.sem_inc(sx_rdy, 4)
        pe.sem_inc(ou_rdy, 2)

        def project(s, j, g=None):
            pe.wait_ge(pj_done, 6 * (s + 1) + j - 1)
            bank = p_proj[:, j % 2, :]
            if j == 0:
                pe.wait_ge(xqs_done, s + 1)
            if j < 3:
                for n, o, lo, w in (((0, 0, CQ, 512),), ((1, 0, CQX, 512),),
                                    ((2, 0, CK, 256), (3, 256, CV, 256)))[j]:
                    for i in range(2 * KB):
                        k = i // 2
                        if g is not None and i % 2 == 0:
                            pe.wait_ge(wh_done, 4 * (g + 1) + k + 1)
                            pe.wait_ge(wl_done[k], g + 2)
                        m = pe.matmul(bank[0:T, o:o + w], xqs[:, n, k, :], (w_hi, w_lo)[i % 2][:, k, lo:lo + w],
                                      start=(i == 0), stop=(i == 2 * KB - 1))
            else:
                ch = j - 3
                pe.wait_ge(ch_done, 3 * (s + 1) + ch + 1)
                pe.wait_ge(cl_done, 3 * (s + 1) + ch + 1)
                for i in range(3 * KB):
                    k = i // 3
                    a, w = ((c_hi, w_hi), (c_hi, w_lo), (c_lo, w_hi))[i % 3]
                    m = pe.matmul(bank[0:CT, :], a[:, ch, k, :], w[:, k, CKX:CV],
                                  start=(i == 0), stop=(i == 3 * KB - 1))
            m.then_inc(pj_rdy, 1)

        def bank_free(t, n):
            if n < 2:
                pe.wait_ge(pt_done, 5 * t + 4 + n)
            elif n < 7:
                pe.wait_ge(t_done, 5 * (t + 1) + n - 1)
            else:
                pe.wait_ge(pt_done, 5 * (t + 1) + n - 6)

        def turn(t, n):
            pe.wait_ge(ln_done, 6 * (t + 1) + (1, 2, 3, 6, 6)[n])
            bank_free(t, n)
            if n < 3:
                src = (nq, nqx, nk)[n]
                for h in range((4, 4, 2)[n]):
                    m = pe.transpose(p_tr[:, n % 2, h * T:(h + 1) * T], src[0:T, h * P:(h + 1) * P],
                                     ident[0:T, 0:T])
            else:
                for k in range(NC):
                    m = pe.transpose(p_tr[:, n % 2, k * CT:(k + 1) * CT],
                                     nkx[0:CT, k, (n - 3) * P:(n - 2) * P], ident[0:CT, 0:CT])
            m.then_inc(tr_rdy, 1)

        def score_self(t):
            pe.wait_ge(t_done, 5 * (t + 1) + 3)
            pe.wait_ge(es_done, t + 1)
            for h in range(HP):
                m = pe.matmul(p_self[0:T, h * T:(h + 1) * T], qT[:, h * T:(h + 1) * T],
                              kT[:, h // HPG * T:(h // HPG + 1) * T], start=True, stop=True)
            m.then_inc(ss_rdy, 1)

        def score_cross(t, h):
            pe.wait_ge(t_done, 5 * (t + 1) + 4 + h // HPG)
            pe.wait_ge(ex_done, 4 * (t + 1) + h - 1)
            pe.matmul(p_cross[0:T, h % 2, 0:TC], qxT[:, h * T:(h + 1) * T], kxT[:, h // HPG, :],
                      start=True, stop=True).then_inc(sx_rdy, 1)

        def turn_self(t):
            pe.wait_ge(ns_done, t + 2)
            bank_free(t, 5)
            for h in range(HP):
                m = pe.transpose(p_tr[0:T, 1, h * T:(h + 1) * T], pself[0:T, h, :], ident[0:T, 0:T])
            m.then_inc(tr_rdy, 1)

        def turn_cross(t, h):
            pe.wait_ge(nx_done, 4 * (t + 1) + h + 1)
            bank_free(t, 6 + h)
            for k in range(NC):
                m = pe.transpose(p_tr[0:CT, h % 2, k * T:(k + 1) * T], pcross[0:T, h, k * CT:(k + 1) * CT],
                                 ident[0:T, 0:T])
            m.then_inc(tr_rdy, 1)

        def outputs(t, g, par):
            pe.wait_ge(pt_done, 5 * (t + 1) + (3, 5)[g])
            pe.wait_ge(pj_done, 6 * (t + 1) + 6)
            pe.wait_ge(ya_done, 2 * (t + 1) + g)
            pe.matmul(p_out[:, 0:HPG * T], val[0:T, par, g * P:(g + 1) * P],
                      flat(pselfT[0:T, HPG * g:HPG * (g + 1), :]), start=True, stop=True)
            for k in range(NC):
                m = pe.matmul(p_out[:, HPG * T:2 * HPG * T], valx[0:CT, par, k, g * P:(g + 1) * P],
                              flat(pcrossT[0:CT, k, HPG * g:HPG * (g + 1), :]),
                              start=(k == 0), stop=(k == NC - 1))
            m.then_inc(ou_rdy, 1)

        def step(s, par, t, g, first, k):
            A, Q = s is not None and not first, t is not None
            if A: project(s, 0)
            if Q: turn(t, 0)
            if Q: turn(t, 1)
            if A: project(s, 1)
            if Q: turn(t, 2)
            if Q: turn(t, 3)
            if A: project(s, 2)
            if Q: score_self(t)
            if Q: score_cross(t, 0)
            if Q: score_cross(t, 1)
            if Q: turn(t, 4)
            if A: project(s, 3)
            if Q: turn_self(t)
            if Q: turn_cross(t, 0)
            if Q: score_cross(t, 2)
            if Q: turn_cross(t, 1)
            if Q: score_cross(t, 3)
            if A: project(s, 4)
            if first: project(s, 0, g)
            if Q: outputs(t, 0, 1 - par)
            if Q: turn_cross(t, 2)
            if Q: turn_cross(t, 3)
            if A: project(s, 5)
            if first: project(s, 1)
            if Q: outputs(t, 1, 1 - par)
            if first:
                for j in range(2, 6):
                    project(s, j)

        passes(pe, step)

    @block.vector
    def _(v):
        v.sem_inc(rd_done, 6)
        v.sem_inc(ln_done, 6)
        v.sem_inc(pt_done, 5)
        v.sem_inc(ms_done, 1)
        v.sem_inc(ns_done, 1)
        v.sem_inc(mx_done, 4)
        v.sem_inc(nx_done, 4)
        v.sem_inc(ya_done, 2)
        for k in range(KB - 1):
            v.sem_inc(wl_done[k], 1)
        CH = 9

        def smooth_of(g):
            v.wait_ge(ya_done, 2 * B * g + 2)
            v.tensor_copy(smg[:, :], smi[:, bass.ds(g, 1), :].rearrange("p a b -> p (a b)"))

        def w_low(g, k):
            v.wait_ge(wh_done, 4 * (g + 1) + k + 1)
            v.wait_ge(pj_rdy, 6 * B * g + 6)
            v.tensor_tensor(w_lo[:, k, :], w_raw[:, k, :], w_hi[:, k, :].bitcast(F32),
                            ALU.subtract).then_inc(wl_done[k], 1)

        def inputs(s, b):
            v.wait_ge(pj_rdy, 6 * s + 3)
            for n in range(4):
                last = v.tensor_copy(xqs[:, n, :, :], xq[:, n, :, bass.ds(b * T, T)])
            last.then_inc(xqs_done, 1)

        def sums(s, j):
            rows, lo, hi = STAT[j]
            v.wait_ge(pj_done, 6 * (s + 1) + j + 1)
            v.wait_ge(va_done, 6 * s + j + 1)
            v.tensor_reduce(ss[0:rows, lo:hi],
                            sq[0:rows, j % 2, 0:(hi - lo) * HD].rearrange("p (h d) -> p h d", d=HD),
                            AX, ALU.add).then_inc(rd_done, 1)

        def scale(s, j):
            rows, lo, hi = STAT[j]
            v.wait_ge(rs_done, 6 * (s + 1) + j + 1)
            buf = (nq[0:T, :], nqx[0:T, :], nk[0:T, :], nkx[0:CT, 0, :], nkx[0:CT, 1, :], nkx[0:CT, 2, :])[j]
            buf = buf.rearrange("p (h d) -> p h d", d=HD)
            v.tensor_tensor(buf, buf, rs[0:rows, lo:hi].unsqueeze(2).to_broadcast([rows, hi - lo, HD]),
                            ALU.mult).then_inc(ln_done, 1)

        def max_self(t):
            v.wait_ge(ss_rdy, t + 2)
            v.wait_ge(es_done, t + 1)
            v.tensor_reduce(nmax[0:T, 0:HP], p_self[0:T, 0:HP * T].rearrange("p (h d) -> p h d", d=T),
                            AX, ALU.max, negate=True).then_inc(ms_done, 1)

        def norm_self(t):
            v.wait_ge(es_done, t + 2)
            v.wait_ge(tr_rdy, 10 * t + 6)
            v.reciprocal(linv[0:T, 0:HP], lsum[0:T, 0:HP]).then_inc(dv, 1)
            v.wait_ge(dv, CH * t + 1)
            v.tensor_tensor(pself[0:T, :, :], pself[0:T, :, :],
                            linv[0:T, 0:HP].unsqueeze(2).to_broadcast([T, HP, T]), ALU.mult).then_inc(ns_done, 1)

        def max_cross(t, h):
            v.wait_ge(sx_rdy, 4 * (t + 1) + h + 1)
            v.wait_ge(ex_done, 4 * t + h + 1)
            v.tensor_reduce(nmax[0:T, 4 + h:5 + h], p_cross[0:T, h % 2, 0:TC], AX, ALU.max,
                            negate=True).then_inc(mx_done, 1)

        def norm_cross(t, h):
            v.wait_ge(ex_done, 4 * (t + 1) + h + 1)
            v.reciprocal(linv[0:T, 4 + h:5 + h], lsum[0:T, 4 + h:5 + h]).then_inc(dv, 1)
            v.wait_ge(dv, CH * t + 2 + h)
            v.tensor_scalar(pcross[0:T, h, :], pcross[0:T, h, :], linv[0:T, 4 + h:5 + h], None,
                            ALU.mult).then_inc(nx_done, 1)

        def take_self(t):
            v.wait_ge(tr_rdy, 10 * (t + 1) + 6)
            v.wait_ge(ou_rdy, 2 * t + 2)
            v.tensor_copy(flat(pselfT[0:T, :, :]), p_tr[0:T, 1, 0:HP * T]).then_inc(pt_done, 1)

        def take_cross(t, h):
            v.wait_ge(tr_rdy, 10 * (t + 1) + 7 + h)
            v.wait_ge(ou_rdy, 2 * t + 2)
            v.tensor_copy(pcrossT[0:CT, :, h, :],
                          p_tr[0:CT, h % 2, 0:NC * T].rearrange("p (k t) -> p k t", k=NC)).then_inc(pt_done, 1)

        def smoothed(t, g):
            v.wait_ge(ou_rdy, 2 * (t + 1) + g + 1)
            v.tensor_tensor(yb[:, g * 4 * T:(g + 1) * 4 * T].rearrange("p (a t) -> p a t", t=T),
                            p_out[:, 0:4 * T].rearrange("p (a t) -> p a t", t=T),
                            smg[:, 4 * g:4 * g + 4].unsqueeze(2).to_broadcast([P, 4, T]),
                            ALU.mult).then_inc(ya_done, 1)

        def rounded(t):
            v.wait_ge(ya_done, 2 * (t + 1) + 2)
            v.tensor_scalar(yb[:, :], yb[:, :], FP8_MAX, -FP8_MAX, ALU.min, ALU.max).then_inc(dv, 1)
            v.wait_ge(dv, CH * t + 6)
            v.tensor_scalar(ye[:, :].bitcast(U16), yb[:, :].bitcast(U16), 0x7F80, None,
                            ALU.bitwise_and).then_inc(dv, 1)
            v.wait_ge(dv, CH * t + 7)
            v.tensor_scalar(ye[:, :], ye[:, :], 2.0 ** -6, 1.5 * 2.0 ** 4, ALU.max, ALU.mult).then_inc(dv, 1)
            v.wait_ge(dv, CH * t + 8)
            v.tensor_tensor(ysum[:, :], yb[:, :], ye[:, :], ALU.add).then_inc(dv, 1)
            v.wait_ge(dv, CH * t + 9)
            v.wait_ge(cat_out, 16 * (t + 1))
            v.tensor_tensor(cat[:, :], ysum[:, :], ye[:, :], ALU.subtract).then_inc(ct_done, 1)

        def step(s, b_next, t, g, first, k):
            A, Q = s is not None and not first, t is not None
            if A: sums(s, 0)
            if A: sums(s, 1)
            if Q: max_self(t)
            if A: scale(s, 0)
            if first and not Q: w_low(g, 0)
            if Q: max_cross(t, 0)
            if Q: max_cross(t, 1)
            if Q: norm_self(t)
            if Q: norm_cross(t, 0)
            if Q: norm_cross(t, 1)
            if first: w_low(g, 1)
            if Q: take_self(t)
            if A: sums(s, 2)
            if Q: take_cross(t, 0)
            if Q: max_cross(t, 2)
            if A: scale(s, 1)
            if Q: take_cross(t, 1)
            if Q: max_cross(t, 3)
            if A: scale(s, 2)
            if A and b_next is not None: inputs(s + 1, b_next)
            if Q: norm_cross(t, 2)
            if Q: norm_cross(t, 3)
            if k is not None: weights.means(v, g, k)
            if first: w_low(g, 2)
            if A: sums(s, 3)
            if Q: smoothed(t, 0)
            if Q: take_cross(t, 2)
            if Q: take_cross(t, 3)
            if A: scale(s, 3)
            if A: sums(s, 4)
            if Q: smoothed(t, 1)
            if A: scale(s, 4)
            if A: sums(s, 5)
            if A: scale(s, 5)
            if first: sums(s, 0)
            if first: sums(s, 1)
            if Q: rounded(t)
            if first:
                smooth_of(g)
                for j in range(6):
                    if j > 1:
                        sums(s, j)
                    if j > 0:
                        scale(s, j - 1)
                    if j == 3:
                        inputs(s + 1, b_next)
                scale(s, 5)

        inputs(0, 0)
        step(0, 1, None, 0, True, None)
        with v.Fori(0, GP - 1) as gp:
            s0 = gp * B
            with v.Fori(0, 3) as i:
                s = s0 + 2 * i
                step(s + 1, 2 * i + 2, s, gp + 1, False, None)
                step(s + 2, 2 * i + 3, s + 1, gp + 1, False, i)
            step(s0 + 7, 0, s0 + 6, gp + 1, False, 3)
            step(s0 + 8, 1, s0 + 7, gp + 1, True, None)
        s0 = (GP - 1) * B
        with v.Fori(0, 3) as i:
            s = s0 + 2 * i
            step(s + 1, 2 * i + 2, s, None, False, None)
            step(s + 2, 2 * i + 3, s + 1, None, False, None)
        step(s0 + 7, None, s0 + 6, None, False, None)
        step(None, None, s0 + 7, None, False, None)


STAT = ((T, 0, 4), (T, 4, 8), (T, 8, 10), (CT, 10, 12), (CT, 12, 14), (CT, 14, 16))
TURNED = (HP * T, HP * T, 2 * T, TC, TC)


def projection(nc, c, sb, ps, sem, x, wproj, catd, W, ident, mhalf, proj_scale,
               x1, xT, xhi, xlo, shared, w_load, cat_load, ffn):
    NB = 8
    w_raw = shared[:, 0:4 * D].rearrange("p (r d) -> p r d", r=4)
    w_hi = sb(c, "p_hi", [P, 2, D], F32R)
    w_lo = sb(c, "p_lo", [P, 2, D], F32R)
    odd = sb(c, "p_cat", [P, B, NB * T], BF16)
    cat = (cat_tile(shared), odd[:, :, :])
    catr = sb(c, "p_catr", [P, 2, NT], F32R)
    xs = sb(c, "xs1", [P, TJ, D])
    st = sb(c, "st1", [P, TJ, 6])
    mv = sb(c, "mv1", [P, TJ, 2])
    rstd = sb(c, "rstd1", [P, TJ])
    shift = sb(c, "shift", [P, TJ])
    acc = ps(c, "p_acc", [P, TJ, D])

    x_in = sem(c, "x_in_p")
    hi_done = sem(c, "ph_done")
    lo_done = sem(c, "pl_done")
    cr_done = sem(c, "cr_done")
    mm_done = sem(c, "pm_done")
    acc_done = sem(c, "acc_done")
    x1_done = sem(c, "x1_done")
    bn_done = sem(c, "bn_done")
    ag_done = sem(c, "ag_done")
    stat_done = sem(c, "stat_done1")
    rstd_pow = sem(c, "rstd_pow")
    rstd_done = sem(c, "rstd_done1")
    norm_done = sem(c, "norm_done1")
    tr_done = sem(c, "tr_done1")
    xT_done = sem(c, "xT_done")
    xh_done = sem(c, "xh_done")
    block = c.enter_context(nc.Block())
    N = 2 * NB

    @block.sync
    def _(sp):
        def load_cat(i, r):
            sp.dma_start(cat[r], catd[(2 * i + r) * B:(2 * i + r + 1) * B].rearrange("b p n -> p b n")
                         ).then_inc(cat_load[r], 16)

        def load_w(i, n):
            sp.wait_ge(hi_done, N * (i + 1) + n - 3)
            sp.wait_ge(lo_done, N * (i + 1) + n - 3)
            sp.dma_start(w_raw[:, n % 4, :], wproj[2 * i + n // NB, n % NB]).then_inc(w_load[n % 4], 16)

        load_cat(0, 1)
        for n in range(4, N):
            load_w(0, n)
            if n == 7:
                sp.dma_start(xs[:, :, :], x.rearrange("b t d -> (b t) d").rearrange("(j p) d -> p j d", p=P)
                             ).then_inc(x_in, 16)
        for n in range(N):
            if n % NB == 0:
                sp.wait_ge(cr_done, N + NB * (n // NB + 1))
                load_cat(1, n // NB)
            load_w(1, n)
            if n == NB:
                for m in range(3):
                    ffn.fetch(sp, W, 0, m)

    @block.gpsimd
    def _(pool):
        for j in range(TJ):
            one = slice(j, j + 1)
            pool.wait_ge(stat_done, j + 1)
            pool.tensor_tensor(rstd[:, one], mv[:, j, 1:2], mhalf[:, 0:1], ALU.pow).then_inc(rstd_pow, 1)
            pool.wait_ge(rstd_pow, j + 1)
            pool.tensor_tensor(shift[:, one], mv[:, j, 0:1], rstd[:, one], ALU.mult).then_inc(rstd_done, 1)

    @block.scalar
    def _(act):
        act.sem_inc(hi_done, N)
        for n in range(3):
            act.sem_inc(ffn.h_done[n], 1)
        with act.Fori(0, GP // 2) as i:
            for n in range(N):
                act.wait_ge(w_load[n % 4], 64 * i + 16 * (n // 4 + 1))
                act.wait_ge(mm_done, N * (i + 1) + n - 1)
                act.activation(w_hi[:, n % 2, :], w_raw[:, n % 4, :], ACT.Copy).then_inc(hi_done, 1)
        ffn.high(act, 0, 0)
        ffn.high(act, 0, 1)
        for j in range(TJ):
            act.wait_ge(rstd_done, j + 1)
            act.activation(xs[:, j, :], x1[:, j, :], ACT.Identity, bias=shift[:, j:j + 1],
                           scale=rstd[:, j:j + 1]).then_inc(norm_done, 1)
        for n in range(2 * KB):
            k, (lo, hi) = n % KB, GROUP[n // KB]
            cols = slice(lo * P, hi * P)
            act.wait_ge(tr_done, n + 1)
            act.activation(xT[:, k, cols], acc[:, n % 2, 0:(hi - lo) * P], ACT.Copy).then_inc(xT_done, 1)
            act.activation(xhi[:, k, cols], acc[:, n % 2, 0:(hi - lo) * P], ACT.Copy).then_inc(xh_done, 1)

    @block.tensor
    def _(pe):
        pe.sem_inc(mm_done, N)

        def ready(i, n):
            pe.wait_ge(hi_done, N * (i + 1) + n + 1)
            pe.wait_ge(lo_done, N * (i + 1) + n + 1)
            pe.wait_ge(cr_done, N * (i + 1) + n + 1)

        def block_of(n, j, first=False, last=False):
            for part, w in enumerate((w_hi, w_lo)):
                m = pe.matmul(acc[:, j, :], catr[:, n % 2, j * P:(j + 1) * P], w[:, n % 2, :],
                              start=(first and part == 0), stop=(last and part == 1), skip_group_check=True)
            return m

        for i in range(GP // 2):
            for n in range(N if i == 0 else N - 2):
                ready(i, n)
                for j in range(TJ):
                    m = block_of(n, j, first=(i == 0 and n == 0))
                m.then_inc(mm_done, 1)
        ready(GP // 2 - 1, N - 2)
        ready(GP // 2 - 1, N - 1)
        for j in range(TJ):
            block_of(N - 2, j)
            block_of(N - 1, j, last=True).then_inc(acc_done, 1)
        pe.wait_ge(x1_done, 2)
        for n in range(2 * KB):
            k, (lo, hi) = n % KB, GROUP[n // KB]
            pe.wait_ge(norm_done, hi)
            if n >= 2:
                pe.wait_ge(xh_done, n - 1)
            for j in range(lo, hi):
                t = pe.transpose(acc[:, n % 2, (j - lo) * P:(j - lo + 1) * P], xs[:, j, k * P:(k + 1) * P],
                                 ident[:, :])
            t.then_inc(tr_done, 1)

    @block.vector
    def _(v):
        v.sem_inc(lo_done, N)
        v.sem_inc(cr_done, N)
        for n in range(3):
            v.sem_inc(ffn.l_done[n], 1)
        with v.Fori(0, GP // 2) as i:
            for n in range(N):
                r, j = n // NB, n % NB
                v.wait_ge(cat_load[r], 16 * (i + 1))
                v.wait_ge(mm_done, N * (i + 1) + n - 1)
                v.tensor_copy(catr[:, n % 2, :].rearrange("p (b t) -> p b t", b=B),
                              cat[r][:, :, j * T:(j + 1) * T]).then_inc(cr_done, 1)
                v.wait_ge(hi_done, N * (i + 1) + n + 1)
                v.tensor_tensor(w_lo[:, n % 2, :], w_raw[:, n % 4, :], w_hi[:, n % 2, :].bitcast(F32),
                                ALU.subtract).then_inc(lo_done, 1)
        ffn.low(v, 0, 0)
        ffn.low(v, 0, 1)
        v.wait_ge(x_in, 16)
        for j in range(TJ + 2):
            if j < TJ:
                v.wait_ge(acc_done, j + 1)
                v.scalar_tensor_tensor(out=x1[:, j, :], in0=acc[:, j, :], scalar=proj_scale[:, 0:1],
                                       in1=xs[:, j, :], op0=ALU.mult, op1=ALU.add).then_inc(x1_done, 1)
            if 1 <= j <= TJ:
                v.wait_ge(x1_done, j)
                v.bn_stats(st[:, j - 1, :], x1[:, j - 1, :]).then_inc(bn_done, 1)
            if j >= 2:
                v.wait_ge(bn_done, j - 1)
                v.bn_aggr(mv[:, j - 2, :], st[:, j - 2, :]).then_inc(ag_done, 1)
                v.wait_ge(ag_done, j - 1)
                v.tensor_scalar(mv[:, j - 2, 0:1], mv[:, j - 2, 0:1], -1.0, None, ALU.mult)
                v.tensor_scalar(mv[:, j - 2, 1:2], mv[:, j - 2, 1:2], EPS, None, ALU.add).then_inc(stat_done, 1)
        for n in range(2 * KB):
            k, (lo, hi) = n % KB, GROUP[n // KB]
            cols = slice(lo * P, hi * P)
            v.wait_ge(xh_done, n + 1)
            v.tensor_tensor(xlo[:, k, cols], xT[:, k, cols], xhi[:, k, cols].bitcast(F32), ALU.subtract)


def experts(nc, c, sb, ps, sem, Wr, W, gate, x1, xT, xhi, xlo, ffn, out):
    hi, lo, h_done, l_done = ffn.hi, ffn.lo, ffn.h_done, ffn.l_done
    sg = sb(c, "sg", [P, 2, HALF])
    hf = sb(c, "hf", [P, 2, HALF])
    hhi = sb(c, "hhi", [P, FB, NT], F32R)
    hlo = sb(c, "hlo", [P, FB, NT], F32R)
    ce = sb(c, "ce", [P, TJ])
    coef = sb(c, "coef", [P, TJ, EX])
    wr = sb(c, "wr", [P, KB, EX])
    lg = sb(c, "lg", [P, TJ, EX])
    pr = sb(c, "pr", [P, TJ, EX])
    m1 = sb(c, "m1", [P, TJ])
    top = sb(c, "top", [P, TJ, EX])
    idx = sb(c, "idx", [P, TJ, EX], U32)
    idf = sb(c, "idf", [P, TJ, EX])
    iota = sb(c, "iota", [P, EX])
    sel = sb(c, "sel", [P, TJ, EX])
    pg = ps(c, "pg", [P, 2, 512])
    pu = ps(c, "pu", [P, 2, 512])
    pd = ps(c, "pd", [P, 2, 512])
    p_lg = ps(c, "p_lg", [P, 512])

    gu_rdy = sem(c, "gu_rdy")
    sg_done = sem(c, "sg_done")
    hm_done = sem(c, "hm_done")
    hh_done = sem(c, "hh_done")
    hl_done = sem(c, "hl_done")
    dn_rdy = sem(c, "dn_rdy")
    ac_done = sem(c, "ac_done")
    ce_done = sem(c, "ce_done")
    stored = sem(c, "stored")
    wr_in = sem(c, "wr_in")
    iota_done = sem(c, "iota_done")
    lg_rdy = sem(c, "lg_rdy")
    lg_cen = sem(c, "lg_cen")
    ex_done = sem(c, "lg_exp")
    dve = sem(c, "dve_chain2")
    block = c.enter_context(nc.Block())

    tokens = out.rearrange("b t d -> (b t) d")

    @block.sync
    def _(sp):
        sp.dma_start(wr[:, :, :], Wr.rearrange("(k p) e -> p k e", p=P)).then_inc(wr_in, 16)
        with sp.Fori(1, EX) as e:
            for n in range(3):
                sp.wait_ge(h_done[n], e + 1)
                sp.wait_ge(l_done[n], e + 1)
                ffn.fetch(sp, W, e, n)
        for j in range(TJ):
            sp.wait_ge(ac_done, TJ * EX + j + 1)
            sp.dma_start(tokens[j * P:(j + 1) * P, :], x1[:, j, :]).then_inc(stored, 16)
        sp.wait_ge(stored, 16 * TJ)

    @block.gpsimd
    def _(pool):
        pool.iota(iota[:, :], pattern=[[1, EX]], base=0, channel_multiplier=0,
                  allow_small_or_imprecise_dtypes=True).then_inc(iota_done, 1)

    @block.scalar
    def _(act):
        act.sem_inc(sg_done, 8)
        act.sem_inc(hh_done, 8)

        def split(e, n):
            if n < 2:
                act.wait_ge(gu_rdy, 8 * e + 8)
            else:
                act.wait_ge(dn_rdy, TJ * e + TJ)
            ffn.high(act, e, n)

        def silu(e, m):
            act.wait_ge(gu_rdy, 8 * (e + 1) + m + 1)
            act.wait_ge(hm_done, 8 * (e + 1) + m - 1)
            act.activation(sg[:, m % 2, :], pg[:, m % 2, 0:HALF], ACT.Silu).then_inc(sg_done, 1)

        def high(e, m):
            act.wait_ge(hm_done, 8 * (e + 1) + m + 1)
            act.wait_ge(dn_rdy, TJ * e + TJ)
            act.activation(hhi[:, m % FB, m // FB * HALF:(m // FB + 1) * HALF], hf[:, m % 2, :],
                           ACT.Copy).then_inc(hh_done, 1)

        def expert(e, first=False, last=False):
            silu(e, 0)
            split(e, 2)
            for m in range(1, 8):
                high(e, m - 1)
                silu(e, m)
            high(e, 7)
            if first:
                act.wait_ge(lg_cen, 1)
                act.activation(pr[:, :, :], lg[:, :, :], ACT.Exp).then_inc(ex_done, 1)
            if not last:
                split(e + 1, 0)
                split(e + 1, 1)

        expert(0, first=True)
        with act.Fori(1, EX - 1) as e:
            expert(e)
        expert(EX - 1, last=True)

    @block.tensor
    def _(pe):
        pe.sem_inc(gu_rdy, 8)
        pe.sem_inc(dn_rdy, TJ)
        def expert(e, first=False):
            for m in range(8):
                f, h = m % FB, m // FB
                if m == 0:
                    for n in range(2):
                        pe.wait_ge(h_done[n], e + 2)
                        pe.wait_ge(l_done[n], e + 2)
                pe.wait_ge(hm_done, 8 * (e + 1) + m - 1)
                for n, bank in ((0, pg), (1, pu)):
                    for i in range(3 * KB):
                        k = i // 3
                        w, a = ((hi, xhi), (hi, xlo), (lo, xhi))[i % 3]
                        mm = pe.matmul(bank[:, m % 2, 0:HALF], w[n][:, k, f * P:(f + 1) * P],
                                       a[:, k, h * HALF:(h + 1) * HALF], start=(i == 0), stop=(i == 3 * KB - 1))
                mm.then_inc(gu_rdy, 1)
            if first:
                pe.wait_ge(wr_in, 16)
                for j in range(TJ):
                    for k in range(KB):
                        mm = pe.matmul(p_lg[:, j * EX:(j + 1) * EX], xT[:, k, j * P:(j + 1) * P], wr[:, k, :],
                                       start=(k == 0), stop=(k == KB - 1))
                mm.then_inc(lg_rdy, 1)
            pe.wait_ge(h_done[2], e + 2)
            pe.wait_ge(l_done[2], e + 2)
            for j in range(TJ):
                if j == 0:
                    pe.wait_ge(hl_done, 8 * (e + 1) + FB)
                elif (j + 1) * P > HALF >= j * P:
                    pe.wait_ge(hl_done, 8 * (e + 1) + 2 * FB)
                pe.wait_ge(ac_done, TJ * (e + 1) + j - 1)
                for i in range(3 * FB):
                    k = i // 3
                    a, w = ((hhi, hi), (hhi, lo), (hlo, hi))[i % 3]
                    mm = pe.matmul(pd[:, j % 2, :], a[:, k, j * P:(j + 1) * P], w[2][:, k, :],
                                   start=(i == 0), stop=(i == 3 * FB - 1))
                mm.then_inc(dn_rdy, 1)

        expert(0, first=True)
        with pe.Fori(1, EX) as e:
            expert(e)

    @block.vector
    def _(v):
        v.sem_inc(hm_done, 8)
        v.sem_inc(hl_done, 8)
        v.sem_inc(ac_done, TJ)

        def product(e, m):
            v.wait_ge(sg_done, 8 * (e + 1) + m + 1)
            v.wait_ge(hh_done, 8 * (e + 1) + m - 1)
            v.tensor_tensor(hf[:, m % 2, :], sg[:, m % 2, :], pu[:, m % 2, 0:HALF], ALU.mult).then_inc(hm_done, 1)

        def low(e, m):
            v.wait_ge(hh_done, 8 * (e + 1) + m + 1)
            cols = slice(m // FB * HALF, (m // FB + 1) * HALF)
            v.tensor_tensor(hlo[:, m % FB, cols], hf[:, m % 2, :], hhi[:, m % FB, cols].bitcast(F32),
                            ALU.subtract).then_inc(hl_done, 1)

        def add(e, j):
            v.wait_ge(dn_rdy, TJ * (e + 1) + j + 1)
            if j == 0:
                v.wait_ge(ce_done, e + 1)
            v.scalar_tensor_tensor(out=x1[:, j, :], in0=pd[:, j % 2, :], scalar=ce[:, j:j + 1],
                                   in1=x1[:, j, :], op0=ALU.mult, op1=ALU.add).then_inc(ac_done, 1)

        count = [0]

        def link(ins):
            count[0] += 1
            ins.then_inc(dve, 1)
            v.wait_ge(dve, count[0])

        def route():
            v.wait_ge(lg_rdy, 1)
            lp = p_lg[:, 0:TJ * EX].rearrange("p (b e) -> p b e", e=EX)
            link(v.tensor_reduce(m1[:, :], lp, AX, ALU.max))
            v.tensor_tensor(lg[:, :, :], lp, m1[:, :].unsqueeze(2).to_broadcast([P, TJ, EX]),
                            ALU.subtract).then_inc(lg_cen, 1)
            v.wait_ge(ex_done, 1)
            link(v.tensor_reduce(m1[:, :], pr[:, :, :], AX, ALU.add))
            link(v.reciprocal(m1[:, :], m1[:, :]))
            link(v.tensor_tensor(pr[:, :, :], pr[:, :, :], m1[:, :].unsqueeze(2).to_broadcast([P, TJ, EX]),
                                 ALU.mult))
            for j in range(TJ):
                last = v.max(top[:, j, :], pr[:, j, :])
            link(last)
            for j in range(TJ):
                last = v.max_index(idx[:, j, :], top[:, j, :], pr[:, j, :])
            link(last)
            link(v.tensor_copy(idf[:, :, :], idx[:, :, :]))
            link(v.tensor_tensor(m1[:, :], top[:, :, 0], top[:, :, 1], ALU.add))
            link(v.reciprocal(m1[:, :], m1[:, :]))
            link(v.tensor_scalar(m1[:, :], m1[:, :], gate[:, 1:2], None, ALU.mult))
            link(v.tensor_tensor(top[:, :, :], top[:, :, :], m1[:, :].unsqueeze(2).to_broadcast([P, TJ, EX]),
                                 ALU.mult))
            v.wait_ge(iota_done, 1)
            io = iota[:, :].unsqueeze(1).to_broadcast([P, TJ, EX])
            for r, dst in ((0, coef), (1, sel)):
                link(v.tensor_tensor(dst[:, :, :], io, idf[:, :, r].unsqueeze(2).to_broadcast([P, TJ, EX]),
                                     ALU.is_equal))
                link(v.tensor_tensor(dst[:, :, :], dst[:, :, :],
                                     top[:, :, r].unsqueeze(2).to_broadcast([P, TJ, EX]), ALU.mult))
            link(v.tensor_tensor(coef[:, :, :], coef[:, :, :], sel[:, :, :], ALU.add))

        def expert(e, first=False, last=False):
            product(e, 0)
            ffn.low(v, e, 2)
            for m in range(1, 8):
                low(e, m - 1)
                product(e, m)
            low(e, 7)
            if first:
                route()
            v.wait_ge(ac_done, TJ * e + TJ)
            v.tensor_copy(ce[:, :], coef[:, :, bass.ds(e, 1)].rearrange("p j e -> p (j e)")
                          ).then_inc(ce_done, 1)
            add(e, 0)
            add(e, 1)
            if not last:
                ffn.low(v, e + 1, 0)
            add(e, 2)
            add(e, 3)
            if not last:
                ffn.low(v, e + 1, 1)
            for j in range(4, TJ):
                add(e, j)

        expert(0, first=True)
        with v.Fori(1, EX - 1) as e:
            expert(e)
        expert(EX - 1, last=True)


def kernel(**inputs):
    import numpy as np
    import concourse.bacc as bacc
    from concourse.bass_utils import run_bass_kernel_spmd

    a = {k: np.asarray(v) for k, v in inputs.items()}
    L = "L0_xattn_"

    def channels(v):
        return v.reshape(KB, P).T

    vecs = np.concatenate(
        [channels(a[L + n]) for n in ("ln_w", "ln_b", "q_in_scale", "qx_in_scale", "k_in_scale", "v_in_scale")]
        + [a[L + n].reshape(P, 1) for n in ("qln_w", "qln_b", "kln_w", "kln_b",
                                            "qxln_w", "qxln_b", "kxln_w", "kxln_b")], axis=1)
    scalars = np.array([a[L + n].reshape(()) for n in ("wq_scale", "wqx_scale", "wk_scale", "wv_scale",
                                                       "proj_in_scale", "proj_w_scale")]
                       + [a["g_xattn"].reshape(()), a["g_ffn"].reshape(())])
    kv = a[L + "w_kv_x"]
    parts = [(a[L + "wq"], 512), (a[L + "wqx"], 512), (a[L + "wk"], 256), (kv[:G * HD], 256),
             (kv[G * HD:], 256), (a[L + "wv"], 256)]
    w_in = np.concatenate([w.reshape(GP, n, KB, P).transpose(0, 3, 2, 1) for w, n in parts], axis=3)
    order = (1, 2, 0, 3)
    wproj = a[L + "wproj"].T.reshape(2, GP, 2, HPG, P, D).transpose(*order, 4, 5).reshape(GP, 8, P, D)
    smooth = a[L + "proj_smooth"].reshape(2, GP, 2, HPG, P).transpose(*order, 4).reshape(GP, 8, P)
    ctxT = a["ctx_2048"].reshape(B, NC, CT, KB, P).transpose(0, 1, 4, 3, 2)
    arrays = {
        "x": a["x"], "ctxT": ctxT, "vecs": vecs, "scalars": scalars,
        "smooth": smooth.transpose(2, 0, 1), "w_in": w_in, "wproj": wproj,
        "Wr": a["L0_ffn_Wr"], "Wg": a["L0_ffn_Wg"], "Wu": a["L0_ffn_Wu"], "Wd": a["L0_ffn_Wd"],
    }
    nc = bacc.Bacc("TRN2", target_bir_lowering=False, num_devices=1)
    feed, args = {}, []
    for name, v in arrays.items():
        v = np.ascontiguousarray(v)
        feed[f"in_{name}"] = v
        args.append(nc.dram_tensor(f"in_{name}", v.shape, mybir.dt.from_np(v.dtype), kind="ExternalInput").ap())
    o = nc.dram_tensor("out_0", (B, T, D), F32, kind="ExternalOutput").ap()
    transformer_block(nc, *args, o)
    r = run_bass_kernel_spmd(nc, [feed], core_ids=[0])
    return r.results[0]["out_0"]
```
